# Optimizing a Trainium2 kernel written in Bass

```python
import numpy as np
import jax
import jax.numpy as jnp

def _softmax(x, axis=-1):
    return jax.nn.softmax(x, axis=axis)

def _gelu(x):
    return jax.nn.gelu(x, approximate=True)

def _silu(x):
    return jax.nn.silu(x)

def _sigmoid(x):
    return jax.nn.sigmoid(x)

def _layernorm(x, axis=-1, eps=1e-05):
    m = jnp.mean(x, axis=axis, keepdims=True)
    v = jnp.var(x, axis=axis, keepdims=True)
    return (x - m) / jnp.sqrt(v + eps)

def _scatter_add(tgt, idx, src, axis=0):
    return tgt.at[idx].add(src)

def _segment_sum(src, seg, n):
    return jax.ops.segment_sum(src, seg, n)
kernel_name = 'mk_xattn_ffn_d2_seqx_r8_a21023'

def setup_inputs(seed: int=0):
    np.random.seed(seed)
    _w = jnp.asarray

    def _rec_inputs():
        import jax
        import jax.numpy as jnp
        _rk = jax.random.key(seed)
        x = 7.22e-05 + 1 * jax.random.normal(jax.random.fold_in(_rk, 1), (128, 64, 128), jnp.float32)
        _lenS = 64 - jax.random.randint(jax.random.fold_in(_rk, 7), (128,), 0, max(1, 64 // 4) + 1, jnp.int32)
        _lenS2 = 64 - jax.random.randint(jax.random.fold_in(_rk, 8), (128,), 0, max(1, 64 // 4) + 1, jnp.int32)
        _ctx_768P = jax.random.normal(jax.random.fold_in(_rk, 11), (128, 16, 96), jnp.float32)
        _ctx_768c = jax.random.dirichlet(jax.random.fold_in(_rk, 511), 0.3 * jnp.ones((16,), jnp.float32), (128, 64))
        _ctx_768t = jnp.einsum('bsk,bkd->bsd', _ctx_768c, _ctx_768P)
        _ctx_768t = _ctx_768t * jax.lax.rsqrt(jnp.mean(jnp.square(_ctx_768t)) + 1e-12) * 0.953939
        ctx_768 = -0.000191848 + 0.999787 * (_ctx_768t + 0.3 * jax.random.normal(jax.random.fold_in(_rk, 611), (128, 64, 96), jnp.float32))
        _validS = jnp.arange(64)[None, :] < _lenS[:, None]
        _validS2 = jnp.arange(64)[None, :] < _lenS2[:, None]
        _causal = jnp.tril(jnp.ones((64, 64), dtype=bool))
        mask_BxS2_bk0 = jnp.logical_not(jnp.broadcast_to(_validS2[:, :], (128, 64)))
        mask_BxS_bf1 = jnp.ones((128, 64), dtype=bool)
        mask_BxS2_bf1 = jnp.ones((128, 64), dtype=bool)
        return (x, ctx_768, mask_BxS2_bk0, mask_BxS_bf1, mask_BxS2_bf1)
    x, ctx_768, mask_BxS2_bk0, mask_BxS_bf1, mask_BxS2_bf1 = _rec_inputs()

    def _L0_xattn_setup():
        import jax, jax.numpy as jnp
        import numpy as np
        HEADS = 8
        DIM_HEAD = 64
        QUERY_DIM = 128
        CONTEXT_DIM = 96
        INNER = HEADS * DIM_HEAD
        key = jax.random.key(seed)
        ks = jax.random.split(key, 8)
        b, n, j = (4, 256, 256)
        x = jax.random.normal(ks[0], (b, n, QUERY_DIM), dtype=jnp.float32)
        context = jax.random.normal(ks[1], (b, j, CONTEXT_DIM), dtype=jnp.float32)
        mask = jax.random.randint(ks[2], (b, j), 0, 2).astype(jnp.bool_)
        W_q = jax.random.normal(ks[3], (QUERY_DIM, INNER), dtype=jnp.float32) / np.sqrt(QUERY_DIM)
        W_k = jax.random.normal(ks[4], (CONTEXT_DIM, INNER), dtype=jnp.float32) / np.sqrt(CONTEXT_DIM)
        W_v = jax.random.normal(ks[5], (CONTEXT_DIM, INNER), dtype=jnp.float32) / np.sqrt(CONTEXT_DIM)
        W_o = jax.random.normal(ks[6], (INNER, QUERY_DIM), dtype=jnp.float32) / np.sqrt(INNER)
        b_o = jax.random.normal(ks[7], (QUERY_DIM,), dtype=jnp.float32) * 0.01
        return {'x': x, 'context': context, 'mask': mask, 'W_q': W_q, 'W_k': W_k, 'W_v': W_v, 'W_o': W_o, 'b_o': b_o}
    _L0_xattn_all = _L0_xattn_setup()
    _L0_xattn_in = {k: v for k, v in _L0_xattn_all.items() if k in ('W_q', 'W_k', 'W_v', 'W_o', 'b_o')}
    del _L0_xattn_all

    def _L0_ffn_setup():
        import jax, jax.numpy as jnp
        import numpy as np
        BLOCK = 32
        W_BITS = 4
        ACT_BITS = 16

        def act_qdq(x):
            qmax = 2.0 ** (ACT_BITS - 1) - 1.0
            scale = jnp.maximum(jnp.max(jnp.abs(x)) / qmax, 1e-12)
            return jnp.clip(jnp.round(x / scale), -qmax - 1.0, qmax) * scale

        def fixed_qdq_u16(x):
            scale = 1.0 / 65536.0
            return jnp.clip(jnp.round(x / scale), 0.0, 65535.0) * scale

        def lpbq_dequant(w):
            O, I = w.shape
            qmax = 2.0 ** (W_BITS - 1) - 1.0
            wb = w.reshape(O, I // BLOCK, BLOCK)
            s = jnp.maximum(jnp.max(jnp.abs(wb), axis=-1, keepdims=True) / qmax, 1e-12)
            wq = jnp.clip(jnp.round(wb / s), -qmax - 1.0, qmax) * s
            return wq.reshape(O, I)
        key = jax.random.key(seed)
        k1, k2, k3, k4 = jax.random.split(key, 4)
        B, S, H, I = (2, 512, 128, 384)
        x = jax.random.normal(k1, (B, S, H), jnp.float32)
        w_gate = jax.random.normal(k2, (I, H), jnp.float32) * 0.02
        w_up = jax.random.normal(k3, (I, H), jnp.float32) * 0.02
        w_down = jax.random.normal(k4, (H, I), jnp.float32) * 0.02
        return {'x': x, 'w_gate': w_gate, 'w_up': w_up, 'w_down': w_down}
    _L0_ffn_all = _L0_ffn_setup()
    _L0_ffn_in = {k: v for k, v in _L0_ffn_all.items() if k in ('w_gate', 'w_up', 'w_down')}
    del _L0_ffn_all

    def _L1_xattn_setup():
        import jax, jax.numpy as jnp
        import numpy as np
        B, T, DT, G, DV = (16, 64, 128, 72, 96)
        H, DH = (4, 32)
        INNER = H * DH
        HID = 4 * DT
        N_STATE = 64
        K_TOP = 32

        def layernorm(x, g, b, eps=1e-05):
            m = x.mean(-1, keepdims=True)
            v = x.var(-1, keepdims=True)
            return (x - m) * jax.lax.rsqrt(v + eps) * g + b

        def s4d(x, log_dt, A_re, A_im, C_re, C_im, D_skip):
            Bb, L, D = x.shape
            dt = jnp.exp(log_dt)
            A = A_re + 1j * A_im
            C = C_re + 1j * C_im
            dtA = dt[:, None] * A
            dC = C * (jnp.exp(dtA) - 1.0) / A
            powers = jnp.exp(dtA[:, :, None] * jnp.arange(L))
            K = 2.0 * jnp.einsum('dn,dnl->dl', dC, powers).real
            n = 2 * L
            Kf = jnp.fft.rfft(K, n=n, axis=-1)
            xf = jnp.fft.rfft(x, n=n, axis=1)
            y = jnp.fft.irfft(xf * Kf.T[None], n=n, axis=1)[:, :L]
            return y + x * D_skip
        key = jax.random.key(seed)
        ks = jax.random.split(key, 16)
        s = 0.02
        inp = {'x_text': jax.random.normal(ks[0], (B, T, DT), jnp.float32), 'x_vision': jax.random.normal(ks[1], (B, G, DV), jnp.float32), 'text_mask': jnp.ones((B, T), bool), 'vision_mask': jnp.ones((B, G), bool), 'Wq': jax.random.normal(ks[2], (DT, INNER), jnp.float32) * s, 'Wk': jax.random.normal(ks[3], (DV, INNER), jnp.float32) * s, 'Wv': jax.random.normal(ks[4], (DV, DT), jnp.float32) * s, 'W_film_in': jax.random.normal(ks[5], (DT, 2 * DT), jnp.float32) * s, 'b_film_in': jnp.zeros((2 * DT,), jnp.float32), 'W_film_out': jax.random.normal(ks[6], (DT, 2 * DT), jnp.float32) * s, 'b_film_out': jnp.zeros((2 * DT,), jnp.float32), 'g_norm_in': jnp.ones((DT,), jnp.float32), 'b_norm_in': jnp.zeros((DT,), jnp.float32), 'g_norm_out': jnp.ones((DT,), jnp.float32), 'b_norm_out': jnp.zeros((DT,), jnp.float32), 'g_ffn': jnp.ones((DT,), jnp.float32), 'b_ffn': jnp.zeros((DT,), jnp.float32), 'W1': jax.random.normal(ks[7], (DT, HID), jnp.float32) * s, 'b1': jnp.zeros((HID,), jnp.float32), 'W2': jax.random.normal(ks[8], (HID, DT), jnp.float32) * s, 'b2': jnp.zeros((DT,), jnp.float32), 'log_dt': jnp.log(0.001) + jax.random.uniform(ks[9], (DT,), jnp.float32) * (jnp.log(0.1) - jnp.log(0.001)), 'A_re': -0.5 * jnp.ones((DT, N_STATE), jnp.float32), 'A_im': jnp.tile(jnp.pi * jnp.arange(N_STATE, dtype=jnp.float32), (DT, 1)), 'C_re': jax.random.normal(ks[10], (DT, N_STATE), jnp.float32) * 0.5 ** 0.5, 'C_im': jax.random.normal(ks[11], (DT, N_STATE), jnp.float32) * 0.5 ** 0.5, 'D_skip': jax.random.normal(ks[12], (DT,), jnp.float32), 'mod_gate': jnp.array(0.5, jnp.float32)}
        return inp
    _L1_xattn_all = _L1_xattn_setup()
    _L1_xattn_in = {k: v for k, v in _L1_xattn_all.items() if k in ('Wq', 'Wk', 'Wv', 'W_film_in', 'b_film_in', 'W_film_out', 'b_film_out', 'g_norm_in', 'b_norm_in', 'g_norm_out', 'b_norm_out', 'g_ffn', 'b_ffn', 'W1', 'b1', 'W2', 'b2', 'log_dt', 'A_re', 'A_im', 'C_re', 'C_im', 'D_skip', 'mod_gate')}
    del _L1_xattn_all

    def _L1_ffn_setup():
        import jax, jax.numpy as jnp
        import numpy as np
        NUM_EXPERTS = 8
        HIDDEN = 128
        INTER = 128
        BATCH = 2
        SEQ = 128
        TOP_K = 2
        SWIGLU_ALPHA = 1.702
        LIMIT = 7.0

        def _grouped_mm(x, w, expert_ids):
            onehot = jax.nn.one_hot(expert_ids, w.shape[0], dtype=x.dtype)
            y_all = jnp.einsum('tk,ekn->etn', x, w)
            return jnp.einsum('te,etn->tn', onehot, y_all)

        def _gpt_oss_swiglu(x):
            gate = jnp.minimum(x[..., ::2], LIMIT)
            up = jnp.clip(x[..., 1::2], -LIMIT, LIMIT)
            glu = gate * jax.nn.sigmoid(gate * SWIGLU_ALPHA)
            return (up + 1.0) * glu
        key = jax.random.key(seed)
        ks = jax.random.split(key, 7)
        hidden_states = jax.random.normal(ks[0], (BATCH, SEQ, HIDDEN), jnp.float32)
        router_indices = jax.random.randint(ks[1], (BATCH * SEQ, TOP_K), 0, NUM_EXPERTS)
        routing_weights = jax.nn.softmax(jax.random.normal(ks[2], (BATCH * SEQ, NUM_EXPERTS), jnp.float32), axis=-1)
        scale = 0.02
        gate_up_proj = jax.random.normal(ks[3], (NUM_EXPERTS, HIDDEN, 2 * INTER), jnp.float32) * scale
        gate_up_proj_bias = jax.random.normal(ks[4], (NUM_EXPERTS, 2 * INTER), jnp.float32) * scale
        down_proj = jax.random.normal(ks[5], (NUM_EXPERTS, INTER, HIDDEN), jnp.float32) * scale
        down_proj_bias = jax.random.normal(ks[6], (NUM_EXPERTS, HIDDEN), jnp.float32) * scale
        return {'hidden_states': hidden_states, 'router_indices': router_indices, 'routing_weights': routing_weights, 'gate_up_proj': gate_up_proj, 'gate_up_proj_bias': gate_up_proj_bias, 'down_proj': down_proj, 'down_proj_bias': down_proj_bias}
    _L1_ffn_all = _L1_ffn_setup()
    _L1_ffn_in = {k: v for k, v in _L1_ffn_all.items() if k in ('router_indices', 'routing_weights', 'gate_up_proj', 'gate_up_proj_bias', 'down_proj', 'down_proj_bias')}
    del _L1_ffn_all
    return {'x': x, 'ctx_768': ctx_768, 'mask_BxS2_bk0': mask_BxS2_bk0, 'mask_BxS_bf1': mask_BxS_bf1, 'mask_BxS2_bf1': mask_BxS2_bf1, 'L0_xattn_W_q': _L0_xattn_in['W_q'], 'L0_xattn_W_k': _L0_xattn_in['W_k'], 'L0_xattn_W_v': _L0_xattn_in['W_v'], 'L0_xattn_W_o': _L0_xattn_in['W_o'], 'L0_xattn_b_o': _L0_xattn_in['b_o'], 'L0_ffn_w_gate': _L0_ffn_in['w_gate'], 'L0_ffn_w_up': _L0_ffn_in['w_up'], 'L0_ffn_w_down': _L0_ffn_in['w_down'], 'L1_xattn_Wq': _L1_xattn_in['Wq'], 'L1_xattn_Wk': _L1_xattn_in['Wk'], 'L1_xattn_Wv': _L1_xattn_in['Wv'], 'L1_xattn_W_film_in': _L1_xattn_in['W_film_in'], 'L1_xattn_b_film_in': _L1_xattn_in['b_film_in'], 'L1_xattn_W_film_out': _L1_xattn_in['W_film_out'], 'L1_xattn_b_film_out': _L1_xattn_in['b_film_out'], 'L1_xattn_g_norm_in': _L1_xattn_in['g_norm_in'], 'L1_xattn_b_norm_in': _L1_xattn_in['b_norm_in'], 'L1_xattn_g_norm_out': _L1_xattn_in['g_norm_out'], 'L1_xattn_b_norm_out': _L1_xattn_in['b_norm_out'], 'L1_xattn_g_ffn': _L1_xattn_in['g_ffn'], 'L1_xattn_b_ffn': _L1_xattn_in['b_ffn'], 'L1_xattn_W1': _L1_xattn_in['W1'], 'L1_xattn_b1': _L1_xattn_in['b1'], 'L1_xattn_W2': _L1_xattn_in['W2'], 'L1_xattn_b2': _L1_xattn_in['b2'], 'L1_xattn_log_dt': _L1_xattn_in['log_dt'], 'L1_xattn_A_re': _L1_xattn_in['A_re'], 'L1_xattn_A_im': _L1_xattn_in['A_im'], 'L1_xattn_C_re': _L1_xattn_in['C_re'], 'L1_xattn_C_im': _L1_xattn_in['C_im'], 'L1_xattn_D_skip': _L1_xattn_in['D_skip'], 'L1_xattn_mod_gate': _L1_xattn_in['mod_gate'], 'L1_ffn_router_indices': _L1_ffn_in['router_indices'], 'L1_ffn_routing_weights': _L1_ffn_in['routing_weights'], 'L1_ffn_gate_up_proj': _L1_ffn_in['gate_up_proj'], 'L1_ffn_gate_up_proj_bias': _L1_ffn_in['gate_up_proj_bias'], 'L1_ffn_down_proj': _L1_ffn_in['down_proj'], 'L1_ffn_down_proj_bias': _L1_ffn_in['down_proj_bias']}

def reference(x, ctx_768, mask_BxS2_bk0, mask_BxS_bf1, mask_BxS2_bf1, L0_xattn_W_q, L0_xattn_W_k, L0_xattn_W_v, L0_xattn_W_o, L0_xattn_b_o, L0_ffn_w_gate, L0_ffn_w_up, L0_ffn_w_down, L1_xattn_Wq, L1_xattn_Wk, L1_xattn_Wv, L1_xattn_W_film_in, L1_xattn_b_film_in, L1_xattn_W_film_out, L1_xattn_b_film_out, L1_xattn_g_norm_in, L1_xattn_b_norm_in, L1_xattn_g_norm_out, L1_xattn_b_norm_out, L1_xattn_g_ffn, L1_xattn_b_ffn, L1_xattn_W1, L1_xattn_b1, L1_xattn_W2, L1_xattn_b2, L1_xattn_log_dt, L1_xattn_A_re, L1_xattn_A_im, L1_xattn_C_re, L1_xattn_C_im, L1_xattn_D_skip, L1_xattn_mod_gate, L1_ffn_router_indices, L1_ffn_routing_weights, L1_ffn_gate_up_proj, L1_ffn_gate_up_proj_bias, L1_ffn_down_proj, L1_ffn_down_proj_bias):
    import jax
    import jax.numpy as jnp

    def _L0_xattn_ref(x, context, mask, W_q, W_k, W_v, W_o, b_o):
        import jax, jax.numpy as jnp
        import numpy as np
        HEADS = 8
        DIM_HEAD = 64
        QUERY_DIM = 128
        CONTEXT_DIM = 96
        INNER = HEADS * DIM_HEAD
        b, n, _ = x.shape
        j = context.shape[1]
        scale = DIM_HEAD ** (-0.5)
        q = (x @ W_q).reshape(b, n, HEADS, DIM_HEAD)
        k = (context @ W_k).reshape(b, j, HEADS, DIM_HEAD)
        v = (context @ W_v).reshape(b, j, HEADS, DIM_HEAD)
        sim = jnp.einsum('bihd,bjhd->bhij', q, k) * scale
        max_neg = -jnp.finfo(sim.dtype).max
        sim = jnp.where(mask[:, None, None, :], sim, max_neg)
        attn = jax.nn.softmax(sim, axis=-1)
        out = jnp.einsum('bhij,bjhd->bihd', attn, v).reshape(b, n, INNER)
        return out @ W_o + b_o

    def _L0_ffn_ref(x, w_gate, w_up, w_down):
        import jax, jax.numpy as jnp
        import numpy as np
        BLOCK = 32
        W_BITS = 4
        ACT_BITS = 16

        def act_qdq(x):
            qmax = 2.0 ** (ACT_BITS - 1) - 1.0
            scale = jnp.maximum(jnp.max(jnp.abs(x)) / qmax, 1e-12)
            return jnp.clip(jnp.round(x / scale), -qmax - 1.0, qmax) * scale

        def fixed_qdq_u16(x):
            scale = 1.0 / 65536.0
            return jnp.clip(jnp.round(x / scale), 0.0, 65535.0) * scale

        def lpbq_dequant(w):
            O, I = w.shape
            qmax = 2.0 ** (W_BITS - 1) - 1.0
            wb = w.reshape(O, I // BLOCK, BLOCK)
            s = jnp.maximum(jnp.max(jnp.abs(wb), axis=-1, keepdims=True) / qmax, 1e-12)
            wq = jnp.clip(jnp.round(wb / s), -qmax - 1.0, qmax) * s
            return wq.reshape(O, I)
        x = act_qdq(x)
        up = act_qdq(x @ lpbq_dequant(w_up).T)
        gate = act_qdq(x @ lpbq_dequant(w_gate).T)
        sig = fixed_qdq_u16(jax.nn.sigmoid(gate))
        gate = act_qdq(gate * sig)
        o = act_qdq(gate * up)
        return o @ lpbq_dequant(w_down).T

    def _L1_xattn_ref(x_text, x_vision, text_mask, vision_mask, Wq, Wk, Wv, W_film_in, b_film_in, W_film_out, b_film_out, g_norm_in, b_norm_in, g_norm_out, b_norm_out, g_ffn, b_ffn, W1, b1, W2, b2, log_dt, A_re, A_im, C_re, C_im, D_skip, mod_gate):
        import jax, jax.numpy as jnp
        import numpy as np
        B, T, DT, G, DV = (16, 64, 128, 72, 96)
        H, DH = (4, 32)
        INNER = H * DH
        HID = 4 * DT
        N_STATE = 64
        K_TOP = 32

        def layernorm(x, g, b, eps=1e-05):
            m = x.mean(-1, keepdims=True)
            v = x.var(-1, keepdims=True)
            return (x - m) * jax.lax.rsqrt(v + eps) * g + b

        def s4d(x, log_dt, A_re, A_im, C_re, C_im, D_skip):
            Bb, L, D = x.shape
            dt = jnp.exp(log_dt)
            A = A_re + 1j * A_im
            C = C_re + 1j * C_im
            dtA = dt[:, None] * A
            dC = C * (jnp.exp(dtA) - 1.0) / A
            powers = jnp.exp(dtA[:, :, None] * jnp.arange(L))
            K = 2.0 * jnp.einsum('dn,dnl->dl', dC, powers).real
            n = 2 * L
            Kf = jnp.fft.rfft(K, n=n, axis=-1)
            xf = jnp.fft.rfft(x, n=n, axis=1)
            y = jnp.fft.irfft(xf * Kf.T[None], n=n, axis=1)[:, :L]
            return y + x * D_skip
        Bb, Tt, D = x_text.shape
        Gg = x_vision.shape[1]
        Q = (x_text @ Wq).reshape(Bb, Tt, H, DH)
        K = (x_vision @ Wk).reshape(Bb, Gg, H, DH)
        scores = jnp.einsum('bthd,bghd->bhtg', Q, K) / np.sqrt(DH).astype(np.float32)
        scores = jnp.where(vision_mask[:, None, None, :], scores, -jnp.inf)
        topv, topi = jax.lax.top_k(scores, K_TOP)
        probs = jax.nn.softmax(topv, axis=-1)
        bi = jnp.arange(Bb)[:, None, None, None]
        hi = jnp.arange(H)[None, :, None, None]
        ti = jnp.arange(Tt)[None, None, :, None]
        attn = jnp.zeros_like(scores).at[bi, hi, ti, topi].set(probs)
        attn_mean = attn.mean(axis=1)
        V = x_vision @ Wv
        c_t = jnp.einsum('btg,bgd->btd', attn_mean, V)
        c_t = c_t * text_mask[..., None]
        x = layernorm(x_text, g_norm_in, b_norm_in)
        scale_in, shift_in = jnp.split(c_t @ W_film_in + b_film_in, 2, axis=-1)
        x = x * (1.0 + mod_gate * scale_in) + mod_gate * shift_in
        y = s4d(x, log_dt, A_re, A_im, C_re, C_im, D_skip)
        scale_out, shift_out = jnp.split(c_t @ W_film_out + b_film_out, 2, axis=-1)
        y = y * (1.0 + mod_gate * scale_out) + mod_gate * shift_out
        xt = x_text + y
        h = layernorm(xt, g_ffn, b_ffn)
        h = jax.nn.gelu(h @ W1 + b1, approximate=False) @ W2 + b2
        xt = xt + h
        return layernorm(xt, g_norm_out, b_norm_out)

    def _L1_ffn_ref(hidden_states, router_indices, routing_weights, gate_up_proj, gate_up_proj_bias, down_proj, down_proj_bias):
        import jax, jax.numpy as jnp
        import numpy as np
        NUM_EXPERTS = 8
        HIDDEN = 128
        INTER = 128
        BATCH = 2
        SEQ = 128
        TOP_K = 2
        SWIGLU_ALPHA = 1.702
        LIMIT = 7.0

        def _grouped_mm(x, w, expert_ids):
            onehot = jax.nn.one_hot(expert_ids, w.shape[0], dtype=x.dtype)
            y_all = jnp.einsum('tk,ekn->etn', x, w)
            return jnp.einsum('te,etn->tn', onehot, y_all)

        def _gpt_oss_swiglu(x):
            gate = jnp.minimum(x[..., ::2], LIMIT)
            up = jnp.clip(x[..., 1::2], -LIMIT, LIMIT)
            glu = gate * jax.nn.sigmoid(gate * SWIGLU_ALPHA)
            return (up + 1.0) * glu
        B = hidden_states.shape[0]
        H = hidden_states.shape[-1]
        x = hidden_states.reshape(-1, H)
        M = x.shape[0]
        top_k = router_indices.shape[1]
        num_experts = gate_up_proj.shape[0]
        topk_weights = jnp.take_along_axis(routing_weights, router_indices, axis=1)
        flat_experts = router_indices.reshape(-1)
        sort_idx = jnp.argsort(flat_experts)
        sorted_pos = sort_idx // top_k
        expert_sorted = flat_experts[sort_idx]
        grouped = x[sorted_pos]
        gate_up = _grouped_mm(grouped, gate_up_proj, expert_sorted)
        gate_up = gate_up + gate_up_proj_bias[expert_sorted]
        inter = _gpt_oss_swiglu(gate_up)
        down = _grouped_mm(inter, down_proj, expert_sorted)
        down = down + down_proj_bias[expert_sorted]
        down = down * topk_weights.reshape(-1)[sort_idx][:, None]
        out = jnp.zeros((M, H), x.dtype).at[sorted_pos].add(down)
        return out.reshape(B, -1, H)
    x = x + _L0_xattn_ref(_layernorm(x, axis=-1), ctx_768, mask_BxS2_bk0, L0_xattn_W_q, L0_xattn_W_k, L0_xattn_W_v, L0_xattn_W_o, L0_xattn_b_o)
    x = x + _L0_ffn_ref(_layernorm(x, axis=-1), L0_ffn_w_gate, L0_ffn_w_up, L0_ffn_w_down)
    x = x + _L1_xattn_ref(_layernorm(x, axis=-1), ctx_768, mask_BxS_bf1, mask_BxS2_bf1, L1_xattn_Wq, L1_xattn_Wk, L1_xattn_Wv, L1_xattn_W_film_in, L1_xattn_b_film_in, L1_xattn_W_film_out, L1_xattn_b_film_out, L1_xattn_g_norm_in, L1_xattn_b_norm_in, L1_xattn_g_norm_out, L1_xattn_b_norm_out, L1_xattn_g_ffn, L1_xattn_b_ffn, L1_xattn_W1, L1_xattn_b1, L1_xattn_W2, L1_xattn_b2, L1_xattn_log_dt, L1_xattn_A_re, L1_xattn_A_im, L1_xattn_C_re, L1_xattn_C_im, L1_xattn_D_skip, L1_xattn_mod_gate)
    x = x + _L1_ffn_ref(_layernorm(x, axis=-1), L1_ffn_router_indices, L1_ffn_routing_weights, L1_ffn_gate_up_proj, L1_ffn_gate_up_proj_bias, L1_ffn_down_proj, L1_ffn_down_proj_bias)
    return x

_drawn_inputs = setup_inputs


def setup_inputs(seed=0):
    import zlib

    import numpy as np

    out = dict(_drawn_inputs(seed))
    spreads = {'L1_xattn_b_film_in': (0.0, 0.838),
     'L1_xattn_b_film_out': (0.0, 0.881),
     'L1_xattn_g_norm_in': (1.0, 0.2),
     'L1_xattn_b_norm_in': (0.0, 0.415),
     'L1_xattn_g_norm_out': (1.0, 0.2),
     'L1_xattn_b_norm_out': (0.0, 0.325),
     'L1_xattn_g_ffn': (1.0, 0.6),
     'L1_xattn_b_ffn': (0.0, 0.8),
     'L1_xattn_b1': (0.0, 0.8),
     'L1_xattn_b2': (0.0, 1.033),
     'L1_xattn_A_re': (-0.5, 0.6)}
    factors = {'L0_xattn_b_o': 6.808,
     'L0_ffn_w_gate': 6.593,
     'L0_ffn_w_up': 6.489,
     'L0_ffn_w_down': 6.514,
     'L1_xattn_Wq': 8.0,
     'L1_xattn_Wk': 8.0,
     'L1_xattn_Wv': 6.717,
     'L1_xattn_W_film_in': 8.0,
     'L1_xattn_W_film_out': 8.0,
     'L1_xattn_W1': 3.611,
     'L1_xattn_W2': 3.34,
     'L1_ffn_routing_weights': 8.0,
     'L1_ffn_gate_up_proj': 8.0,
     'L1_ffn_gate_up_proj_bias': 8.0,
     'L1_ffn_down_proj': 8.0,
     'L1_ffn_down_proj_bias': 35.151}
    for name, (base, spread) in spreads.items():
        noise = np.random.default_rng([zlib.crc32(name.encode()), seed]).standard_normal(out[name].shape)
        drawn = base * np.exp(spread * noise) if base else spread * noise
        out[name] = jnp.asarray(drawn.astype(out[name].dtype))
    for name, factor in factors.items():
        out[name] = (out[name] * factor).astype(out[name].dtype)
    return out
```

```python
from contextlib import ExitStack

import numpy as np

import concourse.bass as bass
from concourse import mybir

F32 = mybir.dt.float32
I32 = mybir.dt.int32
U8 = mybir.dt.uint8
ALU = mybir.AluOpType
ACT = mybir.ActivationFunctionType
X = mybir.AxisListType.X
XY = mybir.AxisListType.XY
RMAX = bass.bass_isa.ReduceOp.max

P = 128
SEQ = 64
BATCH = 128
D = 128
C = 96
TOK = BATCH * SEQ
TILES = TOK // P
QT = 4
QUADS = TILES // QT
QN = QT * P
H0, H1 = 8, 4
DH0, DH1 = 64, 32
INTER = 384
IC = INTER // P
HID = 512
NS = 64
EXPERTS = 8
EPS = 1e-5
MAGIC = 12582912.0
FAR = 2.0 ** 100
QMAX = 32767.0
TWO_PI = 2 * np.pi


class Steps:

    def __init__(self, eng, sem):
        self.eng, self.sem, self.base, self.n = eng, sem, 0, 0

    def done(self, ins):
        ins.then_inc(self.sem, 1)
        self.n += 1

    def now(self):
        return self.base + self.n

    def then(self, ins):
        self.done(ins)
        self.eng.wait_ge(self.sem, self.now())


class Each(Steps):

    def __init__(self, eng, sem, per):
        super().__init__(eng, sem)
        self.per = per

    def at(self, i):
        self.base, self.n = i * self.per, 0
        return self


def wait(eng, sem, value):
    if isinstance(value, int) and value <= 0:
        return
    eng.wait_ge(sem, value)


def over_pairs(eng, body, steps=(), pairs=QUADS // 2):
    before = [s.n for s in steps]
    for u in range(2):
        body(0, u)
    per = [s.n - b for s, b in zip(steps, before)]
    start = [s.n for s in steps]
    with eng.Fori(1, pairs - 1) as j:
        for s, b, k in zip(steps, start, per):
            s.base, s.n = (j - 1) * k + b, 0
        for u in range(2):
            body(j, u)
    for s, b, k in zip(steps, start, per):
        s.base, s.n = 0, b + (pairs - 2) * k
    for u in range(2):
        body(pairs - 1, u)


class Memory:

    def __init__(self, nc, stack, tag):
        self.nc, self.stack, self.tag = nc, stack, tag

    def sb(self, name, shape, dt=F32):
        return self.stack.enter_context(self.nc.sbuf_tensor(f"{self.tag}_{name}", list(shape), dt))

    def ps(self, name, shape=(P, 512)):
        return self.stack.enter_context(self.nc.psum_tensor(f"{self.tag}_{name}", list(shape), F32))

    def sem(self, name):
        return self.stack.enter_context(self.nc.semaphore(f"{self.tag}_{name}"))


def row(ap1d):
    return ap1d.rearrange("(a n) -> a n", a=1)


def col(ap1d):
    return ap1d.rearrange("(n a) -> n a", a=1)


def exp_steps(dve, st, x, out, tmp, k, pw, poly):
    ln2_hi = 0.693359375
    ln2_lo = -2.12194440054690583e-4
    st.then(dve.tensor_scalar(k, x, 1.4426950408889634, MAGIC, ALU.mult, ALU.add))
    st.then(dve.tensor_scalar(k, k, MAGIC, -126.0, ALU.subtract, ALU.max))
    st.then(dve.tensor_scalar(k, k, 127.0, None, ALU.min))
    st.then(dve.scalar_tensor_tensor(out=tmp, in0=k, scalar=-ln2_hi, in1=x, op0=ALU.mult, op1=ALU.add))
    st.then(dve.scalar_tensor_tensor(out=tmp, in0=k, scalar=-ln2_lo, in1=tmp, op0=ALU.mult, op1=ALU.add))
    st.then(dve.tensor_scalar(poly, tmp, 1.0 / 5040, None, ALU.mult))
    for c in (1.0 / 720, 1.0 / 120, 1.0 / 24, 1.0 / 6, 0.5, 1.0):
        st.then(dve.scalar_tensor_tensor(out=poly, in0=poly, scalar=c, in1=tmp, op0=ALU.add, op1=ALU.mult))
    st.then(dve.tensor_scalar(pw, k, 127.0, 8388608.0, ALU.add, ALU.mult))
    st.then(dve.scalar_tensor_tensor(out=out, in0=poly, scalar=1.0, in1=pw.bitcast(F32),
                                     op0=ALU.add, op1=ALU.mult))


def prepare(nc, a, g):
    with ExitStack() as stack:
        m = Memory(nc, stack, "pre")
        loaded, late, built, pe_ready, act_st, dve_st, pool_st, stored = (
            m.sem(n) for n in ("loaded", "late", "built", "pe", "act", "dve", "pool", "stored"))
        wq = m.sb("wq", (P, H0 * DH0))
        wk = m.sb("wk", (C, H0 * DH0))
        wv = m.sb("wv", (C, H0 * DH0))
        wo = m.sb("wo", (P, 4, D))
        wq1 = m.sb("wq1", (P, P))
        wk1 = m.sb("wk1", (C, P))
        wv1 = m.sb("wv1", (C, P))
        film = m.sb("film", (P, 4 * D))
        bfilm = m.sb("bfilm", (C + 1, 4 * D))
        qraw = m.sb("qraw", (P, 3, INTER))
        gate_raw = qraw[:, 0, :].rearrange("p (c n) -> p c n", c=IC)
        up_raw = qraw[:, 1, :].rearrange("p (c n) -> p c n", c=IC)
        down_raw = qraw[:, 2, :].rearrange("p (c n) -> p c n", c=IC)
        blocks = qraw[:, :, :].rearrange("p w (b n) -> p (w b) n", n=32)
        bamax = m.sb("bamax", (P, 36))
        binv = m.sb("binv", (P, 36))
        masks = m.sb("masks", (P, 3, SEQ), U8)
        mrows = m.sb("mrows", (P, 2, SEQ))
        tmb = m.sb("tmb", (P, 2, SEQ))
        gate_s = m.sb("gate_s", (P, 1))
        one_col = m.sb("one_col", (P, 1))
        turned = m.sb("turned", (P, 16, P))
        pt = [m.ps(f"t{i}") for i in range(8)]

        logdt = m.sb("logdt", (P, 1))
        are, aim, cre, cim = (m.sb(n, (P, NS)) for n in ("are", "aim", "cre", "cim"))
        dskip = m.sb("dskip", (P, 1))
        dt = m.sb("dt", (P, 1))
        t1k, t1t, t1p = (m.sb(n, (P, 1)) for n in ("t1k", "t1t", "t1p"))
        t1i = m.sb("t1i", (P, 1), I32)
        a1, b1, ea, wr, wi, dr, di, z1, z2, z3, inv = (
            m.sb(n, (P, NS)) for n in ("a1", "b1", "ea", "wr", "wi", "dr", "di", "z1", "z2", "z3", "inv"))
        zi = m.sb("zi", (P, NS), I32)
        phase = m.sb("phase", (P, 16, NS))
        turns = m.sb("turns", (P, 16, NS))
        decay = m.sb("decay", (P, 16, NS))
        sine = m.sb("sine", (P, 16, NS))
        half = m.sb("half", (P, 16, NS))
        cosine = m.sb("cosine", (P, 16, NS))
        ur, ui = m.sb("ur", (P, 8, NS)), m.sb("ui", (P, 8, NS))
        prod, prod2 = m.sb("prod", (P, 8, NS)), m.sb("prod2", (P, 8, NS))
        taps = g.taps_sb[:, :]

        block = stack.enter_context(nc.Block())

        @block.sync
        def _(sp):
            n = 0
            for dst, src in (
                (wq[:, :], a["L0_xattn_W_q"]), (wk[:, :], a["L0_xattn_W_k"]), (wv[:, :], a["L0_xattn_W_v"]),
                (wo[:, :, :], a["L0_xattn_W_o"].rearrange("(c p) n -> p c n", p=P)),
                (g.n0[C:C + 1, 0, :], row(a["L0_xattn_b_o"])),
                (wq1[:, :], a["L1_xattn_Wq"]), (wk1[:, :], a["L1_xattn_Wk"]), (wv1[:, :], a["L1_xattn_Wv"]),
                (film[:, 0:2 * D], a["L1_xattn_W_film_in"]), (film[:, 2 * D:], a["L1_xattn_W_film_out"]),
                (bfilm[C:C + 1, 0:2 * D], row(a["L1_xattn_b_film_in"])),
                (bfilm[C:C + 1, 2 * D:], row(a["L1_xattn_b_film_out"])),
                (gate_raw, a["L0_ffn_w_gate"].rearrange("(c p) n -> p c n", p=P)),
                (up_raw, a["L0_ffn_w_up"].rearrange("(c p) n -> p c n", p=P)),
                (qraw[:, 2, :], a["L0_ffn_w_down"]),
                (masks[:, 0, :], a["mask_BxS2_bk0"]), (masks[:, 1, :], a["mask_BxS2_bf1"]),
                (masks[:, 2, :], a["mask_BxS_bf1"]),
                (gate_s[:, :], bass.AP(a["L1_xattn_mod_gate"].tensor, 0, [[0, P], [1, 1]])),
                (logdt[:, :], col(a["L1_xattn_log_dt"])), (dskip[:, :], col(a["L1_xattn_D_skip"])),
                (are[:, :], a["L1_xattn_A_re"]), (aim[:, :], a["L1_xattn_A_im"]),
                (cre[:, :], a["L1_xattn_C_re"]), (cim[:, :], a["L1_xattn_C_im"]),
                (g.w1[:, :], a["L1_xattn_W1"]),
                (g.w2[:, :, :], a["L1_xattn_W2"].rearrange("(c p) n -> p c n", p=P)),
                (g.b1[:, :], a["L1_xattn_b1"].rearrange("(c p) -> p c", p=P)),
                (g.ffn_g[:, :], col(a["L1_xattn_g_ffn"])), (g.ffn_b[:, :], col(a["L1_xattn_b_ffn"])),
            ):
                with nc.allow_non_contiguous_dma(reason="small constants"):
                    sp.dma_start(dst, src).then_inc(loaded, 16)
                n += 1
            for k, name in enumerate(("g_norm_in", "b_norm_in", "b2", "g_norm_out", "b_norm_out")):
                src = a[f"L1_xattn_{name}"]
                sp.dma_start(g.wide[:, k, :], bass.AP(src.tensor, 0, [[0, P], [1, D]])).then_inc(loaded, 16)
                n += 1
            assert n == 35
            x_src = a["x"].rearrange("b s d -> (b s) d").rearrange("(t p) d -> p t d", p=P)
            for q in range(4):
                sp.dma_start(g.x[:, 16 * q:16 * q + 16, :], x_src[:, 16 * q:16 * q + 16, :]).then_inc(late, 16)
            sp.wait_ge(built, 1)
            sp.dma_start(g.mask_rows.rearrange("m (b s) -> b m s", b=BATCH), mrows[:, :, :]).then_inc(stored, 16)
            sp.wait_ge(built, 2)
            sp.dma_start(g.taps_out, taps.unsqueeze(1).to_broadcast([D, SEQ, 2 * SEQ])).then_inc(g.taps_stored, 16)
            sp.wait_ge(stored, 16)
            sp.wait_ge(late, 64)

        ALL = 16 * 35
        QUANT_AT = 7
        TMASK_AT = 10
        PHASES_AT = TMASK_AT + 14 + 3 + 2 + 3 + 1

        @block.gpsimd
        def _(pool):
            st = Steps(pool, pool_st)
            st.then(pool.memset(g.ident[:, :], 0.0))
            st.then(pool.affine_select(out=g.ident[:, :], in_=g.ident[:, :], compare_op=ALU.not_equal, fill=1.0,
                                       base=0, pattern=[[-1, P]], channel_multiplier=1))
            st.then(pool.memset(g.pairsum[:, :], 0.0))
            for base in (0, -SEQ):
                st.then(pool.affine_select(out=g.pairsum[:, :], in_=g.pairsum[:, :], compare_op=ALU.not_equal,
                                           fill=0.25, base=base, pattern=[[-1, SEQ]], channel_multiplier=1))
            st.then(pool.memset(g.minus_half[:, :], -0.5))
            st.then(pool.memset(g.eps[:, :], EPS))
            st.then(pool.memset(one_col[:, :], 1.0))
            pool.wait_ge(loaded, ALL)
            st.then(pool.memset(g.n0[C:C + 1, 1:H0, :], 0.0))

        turns_of = ([(wq[:, 128 * i:128 * i + 128], P, P) for i in range(4)]
                    + [(wk[:, 128 * i:128 * i + 128], C, P) for i in range(4)]
                    + [(wv[:, 128 * i:128 * i + 128], C, P) for i in range(4)]
                    + [(wq1[:, :], P, P), (wk1[:, :], C, P), (wv1[:, :], C, P)])
        quant_of = ([gate_raw[:, i, :] for i in range(IC)] + [up_raw[:, i, :] for i in range(IC)]
                    + [down_raw[:, i, :] for i in range(IC)])

        @block.tensor
        def _(pe):
            pe.wait_ge(loaded, ALL)
            pe.wait_ge(pool_st, 2)
            for i, (src, rows, cols) in enumerate(turns_of):
                pe.transpose(pt[i // 4][0:cols, 128 * (i % 4):128 * (i % 4) + rows], src,
                             g.ident[0:rows, 0:rows]).then_inc(pe_ready, 1)
            pe.wait_ge(act_st, 1)
            n = len(turns_of)
            for h in range(H0):
                r = DH0 * (h % 2)
                pe.matmul(pt[4 + h % 2][:, 128 * (h // 2):128 * (h // 2) + C], turned[r:r + DH0, h // 2, 0:P],
                          turned[r:r + DH0, 4 + h // 2, 0:C], start=True, stop=True).then_inc(pe_ready, 1)
            for h in range(H0):
                r = DH0 * (h % 2)
                pe.matmul(pt[6 + h % 2][0:C, 128 * (h // 2):128 * (h // 2) + D], turned[r:r + DH0, 8 + h // 2, 0:C],
                          wo[r:r + DH0, h // 2, :], start=True, stop=True).then_inc(pe_ready, 1)
            n += 16
            pe.wait_ge(act_st, 2)
            for h in range(H1):
                r = DH1 * h
                pe.matmul(pt[h][:, 0:C], turned[r:r + DH1, 12, 0:P],
                          turned[r:r + DH1, 13, 0:C], start=True, stop=True).then_inc(pe_ready, 1)
            pe.matmul(pt[4][0:C, :], turned[:, 14, 0:C], film[:, :], start=True, stop=True).then_inc(pe_ready, 1)
            pe.wait_ge(dve_st, QUANT_AT)
            for i, src in enumerate(quant_of):
                pe.transpose(pt[5 + i // 4][:, 128 * (i % 4):128 * (i % 4) + 128], src,
                             g.ident[:, :]).then_inc(pe_ready, 1)
            pe.wait_ge(dve_st, TMASK_AT)
            pe.wait_ge(act_st, 3)
            pe.transpose(pt[0][:, 0:P], tmb[:, :, :].rearrange("p a s -> p (a s)"), g.ident[:, :]).then_inc(pe_ready, 1)

        @block.scalar
        def _(act):
            act.wait_ge(pe_ready, 15)
            st = Steps(act, act_st)
            for b in range(4):
                k = 4 if b < 3 else 3
                rows = P if b in (0, 3) else C
                src = pt[b][:, 0:128 * k].rearrange("p (i n) -> p i n", n=128)
                if b == 3:
                    act.copy(turned[:, 12:13, :], src[:, 0:1, :])
                    ins = act.copy(turned[:, 13:15, 0:C], src[:, 1:3, 0:C])
                else:
                    ins = act.copy(turned[:, 4 * b:4 * b + k, 0:rows], src[:, :, 0:rows])
            st.then(ins)
            act.wait_ge(pe_ready, 31)
            for b in range(2):
                act.copy(g.m0[:, b::2, :],
                         pt[4 + b][:, :].rearrange("p (i n) -> p i n", n=128)[:, :, 0:C])
                ins = act.copy(g.n0[0:C, b::2, :],
                               pt[6 + b][0:C, :].rearrange("p (i n) -> p i n", n=128))
            st.then(ins)
            act.wait_ge(pe_ready, 36)
            for h in range(H1):
                act.copy(g.m1[:, h, :], pt[h][:, 0:C])
            act.mul(g.film[0:C, :], pt[4][0:C, :], gate_s[0:C, 0:1])
            ins = act.mul(g.film[C:C + 1, :], bfilm[C:C + 1, :], gate_s[C:C + 1, 0:1])
            st.then(ins)
            fr = g.film[C:C + 1, :].rearrange("p (a b n) -> p a b n", a=2, b=2)
            act.wait_ge(pool_st, 8)
            st.then(act.activation(fr[:, :, 0, :], fr[:, :, 0, :], ACT.Identity, bias=one_col[C:C + 1, 0:1]))
            act.wait_ge(pe_ready, 45)
            act.copy(g.gate_t[:, 0:3 * P], pt[5][:, 0:3 * P])
            act.copy(g.up_t[:, 0:P], pt[5][:, 3 * P:])
            act.copy(g.up_t[:, P:3 * P], pt[6][:, 0:2 * P])
            act.copy(g.down_t[:, 0:2, :], pt[6][:, 2 * P:].rearrange("p (i n) -> p i n", n=P))
            ins = act.copy(g.down_t[:, 2, :], pt[7][:, 0:P])
            act.wait_ge(pe_ready, 46)
            ins = act.copy(g.tmask[:, :], pt[0][:, 0:P])
            st.then(ins)
            act.wait_ge(dve_st, PHASES_AT)
            st.then(act.activation(decay[:, :, :], decay[:, :, :], ACT.Exp))
            act.activation(sine[:, :, :], phase[:, :, :], ACT.Sin)
            st.then(act.activation(half[:, :, :], phase[:, :, :], ACT.Sin, scale=0.5))

        @block.vector
        def _(dve):
            st = Steps(dve, dve_st)
            dve.wait_ge(loaded, ALL)
            st.then(dve.tensor_reduce(bamax[:, :], blocks, X, ALU.max, apply_absolute_value=True))
            st.then(dve.tensor_scalar(bamax[:, :], bamax[:, :], 1.0 / 7.0, 1e-12, ALU.mult, ALU.max))
            st.then(dve.reciprocal(binv[:, :], bamax[:, :]))
            st.then(dve.tensor_tensor(blocks, blocks, binv[:, :].unsqueeze(2).to_broadcast([P, 36, 32]), ALU.mult))
            st.then(dve.tensor_scalar(blocks, blocks, MAGIC, MAGIC, ALU.add, ALU.subtract))
            st.then(dve.tensor_scalar(blocks, blocks, 7.0, -8.0, ALU.min, ALU.max))
            st.then(dve.tensor_tensor(blocks, blocks, bamax[:, :].unsqueeze(2).to_broadcast([P, 36, 32]), ALU.mult))
            assert st.n == QUANT_AT
            st.then(dve.tensor_scalar(mrows[:, :, :], masks[:, 0:2, :], -1.0, FAR, ALU.add, ALU.mult))
            dve.sem_inc(built, 1)
            st.then(dve.tensor_copy(tmb[:, 0, :], masks[:, 2, :]))
            st.then(dve.tensor_copy(tmb[:, 1, :], masks[:, 2, :]))
            assert st.n == TMASK_AT
            exp_steps(dve, st, logdt[:, :], dt[:, :], t1t[:, :], t1k[:, :], t1i[:, :], t1p[:, :])
            st.then(dve.tensor_scalar(a1[:, :], are[:, :], dt[:, 0:1], None, ALU.mult))
            st.then(dve.tensor_scalar(b1[:, :], aim[:, :], dt[:, 0:1], None, ALU.mult))
            for k in range(16):
                f = float(k if k < 8 else 8 * (k - 8))
                dve.tensor_scalar(phase[:, k, :], b1[:, :], f, None, ALU.mult)
                last = dve.tensor_scalar(decay[:, k, :], a1[:, :], f, None, ALU.mult)
            st.then(last)
            st.then(dve.tensor_scalar(turns[:, :, :], phase[:, :, :], 1 / TWO_PI, MAGIC, ALU.mult, ALU.add))
            st.then(dve.tensor_scalar(turns[:, :, :], turns[:, :, :], MAGIC, None, ALU.subtract))
            c1 = 6.28125
            c2 = float(np.float32(np.round((TWO_PI - c1) * 2 ** 21) / 2 ** 21))
            c3 = TWO_PI - c1 - c2
            for c in (c1, c2, c3):
                st.then(dve.scalar_tensor_tensor(out=phase[:, :, :], in0=turns[:, :, :], scalar=-c,
                                                 in1=phase[:, :, :], op0=ALU.mult, op1=ALU.add))
            st.then(dve.tensor_scalar(phase[:, :, :], phase[:, :, :], 3.1415925, -3.1415925, ALU.min, ALU.max))
            assert st.n == PHASES_AT, st.n
            exp_steps(dve, st, a1[:, :], ea[:, :], z1[:, :], z2[:, :], zi[:, :], z3[:, :])
            dve.wait_ge(act_st, 7)
            st.then(dve.tensor_tensor(half[:, :, :], half[:, :, :], half[:, :, :], ALU.mult))
            st.then(dve.tensor_scalar(cosine[:, :, :], half[:, :, :], -2.0, 1.0, ALU.mult, ALU.add))
            st.then(dve.scalar_tensor_tensor(out=z1[:, :], in0=ea[:, :], scalar=-1.0, in1=cosine[:, 1, :],
                                             op0=ALU.add, op1=ALU.mult))
            st.then(dve.scalar_tensor_tensor(out=wr[:, :], in0=half[:, 1, :], scalar=-2.0, in1=z1[:, :],
                                             op0=ALU.mult, op1=ALU.add))
            st.then(dve.tensor_tensor(wi[:, :], ea[:, :], sine[:, 1, :], ALU.mult))
            st.then(dve.tensor_tensor(z1[:, :], are[:, :], are[:, :], ALU.mult))
            st.then(dve.tensor_tensor(z2[:, :], aim[:, :], aim[:, :], ALU.mult))
            st.then(dve.tensor_tensor(z1[:, :], z1[:, :], z2[:, :], ALU.add))
            st.then(dve.reciprocal(inv[:, :], z1[:, :]))

            def complex_mult(outr, outi, xr, xi, yr, yi, sign, scale, t1, t2):
                st.then(dve.tensor_tensor(t1, xi, yi, ALU.mult))
                st.then(dve.tensor_tensor(t2, xr, yi, ALU.mult))
                st.then(dve.tensor_tensor(outr, xr, yr, ALU.mult))
                st.then(dve.scalar_tensor_tensor(out=outr, in0=t1, scalar=-float(sign), in1=outr, op0=ALU.mult, op1=ALU.add))
                st.then(dve.tensor_tensor(outi, xi, yr, ALU.mult))
                st.then(dve.scalar_tensor_tensor(out=outi, in0=t2, scalar=float(sign), in1=outi, op0=ALU.mult, op1=ALU.add))

            complex_mult(dr[:, :], di[:, :], wr[:, :], wi[:, :], are[:, :], aim[:, :], -1, 1, z1[:, :], z2[:, :])
            st.then(dve.tensor_tensor(dr[:, :], dr[:, :], inv[:, :], ALU.mult))
            st.then(dve.tensor_tensor(di[:, :], di[:, :], inv[:, :], ALU.mult))
            complex_mult(wr[:, :], wi[:, :], dr[:, :], di[:, :], cre[:, :], cim[:, :], 1, 1, z1[:, :], z2[:, :])
            st.then(dve.tensor_scalar(wr[:, :], wr[:, :], 2.0, None, ALU.mult))
            st.then(dve.tensor_scalar(wi[:, :], wi[:, :], 2.0, None, ALU.mult))
            st.then(dve.tensor_tensor(cosine[:, :, :], cosine[:, :, :], decay[:, :, :], ALU.mult))
            st.then(dve.tensor_tensor(sine[:, :, :], sine[:, :, :], decay[:, :, :], ALU.mult))
            wrb = wr[:, :].unsqueeze(1).to_broadcast([P, 8, NS])
            wib = wi[:, :].unsqueeze(1).to_broadcast([P, 8, NS])
            complex_mult(ur[:, :, :], ui[:, :, :], cosine[:, 8:16, :], sine[:, 8:16, :], wrb, wib, 1, 1,
                         prod[:, :, :], prod2[:, :, :])
            st.then(dve.memset(taps[:, 0:SEQ], 0.0))
            for l1 in range(8):
                st.then(dve.tensor_tensor(prod[:, :, :], cosine[:, 0:8, :],
                                          ur[:, l1, :].unsqueeze(1).to_broadcast([P, 8, NS]), ALU.mult))
                st.then(dve.tensor_tensor(prod2[:, :, :], sine[:, 0:8, :],
                                          ui[:, l1, :].unsqueeze(1).to_broadcast([P, 8, NS]), ALU.mult))
                st.then(dve.tensor_tensor(prod[:, :, :], prod[:, :, :], prod2[:, :, :], ALU.subtract))
                st.then(dve.tensor_reduce(taps[:, SEQ + 8 * l1:SEQ + 8 * l1 + 8], prod[:, :, :], X, ALU.add))
            st.then(dve.tensor_tensor(taps[:, SEQ:SEQ + 1], taps[:, SEQ:SEQ + 1], dskip[:, :], ALU.add))
            dve.sem_inc(built, 1)


def norm_steps(dve, carry, pool_done, st, x_tiles, stats, mv, out_tiles, pool_ready, count):
    for t in range(QT):
        last = dve.bn_stats(stats[:, t, :], x_tiles[t])
    st.then(last)
    dve.memset(carry[:, 0:1], 0.0)
    for t in range(QT):
        last = dve.bn_aggr(mv[:, t, :], stats[:, t, :])
    last.then_inc(pool_ready, 1)
    dve.wait_ge(pool_done, count + 1)
    for t in range(QT):
        last = dve.tensor_scalar(out_tiles[t], x_tiles[t], mv[:, t, 0:1], mv[:, t, 1:2], ALU.subtract, ALU.mult)
    return last


def rstd_steps(pool, g, mv, stats_ready, rstd_ready, link, count):
    pool.wait_ge(stats_ready, count + 1)
    link.then(pool.tensor_tensor(mv[:, :, 1:2], mv[:, :, 1:2], g.eps[:, 0:QT].unsqueeze(2), ALU.add))
    pool.tensor_tensor(mv[:, :, 1:2], mv[:, :, 1:2], g.minus_half[:, 0:QT].unsqueeze(2), ALU.pow).then_inc(rstd_ready, 1)


def attention0(nc, a, g):
    with ExitStack() as stack:
        m = Memory(nc, stack, "at0")
        ctx_in = [m.sem(f"ctx_in{u}") for u in range(2)]
        stats_ready, rstd_ready = m.sem("stats_ready"), m.sem("rstd_ready")
        xn_ready = m.sem("xn_ready")
        ring_ready, ring_evac = m.sem("ring_ready"), m.sem("ring_evac")
        s_ready, shifted, exp_ready = m.sem("s_ready"), m.sem("shifted"), m.sem("exp_ready")
        inv_ready, prob_ready = m.sem("inv_ready"), m.sem("prob_ready")
        pt_ready, pt_evac = m.sem("pt_ready"), m.sem("pt_evac")
        c_ready, c_evac = m.sem("c_ready"), m.sem("c_evac")
        o_ready, x_added = m.sem("o_ready"), m.sem("x_added")
        dve_st, pool_st = m.sem("dve_st"), m.sem("pool_st")

        xn = m.sb("xn", (P, 2, QT, P))
        xnt = m.sb("xnt", (P, 2, QN))
        ctxn = m.sb("ctxn", (P, 2, QT, C))
        ctxt = m.sb("ctxt", (C + 2, 2, QN))
        qm = m.sb("qm", (C + 2, 2, 2 * QT, H0 * SEQ))
        stats = m.sb("stats", (P, 2, QT, 6))
        mv = m.sb("mv", (P, 2, QT, 2))
        sd = m.sb("sd", (P, 2, 8, SEQ))
        mx, sm = m.sb("mx", (P, 2, 8)), m.sb("sm", (P, 2, 8))
        pr = m.sb("pr", (P, 2, 8, SEQ))
        pts = m.sb("pts", (P, 2, 4 * P))
        ct = m.sb("ct", (C + 1, 2, H0, P))
        ring = [m.ps(f"ring{i}") for i in range(2)]
        sp_ = [m.ps(f"s{i}") for i in range(2)]
        ptp = m.ps("pt")
        cp = [m.ps(f"c{i}") for i in range(2)]
        op = m.ps("o")
        block = stack.enter_context(nc.Block())
        RING = 10
        pieces = ((0, 1, 2), (3, 4, 5), (6, 7, 8, 9), ())
        ctx_src = a["ctx_768"].rearrange("b s c -> (b s) c").rearrange("(q t p) c -> q p t c", p=P, t=QT)
        mask_src = g.mask_rows.rearrange("m (q n) -> q m n", q=QUADS)

        @block.sync
        def _(sp):
            def load(j, u):
                q = 2 * j + u
                wait(sp, c_ready, 8 * (q - 1))
                sp.dma_start(ctxn[:, u, :, :], at_quad(ctx_src, q)).then_inc(ctx_in[u], 16)
                sp.dma_start(ctxt[C:C + 2, u, :], at_quad(mask_src, q)).then_inc(ctx_in[u], 16)
            over_pairs(sp, load)

        def front_pe(pe, j, u, ks):
            q = 2 * j + u
            for k in ks:
                n = RING * q + k
                slot = ring[k % 2]
                if k == 0:
                    pe.wait_ge(ctx_in[u], 32 * (j + 1))
                if k == 1:
                    pe.wait_ge(xn_ready, q + 1)
                wait(pe, ring_evac, n - 1 if k != 2 else n)
                if k == 0:
                    for t in range(QT):
                        last = pe.transpose(slot[0:C, t * P:t * P + P], ctxn[:, u, t, :], g.ident[:, :])
                elif k == 1:
                    for t in range(QT):
                        last = pe.transpose(slot[:, t * P:t * P + P], xn[:, u, t, :], g.ident[:, :])
                else:
                    last = pe.matmul(slot[0:C, :], g.m0[:, k - 2, :], xnt[:, u, :], start=True, stop=True)
                last.then_inc(ring_ready, 1)

        def front_act(act, j, u, ks):
            q = 2 * j + u
            for k in ks:
                act.wait_ge(ring_ready, RING * q + k + 1)
                slot = ring[k % 2]
                if k == 0:
                    ins = act.copy(ctxt[0:C, u, :], slot[0:C, :])
                elif k == 1:
                    ins = act.copy(xnt[:, u, :], slot[:, :])
                else:
                    ins = act.copy(qm[0:C, u, :, (k - 2) * SEQ:(k - 1) * SEQ],
                                   slot[0:C, :].rearrange("c (b s) -> c b s", s=SEQ))
                ins.then_inc(ring_evac, 1)

        @block.tensor
        def _(pe):
            def scores(j, u, t):
                q, n = 2 * j + u, 8 * j + 4 * u + t
                wait(pe, ring_evac, RING * (q + 1))
                wait(pe, shifted, n - 1)
                for b in range(2):
                    tok = slice(t * P + b * SEQ, t * P + b * SEQ + SEQ)
                    for p in range(4):
                        c0 = (2 * p + b) * SEQ
                        last = pe.matmul(sp_[t % 2][:, c0:c0 + SEQ], qm[:, u, 2 * t + b, 2 * p * SEQ:2 * (p + 1) * SEQ],
                                         ctxt[:, u, tok], start=True, stop=True)
                last.then_inc(s_ready, 1)

            def turn(n, t):
                pe.wait_ge(prob_ready, n + 1)
                wait(pe, pt_evac, n)
                for p in range(4):
                    last = pe.transpose(ptp[:, p * P:p * P + P],
                                        pr[:, t % 2, 2 * p:2 * p + 2, :].rearrange("p a s -> p (a s)"), g.ident[:, :])
                last.then_inc(pt_ready, 1)

            def attend(n, u, t):
                pe.wait_ge(pt_evac, n + 1)
                for b in range(2):
                    wait(pe, c_evac, 2 * n - 1 + b)
                    r = slice(b * SEQ, b * SEQ + SEQ)
                    pe.matmul(cp[b][0:C, :], ctxn[r, u, t, :], pts[r, t % 2, :],
                              start=True, stop=True).then_inc(c_ready, 1)

            def project(n, q, t):
                pe.wait_ge(c_evac, 2 * n + 2)
                if t == 0:
                    wait(pe, x_added, q)
                for h in range(H0):
                    last = pe.matmul(op[:, t * P:t * P + P], ct[:, t % 2, h, :], g.n0[:, h, :],
                                     start=(h == 0), stop=(h == H0 - 1))
                last.then_inc(o_ready, 1)

            def body(j, u):
                for t in range(QT):
                    n, q = 8 * j + 4 * u + t, 2 * j + u
                    more = not (isinstance(q, int) and q == QUADS - 1)
                    if more:
                        front_pe(pe, j + (u == 1), 1 - u, pieces[t])
                    if t < 3:
                        scores(j, u, t + 1)
                    elif more:
                        scores(j + (u == 1), 1 - u, 0)
                    turn(n, t)
                    attend(n, u, t)
                    if t > 0:
                        project(n - 1, q, t - 1)
                    elif not (isinstance(q, int) and q == 0):
                        project(n - 1, q - 1, 3)

            pe.wait_ge(pool_st, 3)
            front_pe(pe, 0, 0, range(RING))
            scores(0, 0, 0)
            over_pairs(pe, body)
            project(TILES - 1, QUADS - 1, 3)

        @block.scalar
        def _(act):
            def exps(n, t):
                act.wait_ge(shifted, n + 1)
                act.activation(sd[:, t % 2, :, :], sd[:, t % 2, :, :], ACT.Exp, scale=DH0 ** -0.5).then_inc(exp_ready, 1)

            def body(j, u):
                for t in range(QT):
                    n, q = 8 * j + 4 * u + t, 2 * j + u
                    more = not (isinstance(q, int) and q == QUADS - 1)
                    if more:
                        front_act(act, j + (u == 1), 1 - u, pieces[t])
                    act.wait_ge(pt_ready, n + 1)
                    act.copy(pts[:, t % 2, :], ptp[:, :]).then_inc(pt_evac, 1)
                    for b in range(2):
                        act.wait_ge(c_ready, 2 * n + 1 + b)
                        act.copy(ct[0:C, t % 2, :, b * SEQ:b * SEQ + SEQ],
                                 cp[b][0:C, :].rearrange("p (h s) -> p h s", s=SEQ)).then_inc(c_evac, 1)
                    if more or t < 3:
                        exps(n + 1, t + 1)

            front_act(act, 0, 0, range(RING))
            exps(0, 0)
            over_pairs(act, body)

        @block.gpsimd
        def _(pool):
            st = Steps(pool, pool_st)
            st.then(pool.memset(qm[C:C + 2, :, :, :], 0.0))
            st.then(pool.memset(qm[C:C + 1, :, :, :], 1.0))
            st.then(pool.memset(ct[C:C + 1, :, :, :], 1.0))

            def rstd(j, u):
                rstd_steps(pool, g, mv[:, u, :, :], stats_ready, rstd_ready, st, 2 * j + u)

            def body(j, u):
                for t in range(QT):
                    n, q = 8 * j + 4 * u + t, 2 * j + u
                    pool.wait_ge(inv_ready, n + 1)
                    wait(pool, pt_ready, n - 1)
                    pool.tensor_tensor(pr[:, t % 2, :, :], sd[:, t % 2, :, :],
                                       sm[:, t % 2, :].unsqueeze(2).to_broadcast([P, 8, SEQ]),
                                       ALU.mult).then_inc(prob_ready, 1)
                    if t == 2 and not (isinstance(q, int) and q >= QUADS - 2):
                        rstd(j + 1, u)

            rstd(0, 0)
            rstd(0, 1)
            over_pairs(pool, body, [st])

        @block.vector
        def _(dve):
            st = Steps(dve, dve_st)

            def norm(j, u):
                q = 2 * j + u
                tiles = [g.xt(q, t) for t in range(QT)]
                last = norm_steps_a(q, u, tiles)

            def norm_steps_a(q, u, tiles):
                wait(dve, ring_ready, RING * (q - 2) + 2)
                last = norm_steps(dve, g.carry, rstd_ready, st, tiles, stats[:, u, :, :], mv[:, u, :, :],
                                  [xn[:, u, t, :] for t in range(QT)], stats_ready, q)
                last.then_inc(xn_ready, 1)

            def shift(n, t):
                dve.wait_ge(s_ready, n + 1)
                src = sp_[t % 2][:, :].rearrange("p (k s) -> p k s", s=SEQ)
                st.then(dve.tensor_reduce(mx[:, t % 2, :], src, X, ALU.max))
                wait(dve, prob_ready, n - 1)
                dve.tensor_tensor(sd[:, t % 2, :, :], src, mx[:, t % 2, :].unsqueeze(2).to_broadcast([P, 8, SEQ]),
                                  ALU.subtract).then_inc(shifted, 1)

            def sums(n, t):
                dve.wait_ge(exp_ready, n + 1)
                st.then(dve.tensor_reduce(sm[:, t % 2, :], sd[:, t % 2, :, :], X, ALU.add))
                dve.reciprocal(sm[:, t % 2, :], sm[:, t % 2, :]).then_inc(inv_ready, 1)

            def add(q):
                dve.wait_ge(o_ready, 4 * (q + 1))
                xs = g.xq(q)
                dve.tensor_tensor(xs, xs, op[:, :], ALU.add).then_inc(x_added, 1)

            def body(j, u):
                for t in range(QT):
                    n, q = 8 * j + 4 * u + t, 2 * j + u
                    sums(n, t)
                    if t < 3 or not (isinstance(q, int) and q == QUADS - 1):
                        shift(n + 1, t + 1)
                    if t == 0 and not (isinstance(q, int) and q == 0):
                        add(q - 1)
                    if t == 2 and not (isinstance(q, int) and q >= QUADS - 2):
                        norm(j + 1, u)

            norm(0, 0)
            norm(0, 1)
            shift(0, 0)
            over_pairs(dve, body, [st])
            add(QUADS - 1)


class Quantised:

    def __init__(self, nc, stack):
        m = Memory(nc, stack, "ffn")
        self.h_t = m.sb("h_t", (P, TOK))
        self.act = m.sb("act", (P, IC, TOK))
        self.peak = m.sb("peak", (P, 2, QUADS))
        self.top = m.sb("top", (P, 2))
        self.scale = m.sb("scale", (P, 5))
        self.inv = m.sb("inv", (P, 5))

    def piece(self, q):
        return self.h_t[:, bass.ds(q * QN, QN)]

    def act_piece(self, q):
        return self.act[:, :, bass.ds(q * QN, QN)]


H_IN, H_UP, H_GATE, H_GATED, H_OUT = range(5)


def scale_dve(dve, st, f, kinds, peak_ready, top_ready):
    n = len(kinds)
    dve.tensor_reduce(f.top[:, 0:n], f.peak[:, 0:n, :], X, ALU.max).then_inc(peak_ready, 1)
    dve.wait_ge(top_ready, 1)
    k = slice(kinds[0], kinds[0] + n)
    st.then(dve.tensor_scalar(f.scale[:, k], f.top[:, 0:n], 1.0 / QMAX, 1e-12, ALU.mult, ALU.max))
    st.then(dve.reciprocal(f.inv[:, k], f.scale[:, k]))


def scale_pool(pool, f, n, peak_ready, top_ready):
    pool.wait_ge(peak_ready, 1)
    pool.partition_all_reduce(f.top[:, 0:n], f.top[:, 0:n], P, RMAX).then_inc(top_ready, 1)


def act_quant(nc, a, g):
    f = g.f
    with ExitStack() as stack:
        m = Memory(nc, stack, "aq")
        stats_ready, rstd_ready, xn_ready = m.sem("stats_ready"), m.sem("rstd_ready"), m.sem("xn_ready")
        turned, evac, peaked = m.sem("turned"), m.sem("evac"), m.sem("peaked")
        peak_ready, top_ready = m.sem("peak_ready"), m.sem("top_ready")
        dve_st, pool_st = m.sem("dve_st"), m.sem("pool_st")
        xn = m.sb("xn", (P, 2, QT, P))
        stats = m.sb("stats", (P, 2, QT, 6))
        mv = m.sb("mv", (P, 2, QT, 2))
        bank = [m.ps(f"t{i}") for i in range(2)]
        block = stack.enter_context(nc.Block())

        @block.tensor
        def _(pe):
            def body(j, u):
                q = 2 * j + u
                pe.wait_ge(xn_ready, q + 1)
                wait(pe, evac, q - 1)
                for t in range(QT):
                    last = pe.transpose(bank[u][:, t * P:t * P + P], xn[:, u, t, :], g.ident[:, :])
                last.then_inc(turned, 1)
            over_pairs(pe, body)

        @block.scalar
        def _(act):
            def body(j, u):
                q = 2 * j + u
                act.wait_ge(turned, q + 1)
                act.copy(f.piece(q), bank[u][:, :]).then_inc(evac, 1)
            over_pairs(act, body)

        @block.gpsimd
        def _(pool):
            st = Steps(pool, pool_st)
            over_pairs(pool, lambda j, u: rstd_steps(pool, g, mv[:, u, :, :], stats_ready, rstd_ready, st, 2 * j + u),
                       [st])
            scale_pool(pool, f, 1, peak_ready, top_ready)

        @block.vector
        def _(dve):
            st = Steps(dve, dve_st)

            def norm(j, u):
                q = 2 * j + u
                wait(dve, turned, q - 1)
                norm_steps(dve, g.carry, rstd_ready, st, [g.xt(q, t) for t in range(QT)], stats[:, u, :, :],
                           mv[:, u, :, :], [xn[:, u, t, :] for t in range(QT)], stats_ready, q).then_inc(xn_ready, 1)

            def body(j, u):
                q = 2 * j + u
                if not (isinstance(q, int) and q == QUADS - 1):
                    norm(j + u, 1 - u)
                dve.wait_ge(evac, q + 1)
                dve.tensor_reduce(f.peak[:, 0, bass.ds(q, 1)], f.piece(q), X, ALU.max,
                                  apply_absolute_value=True).then_inc(peaked, 1)

            norm(0, 0)
            over_pairs(dve, body, [st])
            dve.wait_ge(peaked, QUADS)
            scale_dve(dve, st, f, [H_IN], peak_ready, top_ready)
            dve.wait_ge(evac, QUADS)
            for i in range(4):
                h = f.h_t[:, i * TOK // 4:(i + 1) * TOK // 4]
                st.then(dve.tensor_scalar(h, h, f.inv[:, H_IN:H_IN + 1], MAGIC, ALU.mult, ALU.add))
                st.then(dve.tensor_scalar(h, h, MAGIC, f.scale[:, H_IN:H_IN + 1], ALU.subtract, ALU.mult))


def gate_up_max(nc, a, g):
    f = g.f
    with ExitStack() as stack:
        m = Memory(nc, stack, "gum")
        made, peaked, peak_ready, top_ready, dve_st = (
            m.sem(n) for n in ("made", "peaked", "peak_ready", "top_ready", "dve_st"))
        group = [m.ps(f"p{i}", (P, IC, 512)) for i in range(2)]
        block = stack.enter_context(nc.Block())

        @block.tensor
        def _(pe):
            def body(j, u):
                q = 2 * j + u
                for k, w in enumerate((g.up_t, g.gate_t)):
                    wait(pe, peaked, 2 * q + k - 1)
                    for c in range(IC):
                        last = pe.matmul(group[k][:, c, :], w[:, c * P:c * P + P], f.piece(q), start=True, stop=True)
                    last.then_inc(made, 1)
            over_pairs(pe, body)

        @block.gpsimd
        def _(pool):
            scale_pool(pool, f, 2, peak_ready, top_ready)

        @block.vector
        def _(dve):
            st = Steps(dve, dve_st)

            def body(j, u):
                q = 2 * j + u
                for k in range(2):
                    dve.wait_ge(made, 2 * q + k + 1)
                    dve.tensor_reduce(f.peak[:, k, bass.ds(q, 1)], group[k][:, :, :], XY, ALU.max,
                                      apply_absolute_value=True).then_inc(peaked, 1)
            over_pairs(dve, body)
            dve.wait_ge(peaked, 2 * QUADS)
            scale_dve(dve, st, f, [H_UP, H_GATE], peak_ready, top_ready)


def gate(nc, a, g):
    f = g.f
    with ExitStack() as stack:
        m = Memory(nc, stack, "gate")
        made, shifted, rounded, sig_ready, peaked, peak_ready, top_ready, dve_st = (
            m.sem(n) for n in ("made", "shifted", "rounded", "sig_ready", "peaked", "peak_ready", "top_ready", "dve_st"))
        group = [m.ps(f"p{i}", (P, IC, 512)) for i in range(2)]
        gt = m.sb("gt", (P, 2, IC, QN))
        sg = m.sb("sg", (P, 2, IC, QN))
        magic = m.sb("magic", (P, 1))
        block = stack.enter_context(nc.Block())

        @block.tensor
        def _(pe):
            def body(j, u):
                q = 2 * j + u
                wait(pe, shifted, q - 1)
                for c in range(IC):
                    last = pe.matmul(group[u][:, c, :], g.gate_t[:, c * P:c * P + P], f.piece(q), start=True, stop=True)
                last.then_inc(made, 1)
            over_pairs(pe, body)

        @block.scalar
        def _(act):
            def shift(j, u):
                q = 2 * j + u
                act.wait_ge(made, q + 1)
                wait(act, peaked, q - 1)
                act.activation(gt[:, u, :, :], group[u][:, :, :], ACT.Identity, scale=f.inv[:, H_GATE:H_GATE + 1],
                               bias=magic[:, 0:1]).then_inc(shifted, 1)

            def body(j, u):
                q = 2 * j + u
                if not (isinstance(q, int) and q == QUADS - 1):
                    shift(j + u, 1 - u)
                act.wait_ge(rounded, q + 1)
                act.activation(sg[:, u, :, :], gt[:, u, :, :], ACT.Sigmoid).then_inc(sig_ready, 1)
            act.wait_ge(dve_st, 1)
            shift(0, 0)
            over_pairs(act, body)

        @block.gpsimd
        def _(pool):
            scale_pool(pool, f, 1, peak_ready, top_ready)

        @block.vector
        def _(dve):
            st = Steps(dve, dve_st)

            def grid(j, u):
                q = 2 * j + u
                dve.wait_ge(shifted, q + 1)
                dve.tensor_scalar(gt[:, u, :, :], gt[:, u, :, :], MAGIC, f.scale[:, H_GATE:H_GATE + 1],
                                  ALU.subtract, ALU.mult).then_inc(rounded, 1)

            def body(j, u):
                q = 2 * j + u
                if not (isinstance(q, int) and q == QUADS - 1):
                    grid(j + u, 1 - u)
                dve.wait_ge(sig_ready, q + 1)
                s = sg[:, u, :, :]
                st.then(dve.tensor_scalar(s, s, 65536.0, MAGIC, ALU.mult, ALU.add))
                st.then(dve.tensor_scalar(s, s, MAGIC + 65535.0, MAGIC, ALU.min, ALU.subtract))
                st.then(dve.scalar_tensor_tensor(out=f.act_piece(q), in0=s, scalar=1.0 / 65536, in1=gt[:, u, :, :],
                                                 op0=ALU.mult, op1=ALU.mult))
                dve.tensor_reduce(f.peak[:, 0, bass.ds(q, 1)], f.act_piece(q), XY, ALU.max,
                                  apply_absolute_value=True).then_inc(peaked, 1)
            st.then(dve.memset(magic[:, :], MAGIC))
            grid(0, 0)
            over_pairs(dve, body, [st])
            dve.wait_ge(peaked, QUADS)
            scale_dve(dve, st, f, [H_GATED], peak_ready, top_ready)


def up(nc, a, g):
    f = g.f
    with ExitStack() as stack:
        m = Memory(nc, stack, "up")
        made, shifted, again, peaked, peak_ready, top_ready, dve_st = (
            m.sem(n) for n in ("made", "shifted", "again", "peaked", "peak_ready", "top_ready", "dve_st"))
        group = [m.ps(f"p{i}", (P, IC, 512)) for i in range(2)]
        ut = m.sb("ut", (P, 2, IC, QN))
        gt = m.sb("gt", (P, 2, IC, QN))
        magic = m.sb("magic", (P, 1))
        block = stack.enter_context(nc.Block())

        @block.tensor
        def _(pe):
            def body(j, u):
                q = 2 * j + u
                wait(pe, shifted, q - 1)
                for c in range(IC):
                    last = pe.matmul(group[u][:, c, :], g.up_t[:, c * P:c * P + P], f.piece(q), start=True, stop=True)
                last.then_inc(made, 1)
            over_pairs(pe, body)

        @block.scalar
        def _(act):
            def body(j, u):
                q = 2 * j + u
                wait(act, peaked, q - 1)
                act.activation(gt[:, u, :, :], f.act_piece(q), ACT.Identity, scale=f.inv[:, H_GATED:H_GATED + 1],
                               bias=magic[:, 0:1]).then_inc(again, 1)
                act.wait_ge(made, q + 1)
                act.activation(ut[:, u, :, :], group[u][:, :, :], ACT.Identity, scale=f.inv[:, H_UP:H_UP + 1],
                               bias=magic[:, 0:1]).then_inc(shifted, 1)
            act.wait_ge(dve_st, 1)
            over_pairs(act, body)

        @block.gpsimd
        def _(pool):
            scale_pool(pool, f, 1, peak_ready, top_ready)

        @block.vector
        def _(dve):
            st = Steps(dve, dve_st)

            def body(j, u):
                q = 2 * j + u
                gv, uv = gt[:, u, :, :], ut[:, u, :, :]
                dve.wait_ge(again, q + 1)
                st.done(dve.tensor_scalar(gv, gv, MAGIC, f.scale[:, H_GATED:H_GATED + 1], ALU.subtract, ALU.mult))
                dve.wait_ge(shifted, q + 1)
                st.then(dve.tensor_scalar(uv, uv, MAGIC, f.scale[:, H_UP:H_UP + 1], ALU.subtract, ALU.mult))
                st.then(dve.tensor_tensor(f.act_piece(q), gv, uv, ALU.mult))
                dve.tensor_reduce(f.peak[:, 0, bass.ds(q, 1)], f.act_piece(q), XY, ALU.max,
                                  apply_absolute_value=True).then_inc(peaked, 1)
            st.then(dve.memset(magic[:, :], MAGIC))
            over_pairs(dve, body, [st])
            dve.wait_ge(peaked, QUADS)
            scale_dve(dve, st, f, [H_OUT], peak_ready, top_ready)


def down(nc, a, g):
    f = g.f
    with ExitStack() as stack:
        m = Memory(nc, stack, "down")
        shifted, rounded, made, added, dve_st = (m.sem(n) for n in ("shifted", "rounded", "made", "added", "dve_st"))
        ot = m.sb("ot", (P, 2, IC, QN))
        magic = m.sb("magic", (P, 1))
        bank = [m.ps(f"o{i}") for i in range(2)]
        block = stack.enter_context(nc.Block())

        @block.scalar
        def _(act):
            def body(j, u):
                q = 2 * j + u
                wait(act, made, q - 1)
                act.activation(ot[:, u, :, :], f.act_piece(q), ACT.Identity, scale=f.inv[:, H_OUT:H_OUT + 1],
                               bias=magic[:, 0:1]).then_inc(shifted, 1)
            act.wait_ge(dve_st, 1)
            over_pairs(act, body)

        @block.tensor
        def _(pe):
            def body(j, u):
                q = 2 * j + u
                pe.wait_ge(rounded, q + 1)
                wait(pe, added, q - 1)
                for t in range(QT):
                    for c in range(IC):
                        last = pe.matmul(bank[u][:, t * P:t * P + P], ot[:, u, c, t * P:t * P + P], g.down_t[:, c, :],
                                         start=(c == 0), stop=(c == IC - 1))
                last.then_inc(made, 1)
            over_pairs(pe, body)

        @block.vector
        def _(dve):
            st = Steps(dve, dve_st)

            def grid(j, u):
                q = 2 * j + u
                dve.wait_ge(shifted, q + 1)
                dve.tensor_scalar(ot[:, u, :, :], ot[:, u, :, :], MAGIC, f.scale[:, H_OUT:H_OUT + 1],
                                  ALU.subtract, ALU.mult).then_inc(rounded, 1)

            def body(j, u):
                q = 2 * j + u
                if not (isinstance(q, int) and q == QUADS - 1):
                    grid(j + u, 1 - u)
                dve.wait_ge(made, q + 1)
                dve.tensor_tensor(g.xq(q), g.xq(q), bank[u][:, :], ALU.add).then_inc(added, 1)
            st.then(dve.memset(magic[:, :], MAGIC))
            grid(0, 0)
            over_pairs(dve, body)


class Tile:

    def __init__(self, j, k):
        self.j, self.k, self.u, self.t, self.par = j, k, k // QT, k % QT, k % 2
        self.n, self.q = 8 * j + k, 2 * j + k // QT

    def shift(self, by):
        dj, k = divmod(self.k + by, 2 * QT)
        return Tile(self.j + dj if dj else self.j, k)

    def outside(self):
        return isinstance(self.n, int) and not 0 <= self.n < TILES


def over_tiles(eng, body, steps=(), lead=0, lag=0):
    for n in range(-lead, 0):
        body(Tile(*divmod(n, 2 * QT)))

    def quad(j, u):
        for t in range(QT):
            body(Tile(j, QT * u + t))
    over_pairs(eng, quad, steps)
    for n in range(TILES, TILES + lag):
        body(Tile(*divmod(n, 2 * QT)))


class Mixer:

    def __init__(self, nc, stack):
        m = Memory(nc, stack, "mix")
        self.xc = m.sb("xc", (P, TILES, D))
        self.mv = m.sb("mv", (P, TILES, 2))


def attention1(nc, a, g):
    v = g.v
    scale = float(1 / np.sqrt(DH1).astype(np.float32))
    with ExitStack() as stack:
        m = Memory(nc, stack, "at1")
        ctx_in = [m.sem(f"ctx_in{u}") for u in range(2)]
        stats_ready, rstd_ready, h_ready, n_ready, hn_ready = (
            m.sem(n) for n in ("stats_ready", "rstd_ready", "h_ready", "n_ready", "hn_ready"))
        ring_ready, ring_evac = m.sem("ring_ready"), m.sem("ring_evac")
        s_ready, s_evac, top_ready, bias_ready = (m.sem(n) for n in ("s_ready", "s_evac", "top_ready", "bias_ready"))
        e_ready, d_ready, inv_ready, prob_ready = (m.sem(n) for n in ("e_ready", "d_ready", "inv_ready", "prob_ready"))
        am_ready, am_evac, u_ready, u_evac = (m.sem(n) for n in ("am_ready", "am_evac", "u_ready", "u_evac"))
        film_ready, fin_done = m.sem("film_ready"), m.sem("fin_done")
        u_out = [m.sem(f"u_out{u}") for u in range(2)]
        dve_st, pool_st = m.sem("dve_st"), m.sem("pool_st")

        hq = m.sb("hq", (P, 2, QT, P))
        hn = m.sb("hn", (P, 2, QT, P))
        ht = m.sb("ht", (P, 2, QN))
        ctxn = m.sb("ctxn", (P, 2, QT, C))
        ctxt = m.sb("ctxt", (C + 2, 2, QN))
        qm = m.sb("qm", (C + 2, 2, 2 * QT, H1 * SEQ))
        stats = m.sb("stats", (P, 2, QT, 6))
        mv = m.sb("mv", (P, 2, 2, QT, 2))
        so = m.sb("so", (P, 2, 4, SEQ))
        rest = m.sb("rest", (P, 2, 4, SEQ))
        df = m.sb("df", (P, 2, 4, SEQ))
        m8 = m.sb("m8", (P, 2, 4, 4, 8))
        bias = m.sb("bias", (P, 2, 4))
        minus_scale = m.sb("minus_scale", (P, 4))
        sm = m.sb("sm", (P, 2, 4))
        pr = m.sb("pr", (P, 2, 4, SEQ))
        amb = m.sb("amb", (P, 2, P))
        ut = m.sb("ut", (C + 1, 2, QN))
        xt = m.sb("xt", (P, 2, D))
        ring = [m.ps(f"ring{i}") for i in range(2)]
        sps = [m.ps(f"s{i}") for i in range(2)]
        amp = m.ps("am")
        up_ = m.ps("u")
        fip = [m.ps(f"f{i}") for i in range(2)]
        block = stack.enter_context(nc.Block())
        RING = 6
        pieces = ((), (0,), (1, 2, 3), (4, 5))
        POOL_CONSTS = 5
        ctx_src = a["ctx_768"].rearrange("b s c -> (b s) c").rearrange("(q t p) c -> q p t c", p=P, t=QT)
        mask_src = g.mask_rows.rearrange("m (q n) -> q m n", q=QUADS)

        @block.sync
        def _(sp):
            def load(j, u):
                q = 2 * j + u
                wait(sp, u_ready, 4 * (q - 1))
                sp.dma_start(ctxn[:, u, :, :], at_quad(ctx_src, q)).then_inc(ctx_in[u], 16)
                sp.dma_start(ctxt[C:C + 2, u, :], at_quad(mask_src, q)).then_inc(ctx_in[u], 16)
            over_pairs(sp, load)
            sp.wait_ge(u_out[0], 16 * QUADS // 2)
            sp.wait_ge(u_out[1], 16 * QUADS // 2)

        @block.tensor
        def _(pe):
            def front(x):
                if x.outside():
                    return
                for k in pieces[x.t]:
                    n = RING * x.q + k
                    slot = ring[k % 2]
                    if k == 0:
                        pe.wait_ge(ctx_in[x.u], 32 * (x.j + 1))
                    if k == 1:
                        pe.wait_ge(h_ready, x.q + 1)
                    wait(pe, ring_evac, n - 1 if k != 2 else n)
                    if k == 0:
                        for t in range(QT):
                            last = pe.transpose(slot[0:C, t * P:t * P + P], ctxn[:, x.u, t, :], g.ident[:, :])
                    elif k == 1:
                        for t in range(QT):
                            last = pe.transpose(slot[:, t * P:t * P + P], hq[:, x.u, t, :], g.ident[:, :])
                    else:
                        last = pe.matmul(slot[0:C, :], g.m1[:, k - 2, :], ht[:, x.u, :], start=True, stop=True)
                    last.then_inc(ring_ready, 1)

            def scores(x):
                if x.outside():
                    return
                wait(pe, ring_evac, RING * (x.q + 1))
                wait(pe, s_evac, x.n - 1)
                for b in range(2):
                    tok = slice(x.t * P + b * SEQ, x.t * P + b * SEQ + SEQ)
                    for p in range(2):
                        c0 = (2 * p + b) * SEQ
                        last = pe.matmul(sps[x.par][:, c0:c0 + SEQ], qm[:, x.u, 2 * x.t + b, p * P:p * P + P],
                                         ctxt[:, x.u, tok], start=True, stop=True)
                last.then_inc(s_ready, 1)

            def attend(x):
                if x.outside():
                    return
                pe.wait_ge(prob_ready, x.n + 1)
                wait(pe, am_evac, x.n)
                for p in range(2):
                    last = pe.matmul(amp[:, 0:SEQ], pr[:, x.par, 2 * p:2 * p + 2, :].rearrange("p a s -> p (a s)"),
                                     g.pairsum[:, :], start=(p == 0), stop=(p == 1))
                last.then_inc(am_ready, 1)
                pe.wait_ge(am_evac, x.n + 1)
                wait(pe, u_evac, x.n)
                pe.matmul(up_[0:C, 0:P], ctxn[:, x.u, x.t, :], amb[:, x.par, :], start=True, stop=True).then_inc(u_ready, 1)
                pe.wait_ge(u_evac, x.n + 1)
                wait(pe, fin_done, x.n - 1)
                pe.matmul(fip[x.par][:, 0:2 * D], ut[:, x.u, x.t * P:x.t * P + P], g.film[:, 0:2 * D],
                          start=True, stop=True).then_inc(film_ready, 1)

            def body(x):
                front(x.shift(QT))
                scores(x.shift(1))
                attend(x.shift(-1))
            pe.wait_ge(pool_st, POOL_CONSTS)
            over_tiles(pe, body, lead=QT, lag=1)

        @block.scalar
        def _(act):
            def front(x):
                if x.outside():
                    return
                for k in pieces[x.t]:
                    act.wait_ge(ring_ready, RING * x.q + k + 1)
                    slot = ring[k % 2]
                    if k == 0:
                        ins = act.copy(ctxt[0:C, x.u, :], slot[0:C, :])
                    elif k == 1:
                        ins = act.copy(ht[:, x.u, :], slot[:, :])
                    else:
                        ins = act.copy(qm[0:C, x.u, :, (k - 2) * SEQ:(k - 1) * SEQ],
                                       slot[0:C, :].rearrange("c (b s) -> c b s", s=SEQ))
                    ins.then_inc(ring_evac, 1)

            def take(x):
                if x.outside():
                    return
                act.wait_ge(s_ready, x.n + 1)
                wait(act, d_ready, x.n - 1)
                act.copy(so[:, x.par, :, :], sps[x.par][:, 0:4 * SEQ].rearrange("p (k s) -> p k s", s=SEQ)).then_inc(s_evac, 1)

            def exps(x):
                if x.outside():
                    return
                act.wait_ge(bias_ready, x.n + 1)
                act.wait_ge(top_ready, x.n + 1)
                for k in range(4):
                    act.activation(so[:, x.par, k, :], so[:, x.par, k, :], ACT.Exp, scale=scale,
                                   bias=bias[:, x.par, k:k + 1])
                    ins = act.activation(rest[:, x.par, k, :], rest[:, x.par, k, :], ACT.Exp, scale=scale,
                                         bias=bias[:, x.par, k:k + 1])
                ins.then_inc(e_ready, 1)

            def attend(x):
                if x.outside():
                    return
                act.wait_ge(am_ready, x.n + 1)
                act.copy(amb[0:SEQ, x.par, 0:SEQ], amp[0:SEQ, 0:SEQ])
                act.copy(amb[SEQ:P, x.par, SEQ:P], amp[SEQ:P, 0:SEQ]).then_inc(am_evac, 1)
                act.wait_ge(u_ready, x.n + 1)
                if x.t == 0:
                    wait(act, u_out[x.u], 16 * x.j)
                act.copy(ut[0:C, x.u, x.t * P:x.t * P + P], up_[0:C, 0:P]).then_inc(u_evac, 1)
                if x.t == QT - 1:
                    act.wait_ge(u_evac, x.n + 1)
                    act.dma_start(g.u_t[:, bass.ds(x.q * QN, QN)], ut[:, x.u, :]).then_inc(u_out[x.u], 16)

            def body(x):
                front(x.shift(QT))
                take(x.shift(1))
                exps(x)
                attend(x.shift(-1))
            over_tiles(act, body, lead=QT, lag=1)

        @block.gpsimd
        def _(pool):
            st = Steps(pool, pool_st)
            st.then(pool.memset(qm[C:C + 2, :, :, :], 1.0))
            st.then(pool.memset(qm[C:C + 1, :, :, :], 0.0))
            st.then(pool.memset(ut[C:C + 1, :, :], 1.0))
            st.then(pool.memset(amb[:, :, :], 0.0))
            st.then(pool.memset(minus_scale[:, :], -scale))
            assert st.n == POOL_CONSTS
            st_rstd, st_rstd2, st_prob = (Each(pool, m.sem(n), k) for n, k in (("st_rstd", 1), ("st_rstd2", 2), ("st_prob", 1)))

            def rstds(x):
                if x.outside() or x.t % 2:
                    return
                if x.t == 0:
                    rstd_steps(pool, g, mv[:, x.u, 0, :, :], stats_ready, rstd_ready, st_rstd.at(x.q), 2 * x.q)
                    return
                rstd_steps(pool, g, mv[:, x.u, 1, :, :], stats_ready, rstd_ready, st_rstd2.at(x.q), 2 * x.q + 1)
                pool.wait_ge(n_ready, x.q + 1)
                n = hn[:, x.u, :, :]
                st_rstd2.then(pool.tensor_tensor(n, n, g.wide[:, 0:1, :].to_broadcast([P, QT, D]), ALU.mult))
                pool.tensor_tensor(n, n, g.wide[:, 1:2, :].to_broadcast([P, QT, D]), ALU.add).then_inc(hn_ready, 1)

            def biases(x):
                if x.outside():
                    return
                pool.wait_ge(top_ready, x.n + 1)
                pool.tensor_tensor(bias[:, x.par, :], m8[:, x.par, :, 0, 0:1].rearrange("p a b -> p (a b)"),
                                   minus_scale[:, :], ALU.mult).then_inc(bias_ready, 1)

            def probs(x):
                if x.outside():
                    return
                pool.wait_ge(inv_ready, x.n + 1)
                s = sm[:, x.par, :].rearrange("p (a b) -> p a b", b=2)
                tm = g.tmask[:, bass.ds(2 * x.n, 2)].unsqueeze(1).to_broadcast([P, 2, 2])
                st_prob.at(x.n).then(pool.tensor_tensor(s, s, tm, ALU.mult))
                wait(pool, am_ready, x.n - 1)
                pool.tensor_tensor(pr[:, x.par, :, :], df[:, x.par, :, :],
                                   sm[:, x.par, :].unsqueeze(2).to_broadcast([P, 4, SEQ]), ALU.mult).then_inc(prob_ready, 1)

            def differences(x):
                if x.outside():
                    return
                pool.wait_ge(e_ready, x.n + 1)
                pool.tensor_tensor(df[:, x.par, :, :], so[:, x.par, :, :], rest[:, x.par, :, :],
                                   ALU.subtract).then_inc(d_ready, 1)

            def body(x):
                biases(x)
                probs(x.shift(-1))
                differences(x)
                rstds(x.shift(QT))
            over_tiles(pool, body, lead=QT, lag=1)

        @block.vector
        def _(dve):
            st_norm, st_norm2, st_top, st_sum, st_fin = (
                Each(dve, m.sem(n), k) for n, k in (("st_norm", 1), ("st_norm2", 1), ("st_top", 7), ("st_sum", 1), ("st_fin", 1)))

            def carry():
                dve.memset(g.carry[:, 0:1], 0.0)

            def norms(x):
                if x.outside() or x.t != 0:
                    return
                wait(dve, ring_ready, RING * (x.q - 2) + 2)
                tiles = [hq[:, x.u, t, :] for t in range(QT)]
                norm_steps(dve, g.carry, rstd_ready, st_norm.at(x.q), [g.xt(x.q, t) for t in range(QT)], stats[:, x.u, :, :],
                           mv[:, x.u, 0, :, :], tiles, stats_ready, 2 * x.q).then_inc(h_ready, 1)
                dve.tensor_copy(v.mv[:, bass.ds(QT * x.q, QT), :], mv[:, x.u, 0, :, :])

            def second_norms(x):
                if x.outside() or x.t != 2:
                    return
                tiles = [hq[:, x.u, t, :] for t in range(QT)]
                dve.wait_ge(h_ready, x.q + 1)
                wait(dve, fin_done, 4 * (x.q - 1))
                norm_steps(dve, g.carry, rstd_ready, st_norm2.at(x.q), tiles, stats[:, x.u, :, :], mv[:, x.u, 1, :, :],
                           [hn[:, x.u, t, :] for t in range(QT)], stats_ready, 2 * x.q + 1).then_inc(n_ready, 1)

            def top(x):
                if x.outside():
                    return
                wait(dve, d_ready, x.n - 1)
                dve.wait_ge(s_evac, x.n + 1)
                carry()
                link = st_top.at(x.n)
                for r in range(4):
                    src = so if r == 0 else rest
                    for k in range(4):
                        last = dve.max(m8[:, x.par, k, r, :], src[:, x.par, k, :])
                    link.then(last)
                    carry()
                    for k in range(4):
                        last = dve.match_replace(rest[:, x.par, k, :], m8[:, x.par, k, r, :], src[:, x.par, k, :], -3.0e38)
                    if r < 3:
                        link.then(last)
                        carry()
                last.then_inc(top_ready, 1)

            def sums(x):
                if x.outside():
                    return
                dve.wait_ge(d_ready, x.n + 1)
                st_sum.at(x.n).then(dve.tensor_reduce(sm[:, x.par, :], df[:, x.par, :, :], X, ALU.add))
                dve.reciprocal(sm[:, x.par, :], sm[:, x.par, :]).then_inc(inv_ready, 1)

            def finish(x):
                if x.outside():
                    return
                dve.wait_ge(hn_ready, x.q + 1)
                dve.wait_ge(film_ready, x.n + 1)
                st_fin.at(x.n).then(dve.tensor_tensor(xt[:, x.par, :], fip[x.par][:, 0:D], hn[:, x.u, x.t, :], ALU.mult))
                dve.tensor_tensor(v.xc[:, bass.ds(x.n, 1), :].rearrange("p a d -> p (a d)"), fip[x.par][:, D:2 * D],
                                  xt[:, x.par, :], ALU.add).then_inc(fin_done, 1)

            def body(x):
                top(x)
                sums(x.shift(-1))
                finish(x.shift(-2))
                norms(x.shift(QT))
                second_norms(x.shift(QT))
            over_tiles(dve, body, lead=QT, lag=2)


def at_quad(src, q):
    if isinstance(q, int):
        return src[q]
    s = src[bass.ds(q, 1)]
    return s.rearrange("a p t c -> (a p) t c") if len(s.shape) == 4 else s.rearrange("a m n -> (a m) n")


def filter_tokens(nc, a, g):
    v = g.v
    GR = 8
    with ExitStack() as stack:
        m = Memory(nc, stack, "fil")
        t_in = [m.sem(f"t_in{u}") for u in range(2)]
        made, moved, zeroed = m.sem("made"), m.sem("moved"), m.sem("zeroed")
        tb = m.sb("tb", (P, 2, GR, P))
        bank = [m.ps(f"y{i}") for i in range(2)]
        block = stack.enter_context(nc.Block())
        groups = D // GR

        @block.gpsimd
        def _(pool):
            pool.memset(tb[:, :, :, :], 0.0).then_inc(zeroed, 1)

        @block.sync
        def _(sp):
            sp.wait_ge(g.taps_stored, 16)
            sp.wait_ge(zeroed, 1)

            def load(j, u):
                i = 2 * j + u
                wait(sp, made, i - 1)
                for b in range(2):
                    sp.dma_start(tb[b * SEQ:b * SEQ + SEQ, u, :, b * SEQ:b * SEQ + SEQ],
                                 g.toeplitz[:, bass.ds(i * GR, GR), :]).then_inc(t_in[u], 16)
            over_pairs(sp, load, pairs=groups // 2)

        @block.tensor
        def _(pe):
            def body(j, u):
                i = 2 * j + u
                pe.wait_ge(t_in[u], 32 * (j + 1))
                wait(pe, moved, i - 1)
                for k in range(GR):
                    last = pe.matmul(bank[u][:, k * TILES:k * TILES + TILES], tb[:, u, k, :],
                                     v.xc[:, :, bass.ds(i * GR + k, 1)].rearrange("p t a -> p (t a)"),
                                     start=True, stop=True)
                last.then_inc(made, 1)
            over_pairs(pe, body, pairs=groups // 2)

        @block.scalar
        def _(act):
            def body(j, u):
                i = 2 * j + u
                act.wait_ge(made, i + 1)
                act.copy(v.xc[:, :, bass.ds(i * GR, GR)].rearrange("p t c -> p c t"),
                         bank[u][:, :].rearrange("p (c t) -> p c t", t=TILES)).then_inc(moved, 1)
            over_pairs(act, body, pairs=groups // 2)


def mix(nc, a, g):
    v = g.v
    with ExitStack() as stack:
        m = Memory(nc, stack, "mx")
        u_in = [m.sem(f"u_in{u}") for u in range(2)]
        out_done = m.sem("out_done")
        film_ready, film_used, stats_ready, rstd_ready, n_ready, turned, turn_evac = (
            m.sem(n) for n in ("film_ready", "film_used", "stats_ready", "rstd_ready", "n_ready", "turned", "turn_evac"))
        hid_ready, hid_done, back_ready, back_used, resid_ready, last_ready, x_ready = (
            m.sem(n) for n in ("hid_ready", "hid_done", "back_ready", "back_used", "resid_ready", "last_ready", "x_ready"))
        ut = m.sb("ut", (C + 1, 2, QN))
        mvs = m.sb("mvs", (P, 2, QT, 2))
        hq = m.sb("hq", (P, QT, D))
        yq = m.sb("yq", (P, QT, D))
        xq = m.sb("xq", (P, 2, QT, D))
        xb = m.sb("xb", (P, 2, QT, D))
        nq = m.sb("nq", (P, 2, QT, D))
        lq = m.sb("lq", (P, 2, QT, D))
        nt = m.sb("nt", (P, 2, QN))
        hid = m.sb("hid", (P, 2, 4, QN))
        stats = m.sb("stats", (P, 2, QT, 6))
        stats2 = m.sb("stats2", (P, 2, QT, 6))
        mv = m.sb("mv", (P, 2, QT, 2))
        mv2 = m.sb("mv2", (P, 2, QT, 2))
        fop = m.ps("fo", (P, 2, 512))
        tp = m.ps("t")
        hp = [m.ps(f"h{i}") for i in range(4)]
        bp = m.ps("b")
        block = stack.enter_context(nc.Block())
        out = g.out.rearrange("b s d -> (b s) d").rearrange("(q t p) d -> q p t d", p=P, t=QT)

        def last_quad(q):
            return isinstance(q, int) and q == QUADS - 1

        def norm_count(q):
            return 0 if isinstance(q, int) and q == 0 else 2 * q - 1

        def last_count(q):
            return 2 * q + 1 if last_quad(q) else 2 * q + 2

        @block.sync
        def _(sp):
            def load(j, u):
                q = 2 * j + u
                wait(sp, film_ready, q - 1)
                sp.dma_start(ut[:, u, :], g.u_t[:, bass.ds(q * QN, QN)]).then_inc(u_in[u], 16)
                if not (isinstance(q, int) and q < 2):
                    store(q - 2)

            def store(q):
                sp.wait_ge(x_ready, q + 1)
                sp.dma_start(at_quad(out, q), g.xq(q).rearrange("p (t d) -> p t d", d=D)).then_inc(out_done, 16)
            over_pairs(sp, load)
            for q in range(QUADS - 2, QUADS):
                store(q)
            sp.wait_ge(out_done, 16 * QUADS)

        @block.tensor
        def _(pe):
            def film(j, u):
                q = 2 * j + u
                pe.wait_ge(u_in[u], 16 * (j + 1))
                wait(pe, film_used, q)
                for t in range(QT):
                    last = pe.matmul(fop[:, t // 2, 256 * (t % 2):256 * (t % 2) + 256], ut[:, u, t * P:t * P + P],
                                     g.film[:, 2 * D:], start=True, stop=True)
                last.then_inc(film_ready, 1)

            def back(q, u):
                wait(pe, back_used, q)
                pe.wait_ge(hid_done, 4 * (q + 1))
                for t in range(QT):
                    for c in range(4):
                        last = pe.matmul(bp[:, t * P:t * P + P], hid[:, u, c, t * P:t * P + P], g.w2[:, c, :],
                                         start=(c == 0), stop=(c == 3))
                last.then_inc(back_ready, 1)

            def body(j, u):
                q = 2 * j + u
                if not last_quad(q):
                    film(j + u, 1 - u)
                if not (isinstance(q, int) and q == 0):
                    back(q - 1, 1 - u)
                pe.wait_ge(n_ready, q + 1)
                wait(pe, turn_evac, q)
                for t in range(QT):
                    last = pe.transpose(tp[:, t * P:t * P + P], nq[:, u, t, :], g.ident[:, :])
                last.then_inc(turned, 1)
                pe.wait_ge(turn_evac, q + 1)
                for c in range(4):
                    wait(pe, hid_done, 4 * (q - 1) + c + 1)
                    pe.matmul(hp[c][:, :], g.w1[:, c * P:c * P + P], nt[:, u, :], start=True, stop=True).then_inc(hid_ready, 1)
            film(0, 0)
            over_pairs(pe, body)
            back(QUADS - 1, 1)

        @block.scalar
        def _(act):
            def body(j, u):
                q = 2 * j + u
                act.wait_ge(turned, q + 1)
                act.activation(nt[:, u, :], tp[:, :], ACT.Identity, scale=g.ffn_g[:, 0:1],
                               bias=g.ffn_b[:, 0:1]).then_inc(turn_evac, 1)
                wait(act, back_ready, q - 1)
                for c in range(4):
                    act.wait_ge(hid_ready, 4 * q + c + 1)
                    act.activation(hid[:, u, c, :], hp[c][:, :], ACT.Gelu, bias=g.b1[:, c:c + 1]).then_inc(hid_done, 1)
            over_pairs(act, body)

        @block.gpsimd
        def _(pool):
            st_first, st_last = Each(pool, m.sem("pool_first"), 1), Each(pool, m.sem("pool_last"), 3)

            def finish(j, u):
                q = 2 * j + u
                st = st_last.at(q)
                rstd_steps(pool, g, mv2[:, u, :, :], stats_ready, rstd_ready, st, last_count(q))
                pool.wait_ge(last_ready, q + 1)
                n = lq[:, u, :, :]
                st.then(pool.tensor_tensor(n, n, g.wide[:, 3:4, :].to_broadcast([P, QT, D]), ALU.mult))
                xs = g.xq(q).rearrange("p (t d) -> p t d", d=D)
                st.then(pool.tensor_tensor(n, n, g.wide[:, 4:5, :].to_broadcast([P, QT, D]), ALU.add))
                pool.tensor_tensor(xs, xs, n, ALU.add).then_inc(x_ready, 1)

            def body(j, u):
                q = 2 * j + u
                rstd_steps(pool, g, mv[:, u, :, :], stats_ready, rstd_ready, st_first.at(q), norm_count(q))
                pool.tensor_tensor(xb[:, u, :, :], xq[:, u, :, :], g.wide[:, 2:3, :].to_broadcast([P, QT, D]),
                                   ALU.add).then_inc(resid_ready, 1)
                if not (isinstance(q, int) and q == 0):
                    finish(j + u - 1, 1 - u)
            over_pairs(pool, body)
            finish(QUADS // 2 - 1, 1)


        @block.vector
        def _(dve):
            st_first, st_last = Each(dve, m.sem("dve_first"), 4), Each(dve, m.sem("dve_last"), 1)

            def first(j, u):
                q = 2 * j + u
                st = st_first.at(q)
                st.then(dve.tensor_copy(mvs[:, u, :, :], v.mv[:, bass.ds(QT * q, QT), :]))
                for t in range(QT):
                    dve.tensor_scalar(hq[:, t, :], g.xt(q, t), mvs[:, u, t, 0:1], mvs[:, u, t, 1:2],
                                      ALU.subtract, ALU.mult)
                dve.wait_ge(film_ready, q + 1)
                fo = fop[:, :, :].rearrange("p a (b n) -> p (a b) n", n=2 * D)
                y = v.xc[:, bass.ds(QT * q, QT), :]
                st.then(dve.tensor_tensor(yq[:, :, :], fo[:, :, 0:D], y, ALU.mult))
                ins = dve.tensor_tensor(yq[:, :, :], fo[:, :, D:2 * D], yq[:, :, :], ALU.add)
                ins.then_inc(film_used, 1)
                dve.wait_ge(film_used, q + 1)
                wait(dve, resid_ready, q - 1)
                st.then(dve.tensor_tensor(xq[:, u, :, :], yq[:, :, :], hq[:, :, :], ALU.add))
                wait(dve, turned, q - 1)
                norm_steps(dve, g.carry, rstd_ready, st, [xq[:, u, t, :] for t in range(QT)], stats[:, u, :, :],
                           mv[:, u, :, :], [nq[:, u, t, :] for t in range(QT)], stats_ready,
                           norm_count(q)).then_inc(n_ready, 1)

            def second(j, u):
                q = 2 * j + u
                st = st_last.at(q)
                dve.wait_ge(back_ready, q + 1)
                dve.wait_ge(resid_ready, q + 1)
                b = xb[:, u, :, :]
                dve.tensor_tensor(b, bp[:, :].rearrange("p (t d) -> p t d", d=D), b, ALU.add).then_inc(back_used, 1)
                dve.wait_ge(back_used, q + 1)
                wait(dve, x_ready, q - 1)
                norm_steps(dve, g.carry, rstd_ready, st, [xb[:, u, t, :] for t in range(QT)], stats2[:, u, :, :],
                           mv2[:, u, :, :], [lq[:, u, t, :] for t in range(QT)], stats_ready,
                           last_count(q)).then_inc(last_ready, 1)

            def body(j, u):
                q = 2 * j + u
                first(j, u)
                if not (isinstance(q, int) and q == 0):
                    second(j + u - 1, 1 - u)
            over_pairs(dve, body)
            second(QUADS // 2 - 1, 1)


def experts(nc, a, g):
    n_tok = a["L1_ffn_router_indices"].shape[0]
    NT = n_tok // P
    with ExitStack() as stack:
        m = Memory(nc, stack, "ex")
        loaded, stats_ready, rstd_ready, xn_ready, dve_st, pool_st, act_st, pe_st, out_done = (
            m.sem(n) for n in ("loaded", "stats_ready", "rstd_ready", "xn_ready", "dve_st", "pool_st", "act_st", "pe_st", "out_done"))
        gu_ready, limited, sig_ready, inter_ready, down_ready, summed = (
            m.sem(n) for n in ("gu_ready", "limited", "sig_ready", "inter_ready", "down_ready", "summed"))
        wgu = m.sb("wgu", (P, EXPERTS, 2 * D))
        wd = m.sb("wd", (P, EXPERTS, D))
        bgu = m.sb("bgu", (P, EXPERTS, 2))
        bd = m.sb("bd", (EXPERTS, D))
        route = m.sb("route", (P, NT, 2), I32)
        routef = m.sb("routef", (P, NT, 2))
        weight = m.sb("weight", (P, NT, EXPERTS))
        iota = m.sb("iota", (P, EXPERTS))
        hit = m.sb("hit", (P, NT, 2, EXPERTS))
        coef = m.sb("coef", (P, NT, EXPERTS))
        coeft = m.sb("coeft", (EXPERTS, NT, P))
        xn = m.sb("xn", (P, NT, D))
        xnt = m.sb("xnt", (P, NT * P))
        stats = m.sb("stats", (P, NT, 6))
        mv = m.sb("mv", (P, NT, 2))
        gu = m.sb("gu", (P, 2, 2, NT * P))
        sg = m.sb("sg", (P, 2, NT * P))
        inter = m.sb("inter", (P, 2, NT * P))
        tp, cp = m.ps("t"), m.ps("c")
        gp = [m.ps(f"g{i}") for i in range(2)]
        dp = [m.ps(f"d{i}") for i in range(2)]
        bp = m.ps("b")
        block = stack.enter_context(nc.Block())
        LOADS = 6
        COEF_AT = 4

        @block.sync
        def _(sp):
            with nc.allow_non_contiguous_dma(reason="small biases, turned"):
                for dst, src in (
                    (wgu[:, :, :], a["L1_ffn_gate_up_proj"].rearrange("e h n -> h e n")),
                    (wd[:, :, :], a["L1_ffn_down_proj"].rearrange("e h n -> h e n")),
                    (bgu[:, :, :], a["L1_ffn_gate_up_proj_bias"].rearrange("e (i k) -> i e k", k=2)),
                    (bd[:, :], a["L1_ffn_down_proj_bias"]),
                    (route[:, :, :], a["L1_ffn_router_indices"].rearrange("(t p) k -> p t k", p=P)),
                    (weight[:, :, :], a["L1_ffn_routing_weights"].rearrange("(t p) e -> p t e", p=P)),
                ):
                    sp.dma_start(dst, src).then_inc(loaded, 16)
            sp.wait_ge(summed, NT * EXPERTS + NT)
            sp.dma_start(g.out.rearrange("b s d -> (b s) d").rearrange("(t p) d -> p t d", p=P)[:, 0:NT, :],
                         g.x[:, 0:NT, :]).then_inc(out_done, 16)
            sp.wait_ge(out_done, 16)

        @block.gpsimd
        def _(pool):
            st = Steps(pool, pool_st)
            for e in range(EXPERTS):
                st.then(pool.memset(iota[:, e:e + 1], float(e)))
            pool.wait_ge(stats_ready, 1)
            st.then(pool.tensor_tensor(mv[:, :, 1:2], mv[:, :, 1:2], g.eps[:, 0:NT].unsqueeze(2), ALU.add))
            pool.tensor_tensor(mv[:, :, 1:2], mv[:, :, 1:2], g.minus_half[:, 0:NT].unsqueeze(2), ALU.pow).then_inc(rstd_ready, 1)

        @block.tensor
        def _(pe):
            pe.wait_ge(xn_ready, NT)
            for t in range(NT):
                last = pe.transpose(tp[:, t * P:t * P + P], xn[:, t, :], g.ident[:, :])
            last.then_inc(pe_st, 1)
            pe.wait_ge(dve_st, COEF_AT)
            for t in range(NT):
                last = pe.transpose(cp[0:EXPERTS, t * P:t * P + P], coef[:, t, :], g.ident[:, :])
            last.then_inc(pe_st, 1)
            pe.wait_ge(loaded, 16 * LOADS)

            def into(e):
                wait(pe, limited, 2 * (e - 1))
                w = wgu[:, e, :].rearrange("p (i k) -> p i k", k=2)
                for k in range(2):
                    last = pe.matmul(gp[e % 2][:, k * NT * P:(k + 1) * NT * P], w[:, :, k], xnt[:, :], start=True, stop=True)
                last.then_inc(gu_ready, 1)

            def outof(e):
                pe.wait_ge(inter_ready, e + 1)
                wait(pe, summed, NT * (e - 1) + NT)
                for t in range(NT):
                    last = pe.matmul(dp[e % 2][:, t * P:t * P + P], inter[:, e % 2, t * P:t * P + P], wd[:, e, :],
                                     start=True, stop=True)
                last.then_inc(down_ready, 1)
            pe.wait_ge(act_st, 2)
            for t in range(NT):
                last = pe.matmul(bp[:, t * P:t * P + P], coeft[:, t, :], bd[:, :], start=True, stop=True)
            last.then_inc(pe_st, 1)
            into(0)
            for e in range(EXPERTS):
                if e + 1 < EXPERTS:
                    into(e + 1)
                outof(e)

        @block.scalar
        def _(act):
            st = Steps(act, act_st)
            act.wait_ge(pe_st, 1)
            st.then(act.copy(xnt[:, :], tp[:, 0:NT * P]))
            act.wait_ge(pe_st, 2)
            st.then(act.copy(coeft[:, :, :], cp[0:EXPERTS, 0:NT * P].rearrange("p (t n) -> p t n", n=P)))
            for e in range(EXPERTS):
                act.wait_ge(limited, 2 * e + 1)
                wait(act, inter_ready, e - 1)
                act.activation(sg[:, e % 2, :], gu[:, e % 2, 0, :], ACT.Sigmoid, scale=1.702).then_inc(sig_ready, 1)

        @block.vector
        def _(dve):
            st = Steps(dve, dve_st)
            dve.wait_ge(loaded, 16 * LOADS)
            dve.wait_ge(pool_st, EXPERTS)
            st.then(dve.tensor_copy(routef[:, :, :], route[:, :, :]))
            for t in range(NT):
                for k in range(2):
                    last = dve.tensor_scalar(hit[:, t, k, :], iota[:, :], routef[:, t, k:k + 1], None, ALU.is_equal)
            st.then(last)
            st.then(dve.tensor_tensor(hit[:, :, 0, :], hit[:, :, 0, :], hit[:, :, 1, :], ALU.add))
            st.then(dve.tensor_tensor(coef[:, :, :], hit[:, :, 0, :], weight[:, :, :], ALU.mult))
            for t in range(NT):
                last = dve.bn_stats(stats[:, t, :], g.x[:, t, :])
            st.then(last)
            assert st.n == COEF_AT + 1
            for t in range(NT):
                last = dve.bn_aggr(mv[:, t, :], stats[:, t, :])
            last.then_inc(stats_ready, 1)
            dve.wait_ge(rstd_ready, 1)
            for t in range(NT):
                dve.tensor_scalar(xn[:, t, :], g.x[:, t, :], mv[:, t, 0:1], mv[:, t, 1:2],
                                  ALU.subtract, ALU.mult).then_inc(xn_ready, 1)
            dve.wait_ge(pe_st, 3)
            dve.wait_ge(xn_ready, NT)
            for t in range(NT):
                dve.tensor_tensor(g.x[:, t, :], g.x[:, t, :], bp[:, t * P:t * P + P], ALU.add).then_inc(summed, 1)

            def limit(e):
                dve.wait_ge(gu_ready, e + 1)
                gv, uv = gu[:, e % 2, 0, :], gu[:, e % 2, 1, :]
                dve.tensor_scalar(gv, gp[e % 2][:, 0:NT * P], bgu[:, e, 0:1], 7.0, ALU.add, ALU.min).then_inc(limited, 1)
                dve.tensor_scalar(uv, gp[e % 2][:, NT * P:], bgu[:, e, 1:2], 7.0, ALU.add, ALU.min).then_inc(limited, 1)
                dve.wait_ge(limited, 2 * e + 2)
                st.then(dve.tensor_scalar(uv, uv, -7.0, 1.0, ALU.max, ALU.add))
                st.then(dve.tensor_tensor(uv, uv, gv, ALU.mult))
                dve.wait_ge(sig_ready, e + 1)
                wait(dve, down_ready, e - 1)
                dve.tensor_tensor(inter[:, e % 2, :], uv, sg[:, e % 2, :], ALU.mult).then_inc(inter_ready, 1)

            def join(e):
                dve.wait_ge(down_ready, e + 1)
                dve.wait_ge(summed, NT * (e + 1))
                for t in range(NT):
                    dve.scalar_tensor_tensor(out=g.x[:, t, :], in0=dp[e % 2][:, t * P:t * P + P],
                                             scalar=coef[:, t, e:e + 1], in1=g.x[:, t, :],
                                             op0=ALU.mult, op1=ALU.add).then_inc(summed, 1)
            for e in range(EXPERTS):
                limit(e)
                if e > 0:
                    join(e - 1)
            join(EXPERTS - 1)


class Resident:

    def __init__(self, nc, stack):
        m = Memory(nc, stack, "g")
        self.x = m.sb("x", (P, TILES, P))
        self.ident = m.sb("ident", (P, P))
        self.pairsum = m.sb("pairsum", (P, SEQ))
        self.minus_half = m.sb("minus_half", (P, 8))
        self.carry = m.sb("carry", (P, 1))
        self.eps = m.sb("eps", (P, 8))
        self.m0 = m.sb("m0", (P, H0, C))
        self.n0 = m.sb("n0", (C + 1, H0, D))
        self.m1 = m.sb("m1", (P, H1, C))
        self.film = m.sb("film", (C + 1, 4 * D))
        self.gate_t = m.sb("gate_t", (P, INTER))
        self.up_t = m.sb("up_t", (P, INTER))
        self.down_t = m.sb("down_t", (P, IC, D))
        self.w1 = m.sb("w1", (P, HID))
        self.w2 = m.sb("w2", (P, 4, D))
        self.b1 = m.sb("b1", (P, 4))
        self.ffn_g = m.sb("ffn_g", (P, 1))
        self.ffn_b = m.sb("ffn_b", (P, 1))
        self.wide = m.sb("wide", (P, 5, D))
        self.tmask = m.sb("tmask", (P, BATCH))
        self.mask_rows = nc.dram_tensor("mask_rows", [2, TOK], F32, kind="Internal").ap()
        self.taps_sb = m.sb("taps_sb", (P, 2 * SEQ))
        self.taps_stored = m.sem("taps_stored")
        SKEW = SEQ * (2 * SEQ + 1)
        skewed = nc.dram_tensor("skewed_taps", [D, SKEW], F32, kind="Internal").ap()
        self.taps_out = skewed.rearrange("d (j m) -> d j m", j=SEQ)[:, :, 0:2 * SEQ]
        self.toeplitz = bass.AP(skewed.tensor, SEQ, [[2 * SEQ, SEQ], [SKEW, D], [1, SEQ]])
        self.u_t = nc.dram_tensor("u_t", [C + 1, TOK], F32, kind="Internal").ap()

    def xt(self, q, t):
        flat = self.x[:, :, :].rearrange("p t d -> p (t d)")
        return flat[:, bass.ds(q * QN + t * P, P)] if not isinstance(q, int) else flat[:, q * QN + t * P:q * QN + t * P + P]

    def xq(self, q):
        flat = self.x[:, :, :].rearrange("p t d -> p (t d)")
        return flat[:, bass.ds(q * QN, QN)] if not isinstance(q, int) else flat[:, q * QN:q * QN + QN]


FFN = [act_quant, gate_up_max, gate, up, down]
ATTENTION1 = [attention1, filter_tokens, mix]


def program(nc, a, out, stages=None):
    with ExitStack() as stack:
        g = Resident(nc, stack)
        g.out = out

        def run(some):
            for stage in some:
                if stages is None or stage in stages:
                    stage(nc, a, g)
        run([prepare, attention0])
        with ExitStack() as ffn:
            g.f = Quantised(nc, ffn)
            run(FFN)
        with ExitStack() as second:
            g.v = Mixer(nc, second)
            run(ATTENTION1)
        run([experts])
        if stages and mix not in stages and experts not in stages:
            dump(nc, a, g, out)


def dump(nc, a, g, out):
    with ExitStack() as stack:
        m = Memory(nc, stack, "dump")
        done = m.sem("done")
        block = stack.enter_context(nc.Block())

        @block.sync
        def _(sp):
            sp.dma_start(out.rearrange("b s d -> (b s) d").rearrange("(t p) d -> p t d", p=P), g.x[:, :, :]).then_inc(done, 16)
            sp.wait_ge(done, 16)


_NAMES = [
    "x", "ctx_768", "mask_BxS2_bk0", "mask_BxS_bf1", "mask_BxS2_bf1",
    "L0_xattn_W_q", "L0_xattn_W_k", "L0_xattn_W_v", "L0_xattn_W_o", "L0_xattn_b_o",
    "L0_ffn_w_gate", "L0_ffn_w_up", "L0_ffn_w_down",
    "L1_xattn_Wq", "L1_xattn_Wk", "L1_xattn_Wv", "L1_xattn_W_film_in", "L1_xattn_b_film_in",
    "L1_xattn_W_film_out", "L1_xattn_b_film_out", "L1_xattn_g_norm_in", "L1_xattn_b_norm_in",
    "L1_xattn_g_norm_out", "L1_xattn_b_norm_out", "L1_xattn_g_ffn", "L1_xattn_b_ffn",
    "L1_xattn_W1", "L1_xattn_b1", "L1_xattn_W2", "L1_xattn_b2", "L1_xattn_log_dt",
    "L1_xattn_A_re", "L1_xattn_A_im", "L1_xattn_C_re", "L1_xattn_C_im", "L1_xattn_D_skip",
    "L1_xattn_mod_gate", "L1_ffn_router_indices", "L1_ffn_routing_weights",
    "L1_ffn_gate_up_proj", "L1_ffn_gate_up_proj_bias", "L1_ffn_down_proj", "L1_ffn_down_proj_bias",
]


def kernel(**inputs):
    import concourse.bacc as bacc
    from concourse.bass_utils import run_bass_kernel_spmd

    nc = bacc.Bacc("TRN2", target_bir_lowering=False, num_devices=1)
    arrays, args = {}, {}
    for name in _NAMES:
        v = np.ascontiguousarray(inputs[name])
        if v.ndim == 0:
            v = v.reshape(1)
        arrays[f"in_{name}"] = v
        args[name] = nc.dram_tensor(f"in_{name}", v.shape, mybir.dt.from_np(v.dtype), kind="ExternalInput").ap()
    out = nc.dram_tensor("out", (BATCH, SEQ, D), F32, kind="ExternalOutput").ap()
    program(nc, args, out)
    return run_bass_kernel_spmd(nc, [arrays], core_ids=[0]).results[0]["out"]
```

```python
from contextlib import ExitStack

import numpy as np

import concourse.bass as bass
from concourse import mybir

F32 = mybir.dt.float32
I32 = mybir.dt.int32
U8 = mybir.dt.uint8
ALU = mybir.AluOpType
ACT = mybir.ActivationFunctionType
X = mybir.AxisListType.X
XY = mybir.AxisListType.XY
RMAX = bass.bass_isa.ReduceOp.max

P = 128
SEQ = 64
BATCH = 128
D = 128
C = 96
TOK = BATCH * SEQ
TILES = TOK // P
QT = 4
QUADS = TILES // QT
QN = QT * P
H0, H1 = 8, 4
DH0, DH1 = 64, 32
INTER = 384
IC = INTER // P
HID = 512
NS = 64
EXPERTS = 8
EPS = 1e-5
MAGIC = 12582912.0
FAR = 2.0 ** 100
QMAX = 32767.0
TWO_PI = 2 * np.pi


class Steps:

    def __init__(self, eng, sem):
        self.eng, self.sem, self.base, self.n = eng, sem, 0, 0

    def done(self, ins):
        ins.then_inc(self.sem, 1)
        self.n += 1

    def now(self):
        return self.base + self.n

    def then(self, ins):
        self.done(ins)
        self.eng.wait_ge(self.sem, self.now())


class Each(Steps):

    def __init__(self, eng, sem, per):
        super().__init__(eng, sem)
        self.per = per

    def at(self, i):
        self.base, self.n = i * self.per, 0
        return self


def wait(eng, sem, value):
    if isinstance(value, int) and value <= 0:
        return
    eng.wait_ge(sem, value)


def over_pairs(eng, body, steps=(), pairs=QUADS // 2):
    before = [s.n for s in steps]
    for u in range(2):
        body(0, u)
    per = [s.n - b for s, b in zip(steps, before)]
    start = [s.n for s in steps]
    with eng.Fori(1, pairs - 1) as j:
        for s, b, k in zip(steps, start, per):
            s.base, s.n = (j - 1) * k + b, 0
        for u in range(2):
            body(j, u)
    for s, b, k in zip(steps, start, per):
        s.base, s.n = 0, b + (pairs - 2) * k
    for u in range(2):
        body(pairs - 1, u)


class Memory:

    def __init__(self, nc, stack, tag):
        self.nc, self.stack, self.tag = nc, stack, tag

    def sb(self, name, shape, dt=F32):
        return self.stack.enter_context(self.nc.sbuf_tensor(f"{self.tag}_{name}", list(shape), dt))

    def ps(self, name, shape=(P, 512)):
        return self.stack.enter_context(self.nc.psum_tensor(f"{self.tag}_{name}", list(shape), F32))

    def sem(self, name):
        return self.stack.enter_context(self.nc.semaphore(f"{self.tag}_{name}"))


def row(ap1d):
    return ap1d.rearrange("(a n) -> a n", a=1)


def col(ap1d):
    return ap1d.rearrange("(n a) -> n a", a=1)


def exp_steps(dve, st, x, out, tmp, k, pw, poly):
    ln2_hi = 0.693359375
    ln2_lo = -2.12194440054690583e-4
    st.then(dve.tensor_scalar(k, x, 1.4426950408889634, MAGIC, ALU.mult, ALU.add))
    st.then(dve.tensor_scalar(k, k, MAGIC, -126.0, ALU.subtract, ALU.max))
    st.then(dve.tensor_scalar(k, k, 127.0, None, ALU.min))
    st.then(dve.scalar_tensor_tensor(out=tmp, in0=k, scalar=-ln2_hi, in1=x, op0=ALU.mult, op1=ALU.add))
    st.then(dve.scalar_tensor_tensor(out=tmp, in0=k, scalar=-ln2_lo, in1=tmp, op0=ALU.mult, op1=ALU.add))
    st.then(dve.tensor_scalar(poly, tmp, 1.0 / 5040, None, ALU.mult))
    for c in (1.0 / 720, 1.0 / 120, 1.0 / 24, 1.0 / 6, 0.5, 1.0):
        st.then(dve.scalar_tensor_tensor(out=poly, in0=poly, scalar=c, in1=tmp, op0=ALU.add, op1=ALU.mult))
    st.then(dve.tensor_scalar(pw, k, 127.0, 8388608.0, ALU.add, ALU.mult))
    st.then(dve.scalar_tensor_tensor(out=out, in0=poly, scalar=1.0, in1=pw.bitcast(F32),
                                     op0=ALU.add, op1=ALU.mult))


def prepare(nc, a, g):
    with ExitStack() as stack:
        m = Memory(nc, stack, "pre")
        loaded, late, built, pe_ready, act_st, dve_st, pool_st, stored = (
            m.sem(n) for n in ("loaded", "late", "built", "pe", "act", "dve", "pool", "stored"))
        wq = m.sb("wq", (P, H0 * DH0))
        wk = m.sb("wk", (C, H0 * DH0))
        wv = m.sb("wv", (C, H0 * DH0))
        wo = m.sb("wo", (P, 4, D))
        wq1 = m.sb("wq1", (P, P))
        wk1 = m.sb("wk1", (C, P))
        wv1 = m.sb("wv1", (C, P))
        film = m.sb("film", (P, 4 * D))
        bfilm = m.sb("bfilm", (C + 1, 4 * D))
        qraw = m.sb("qraw", (P, 3, INTER))
        gate_raw = qraw[:, 0, :].rearrange("p (c n) -> p c n", c=IC)
        up_raw = qraw[:, 1, :].rearrange("p (c n) -> p c n", c=IC)
        down_raw = qraw[:, 2, :].rearrange("p (c n) -> p c n", c=IC)
        blocks = qraw[:, :, :].rearrange("p w (b n) -> p (w b) n", n=32)
        bamax = m.sb("bamax", (P, 36))
        binv = m.sb("binv", (P, 36))
        masks = m.sb("masks", (P, 3, SEQ), U8)
        mrows = m.sb("mrows", (P, 2, SEQ))
        tmb = m.sb("tmb", (P, 2, SEQ))
        gate_s = m.sb("gate_s", (P, 1))
        one_col = m.sb("one_col", (P, 1))
        turned = m.sb("turned", (P, 16, P))
        pt = [m.ps(f"t{i}") for i in range(8)]

        logdt = m.sb("logdt", (P, 1))
        are, aim, cre, cim = (m.sb(n, (P, NS)) for n in ("are", "aim", "cre", "cim"))
        dskip = m.sb("dskip", (P, 1))
        dt = m.sb("dt", (P, 1))
        t1k, t1t, t1p = (m.sb(n, (P, 1)) for n in ("t1k", "t1t", "t1p"))
        t1i = m.sb("t1i", (P, 1), I32)
        a1, b1, ea, wr, wi, dr, di, z1, z2, z3, inv = (
            m.sb(n, (P, NS)) for n in ("a1", "b1", "ea", "wr", "wi", "dr", "di", "z1", "z2", "z3", "inv"))
        zi = m.sb("zi", (P, NS), I32)
        phase = m.sb("phase", (P, 16, NS))
        turns = m.sb("turns", (P, 16, NS))
        decay = m.sb("decay", (P, 16, NS))
        sine = m.sb("sine", (P, 16, NS))
        half = m.sb("half", (P, 16, NS))
        cosine = m.sb("cosine", (P, 16, NS))
        ur, ui = m.sb("ur", (P, 8, NS)), m.sb("ui", (P, 8, NS))
        prod, prod2 = m.sb("prod", (P, 8, NS)), m.sb("prod2", (P, 8, NS))
        taps = g.taps_sb[:, :]

        block = stack.enter_context(nc.Block())

        @block.sync
        def _(sp):
            n = 0
            for dst, src in (
                (wq[:, :], a["L0_xattn_W_q"]), (wk[:, :], a["L0_xattn_W_k"]), (wv[:, :], a["L0_xattn_W_v"]),
                (wo[:, :, :], a["L0_xattn_W_o"].rearrange("(c p) n -> p c n", p=P)),
                (g.n0[C:C + 1, 0, :], row(a["L0_xattn_b_o"])),
                (wq1[:, :], a["L1_xattn_Wq"]), (wk1[:, :], a["L1_xattn_Wk"]), (wv1[:, :], a["L1_xattn_Wv"]),
                (film[:, 0:2 * D], a["L1_xattn_W_film_in"]), (film[:, 2 * D:], a["L1_xattn_W_film_out"]),
                (bfilm[C:C + 1, 0:2 * D], row(a["L1_xattn_b_film_in"])),
                (bfilm[C:C + 1, 2 * D:], row(a["L1_xattn_b_film_out"])),
                (gate_raw, a["L0_ffn_w_gate"].rearrange("(c p) n -> p c n", p=P)),
                (up_raw, a["L0_ffn_w_up"].rearrange("(c p) n -> p c n", p=P)),
                (qraw[:, 2, :], a["L0_ffn_w_down"]),
                (masks[:, 0, :], a["mask_BxS2_bk0"]), (masks[:, 1, :], a["mask_BxS2_bf1"]),
                (masks[:, 2, :], a["mask_BxS_bf1"]),
                (gate_s[:, :], bass.AP(a["L1_xattn_mod_gate"].tensor, 0, [[0, P], [1, 1]])),
                (logdt[:, :], col(a["L1_xattn_log_dt"])), (dskip[:, :], col(a["L1_xattn_D_skip"])),
                (are[:, :], a["L1_xattn_A_re"]), (aim[:, :], a["L1_xattn_A_im"]),
                (cre[:, :], a["L1_xattn_C_re"]), (cim[:, :], a["L1_xattn_C_im"]),
                (g.w1[:, :], a["L1_xattn_W1"]),
                (g.w2[:, :, :], a["L1_xattn_W2"].rearrange("(c p) n -> p c n", p=P)),
                (g.b1[:, :], a["L1_xattn_b1"].rearrange("(c p) -> p c", p=P)),
                (g.ffn_g[:, :], col(a["L1_xattn_g_ffn"])), (g.ffn_b[:, :], col(a["L1_xattn_b_ffn"])),
            ):
                with nc.allow_non_contiguous_dma(reason="small constants"):
                    sp.dma_start(dst, src).then_inc(loaded, 16)
                n += 1
            for k, name in enumerate(("g_norm_in", "b_norm_in", "b2", "g_norm_out", "b_norm_out")):
                src = a[f"L1_xattn_{name}"]
                sp.dma_start(g.wide[:, k, :], bass.AP(src.tensor, 0, [[0, P], [1, D]])).then_inc(loaded, 16)
                n += 1
            assert n == 35
            x_src = a["x"].rearrange("b s d -> (b s) d").rearrange("(t p) d -> p t d", p=P)
            for q in range(4):
                sp.dma_start(g.x[:, 16 * q:16 * q + 16, :], x_src[:, 16 * q:16 * q + 16, :]).then_inc(late, 16)
            sp.wait_ge(built, 1)
            sp.dma_start(g.mask_rows.rearrange("m (b s) -> b m s", b=BATCH), mrows[:, :, :]).then_inc(stored, 16)
            sp.wait_ge(built, 2)
            sp.dma_start(g.taps_out, taps.unsqueeze(1).to_broadcast([D, SEQ, 2 * SEQ])).then_inc(g.taps_stored, 16)
            sp.wait_ge(stored, 16)
            sp.wait_ge(late, 64)

        ALL = 16 * 35
        QUANT_AT = 7
        TMASK_AT = 10
        PHASES_AT = TMASK_AT + 14 + 3 + 2 + 3 + 1

        @block.gpsimd
        def _(pool):
            st = Steps(pool, pool_st)
            st.then(pool.memset(g.ident[:, :], 0.0))
            st.then(pool.affine_select(out=g.ident[:, :], in_=g.ident[:, :], compare_op=ALU.not_equal, fill=1.0,
                                       base=0, pattern=[[-1, P]], channel_multiplier=1))
            st.then(pool.memset(g.pairsum[:, :], 0.0))
            for base in (0, -SEQ):
                st.then(pool.affine_select(out=g.pairsum[:, :], in_=g.pairsum[:, :], compare_op=ALU.not_equal,
                                           fill=0.25, base=base, pattern=[[-1, SEQ]], channel_multiplier=1))
            st.then(pool.memset(g.minus_half[:, :], -0.5))
            st.then(pool.memset(g.eps[:, :], EPS))
            st.then(pool.memset(one_col[:, :], 1.0))
            pool.wait_ge(loaded, ALL)
            st.then(pool.memset(g.n0[C:C + 1, 1:H0, :], 0.0))

        turns_of = ([(wq[:, 128 * i:128 * i + 128], P, P) for i in range(4)]
                    + [(wk[:, 128 * i:128 * i + 128], C, P) for i in range(4)]
                    + [(wv[:, 128 * i:128 * i + 128], C, P) for i in range(4)]
                    + [(wq1[:, :], P, P), (wk1[:, :], C, P), (wv1[:, :], C, P)])
        quant_of = ([gate_raw[:, i, :] for i in range(IC)] + [up_raw[:, i, :] for i in range(IC)]
                    + [down_raw[:, i, :] for i in range(IC)])

        @block.tensor
        def _(pe):
            pe.wait_ge(loaded, ALL)
            pe.wait_ge(pool_st, 2)
            for i, (src, rows, cols) in enumerate(turns_of):
                pe.transpose(pt[i // 4][0:cols, 128 * (i % 4):128 * (i % 4) + rows], src,
                             g.ident[0:rows, 0:rows]).then_inc(pe_ready, 1)
            pe.wait_ge(act_st, 1)
            n = len(turns_of)
            for h in range(H0):
                r = DH0 * (h % 2)
                pe.matmul(pt[4 + h % 2][:, 128 * (h // 2):128 * (h // 2) + C], turned[r:r + DH0, h // 2, 0:P],
                          turned[r:r + DH0, 4 + h // 2, 0:C], start=True, stop=True).then_inc(pe_ready, 1)
            for h in range(H0):
                r = DH0 * (h % 2)
                pe.matmul(pt[6 + h % 2][0:C, 128 * (h // 2):128 * (h // 2) + D], turned[r:r + DH0, 8 + h // 2, 0:C],
                          wo[r:r + DH0, h // 2, :], start=True, stop=True).then_inc(pe_ready, 1)
            n += 16
            pe.wait_ge(act_st, 2)
            for h in range(H1):
                r = DH1 * h
                pe.matmul(pt[h][:, 0:C], turned[r:r + DH1, 12, 0:P],
                          turned[r:r + DH1, 13, 0:C], start=True, stop=True).then_inc(pe_ready, 1)
            pe.matmul(pt[4][0:C, :], turned[:, 14, 0:C], film[:, :], start=True, stop=True).then_inc(pe_ready, 1)
            pe.wait_ge(dve_st, QUANT_AT)
            for i, src in enumerate(quant_of):
                pe.transpose(pt[5 + i // 4][:, 128 * (i % 4):128 * (i % 4) + 128], src,
                             g.ident[:, :]).then_inc(pe_ready, 1)
            pe.wait_ge(dve_st, TMASK_AT)
            pe.wait_ge(act_st, 3)
            pe.transpose(pt[0][:, 0:P], tmb[:, :, :].rearrange("p a s -> p (a s)"), g.ident[:, :]).then_inc(pe_ready, 1)

        @block.scalar
        def _(act):
            act.wait_ge(pe_ready, 15)
            st = Steps(act, act_st)
            for b in range(4):
                k = 4 if b < 3 else 3
                rows = P if b in (0, 3) else C
                src = pt[b][:, 0:128 * k].rearrange("p (i n) -> p i n", n=128)
                if b == 3:
                    act.copy(turned[:, 12:13, :], src[:, 0:1, :])
                    ins = act.copy(turned[:, 13:15, 0:C], src[:, 1:3, 0:C])
                else:
                    ins = act.copy(turned[:, 4 * b:4 * b + k, 0:rows], src[:, :, 0:rows])
            st.then(ins)
            act.wait_ge(pe_ready, 31)
            for b in range(2):
                act.copy(g.m0[:, b::2, :],
                         pt[4 + b][:, :].rearrange("p (i n) -> p i n", n=128)[:, :, 0:C])
                ins = act.copy(g.n0[0:C, b::2, :],
                               pt[6 + b][0:C, :].rearrange("p (i n) -> p i n", n=128))
            st.then(ins)
            act.wait_ge(pe_ready, 36)
            for h in range(H1):
                act.copy(g.m1[:, h, :], pt[h][:, 0:C])
            act.mul(g.film[0:C, :], pt[4][0:C, :], gate_s[0:C, 0:1])
            ins = act.mul(g.film[C:C + 1, :], bfilm[C:C + 1, :], gate_s[C:C + 1, 0:1])
            st.then(ins)
            fr = g.film[C:C + 1, :].rearrange("p (a b n) -> p a b n", a=2, b=2)
            act.wait_ge(pool_st, 8)
            st.then(act.activation(fr[:, :, 0, :], fr[:, :, 0, :], ACT.Identity, bias=one_col[C:C + 1, 0:1]))
            act.wait_ge(pe_ready, 45)
            act.copy(g.gate_t[:, 0:3 * P], pt[5][:, 0:3 * P])
            act.copy(g.up_t[:, 0:P], pt[5][:, 3 * P:])
            act.copy(g.up_t[:, P:3 * P], pt[6][:, 0:2 * P])
            act.copy(g.down_t[:, 0:2, :], pt[6][:, 2 * P:].rearrange("p (i n) -> p i n", n=P))
            ins = act.copy(g.down_t[:, 2, :], pt[7][:, 0:P])
            act.wait_ge(pe_ready, 46)
            ins = act.copy(g.tmask[:, :], pt[0][:, 0:P])
            st.then(ins)
            act.wait_ge(dve_st, PHASES_AT)
            st.then(act.activation(decay[:, :, :], decay[:, :, :], ACT.Exp))
            act.activation(sine[:, :, :], phase[:, :, :], ACT.Sin)
            st.then(act.activation(half[:, :, :], phase[:, :, :], ACT.Sin, scale=0.5))

        @block.vector
        def _(dve):
            st = Steps(dve, dve_st)
            dve.wait_ge(loaded, ALL)
            st.then(dve.tensor_reduce(bamax[:, :], blocks, X, ALU.max, apply_absolute_value=True))
            st.then(dve.tensor_scalar(bamax[:, :], bamax[:, :], 1.0 / 7.0, 1e-12, ALU.mult, ALU.max))
            st.then(dve.reciprocal(binv[:, :], bamax[:, :]))
            st.then(dve.tensor_tensor(blocks, blocks, binv[:, :].unsqueeze(2).to_broadcast([P, 36, 32]), ALU.mult))
            st.then(dve.tensor_scalar(blocks, blocks, MAGIC, MAGIC, ALU.add, ALU.subtract))
            st.then(dve.tensor_scalar(blocks, blocks, 7.0, -8.0, ALU.min, ALU.max))
            st.then(dve.tensor_tensor(blocks, blocks, bamax[:, :].unsqueeze(2).to_broadcast([P, 36, 32]), ALU.mult))
            assert st.n == QUANT_AT
            st.then(dve.tensor_scalar(mrows[:, :, :], masks[:, 0:2, :], -1.0, FAR, ALU.add, ALU.mult))
            dve.sem_inc(built, 1)
            st.then(dve.tensor_copy(tmb[:, 0, :], masks[:, 2, :]))
            st.then(dve.tensor_copy(tmb[:, 1, :], masks[:, 2, :]))
            assert st.n == TMASK_AT
            exp_steps(dve, st, logdt[:, :], dt[:, :], t1t[:, :], t1k[:, :], t1i[:, :], t1p[:, :])
            st.then(dve.tensor_scalar(a1[:, :], are[:, :], dt[:, 0:1], None, ALU.mult))
            st.then(dve.tensor_scalar(b1[:, :], aim[:, :], dt[:, 0:1], None, ALU.mult))
            for k in range(16):
                f = float(k if k < 8 else 8 * (k - 8))
                dve.tensor_scalar(phase[:, k, :], b1[:, :], f, None, ALU.mult)
                last = dve.tensor_scalar(decay[:, k, :], a1[:, :], f, None, ALU.mult)
            st.then(last)
            st.then(dve.tensor_scalar(turns[:, :, :], phase[:, :, :], 1 / TWO_PI, MAGIC, ALU.mult, ALU.add))
            st.then(dve.tensor_scalar(turns[:, :, :], turns[:, :, :], MAGIC, None, ALU.subtract))
            c1 = 6.28125
            c2 = float(np.float32(np.round((TWO_PI - c1) * 2 ** 21) / 2 ** 21))
            c3 = TWO_PI - c1 - c2
            for c in (c1, c2, c3):
                st.then(dve.scalar_tensor_tensor(out=phase[:, :, :], in0=turns[:, :, :], scalar=-c,
                                                 in1=phase[:, :, :], op0=ALU.mult, op1=ALU.add))
            st.then(dve.tensor_scalar(phase[:, :, :], phase[:, :, :], 3.1415925, -3.1415925, ALU.min, ALU.max))
            assert st.n == PHASES_AT, st.n
            exp_steps(dve, st, a1[:, :], ea[:, :], z1[:, :], z2[:, :], zi[:, :], z3[:, :])
            dve.wait_ge(act_st, 7)
            st.then(dve.tensor_tensor(half[:, :, :], half[:, :, :], half[:, :, :], ALU.mult))
            st.then(dve.tensor_scalar(cosine[:, :, :], half[:, :, :], -2.0, 1.0, ALU.mult, ALU.add))
            st.then(dve.scalar_tensor_tensor(out=z1[:, :], in0=ea[:, :], scalar=-1.0, in1=cosine[:, 1, :],
                                             op0=ALU.add, op1=ALU.mult))
            st.then(dve.scalar_tensor_tensor(out=wr[:, :], in0=half[:, 1, :], scalar=-2.0, in1=z1[:, :],
                                             op0=ALU.mult, op1=ALU.add))
            st.then(dve.tensor_tensor(wi[:, :], ea[:, :], sine[:, 1, :], ALU.mult))
            st.then(dve.tensor_tensor(z1[:, :], are[:, :], are[:, :], ALU.mult))
            st.then(dve.tensor_tensor(z2[:, :], aim[:, :], aim[:, :], ALU.mult))
            st.then(dve.tensor_tensor(z1[:, :], z1[:, :], z2[:, :], ALU.add))
            st.then(dve.reciprocal(inv[:, :], z1[:, :]))

            def complex_mult(outr, outi, xr, xi, yr, yi, sign, scale, t1, t2):
                st.then(dve.tensor_tensor(t1, xi, yi, ALU.mult))
                st.then(dve.tensor_tensor(t2, xr, yi, ALU.mult))
                st.then(dve.tensor_tensor(outr, xr, yr, ALU.mult))
                st.then(dve.scalar_tensor_tensor(out=outr, in0=t1, scalar=-float(sign), in1=outr, op0=ALU.mult, op1=ALU.add))
                st.then(dve.tensor_tensor(outi, xi, yr, ALU.mult))
                st.then(dve.scalar_tensor_tensor(out=outi, in0=t2, scalar=float(sign), in1=outi, op0=ALU.mult, op1=ALU.add))

            complex_mult(dr[:, :], di[:, :], wr[:, :], wi[:, :], are[:, :], aim[:, :], -1, 1, z1[:, :], z2[:, :])
            st.then(dve.tensor_tensor(dr[:, :], dr[:, :], inv[:, :], ALU.mult))
            st.then(dve.tensor_tensor(di[:, :], di[:, :], inv[:, :], ALU.mult))
            complex_mult(wr[:, :], wi[:, :], dr[:, :], di[:, :], cre[:, :], cim[:, :], 1, 1, z1[:, :], z2[:, :])
            st.then(dve.tensor_scalar(wr[:, :], wr[:, :], 2.0, None, ALU.mult))
            st.then(dve.tensor_scalar(wi[:, :], wi[:, :], 2.0, None, ALU.mult))
            st.then(dve.tensor_tensor(cosine[:, :, :], cosine[:, :, :], decay[:, :, :], ALU.mult))
            st.then(dve.tensor_tensor(sine[:, :, :], sine[:, :, :], decay[:, :, :], ALU.mult))
            wrb = wr[:, :].unsqueeze(1).to_broadcast([P, 8, NS])
            wib = wi[:, :].unsqueeze(1).to_broadcast([P, 8, NS])
            complex_mult(ur[:, :, :], ui[:, :, :], cosine[:, 8:16, :], sine[:, 8:16, :], wrb, wib, 1, 1,
                         prod[:, :, :], prod2[:, :, :])
            st.then(dve.memset(taps[:, 0:SEQ], 0.0))
            for l1 in range(8):
                st.then(dve.tensor_tensor(prod[:, :, :], cosine[:, 0:8, :],
                                          ur[:, l1, :].unsqueeze(1).to_broadcast([P, 8, NS]), ALU.mult))
                st.then(dve.tensor_tensor(prod2[:, :, :], sine[:, 0:8, :],
                                          ui[:, l1, :].unsqueeze(1).to_broadcast([P, 8, NS]), ALU.mult))
                st.then(dve.tensor_tensor(prod[:, :, :], prod[:, :, :], prod2[:, :, :], ALU.subtract))
                st.then(dve.tensor_reduce(taps[:, SEQ + 8 * l1:SEQ + 8 * l1 + 8], prod[:, :, :], X, ALU.add))
            st.then(dve.tensor_tensor(taps[:, SEQ:SEQ + 1], taps[:, SEQ:SEQ + 1], dskip[:, :], ALU.add))
            dve.sem_inc(built, 1)


def norm_steps(dve, carry, pool_done, st, x_tiles, stats, mv, out_tiles, pool_ready, count):
    norm_stats(dve, carry, st, x_tiles, stats, mv, pool_ready)
    dve.wait_ge(pool_done, count + 1)
    return norm_apply(dve, x_tiles, mv, out_tiles)


def norm_stats(dve, carry, st, x_tiles, stats, mv, pool_ready):
    for t in range(QT):
        last = dve.bn_stats(stats[:, t, :], x_tiles[t])
    st.then(last)
    dve.memset(carry[:, 0:1], 0.0)
    for t in range(QT):
        last = dve.bn_aggr(mv[:, t, :], stats[:, t, :])
    last.then_inc(pool_ready, 1)


def norm_apply(dve, x_tiles, mv, out_tiles):
    for t in range(QT):
        last = dve.tensor_scalar(out_tiles[t], x_tiles[t], mv[:, t, 0:1], mv[:, t, 1:2], ALU.subtract, ALU.mult)
    return last


def rstd_steps(pool, g, mv, stats_ready, rstd_ready, link, count):
    pool.wait_ge(stats_ready, count + 1)
    link.then(pool.tensor_tensor(mv[:, :, 1:2], mv[:, :, 1:2], g.eps[:, 0:QT].unsqueeze(2), ALU.add))
    pool.tensor_tensor(mv[:, :, 1:2], mv[:, :, 1:2], g.minus_half[:, 0:QT].unsqueeze(2), ALU.pow).then_inc(rstd_ready, 1)


def attention0(nc, a, g):
    with ExitStack() as stack:
        m = Memory(nc, stack, "at0")
        ctx_in = [m.sem(f"ctx_in{u}") for u in range(2)]
        stats_ready, rstd_ready = m.sem("stats_ready"), m.sem("rstd_ready")
        xn_ready = m.sem("xn_ready")
        ring_ready, ring_evac = m.sem("ring_ready"), m.sem("ring_evac")
        s_ready, shifted, exp_ready = m.sem("s_ready"), m.sem("shifted"), m.sem("exp_ready")
        inv_ready, prob_ready = m.sem("inv_ready"), m.sem("prob_ready")
        pt_ready, pt_evac = m.sem("pt_ready"), m.sem("pt_evac")
        c_ready, c_evac = m.sem("c_ready"), m.sem("c_evac")
        o_ready, x_added = m.sem("o_ready"), m.sem("x_added")
        dve_st, pool_st = m.sem("dve_st"), m.sem("pool_st")

        xn = m.sb("xn", (P, 2, QT, P))
        xnt = m.sb("xnt", (P, 2, QN))
        ctxn = m.sb("ctxn", (P, 2, QT, C))
        ctxt = m.sb("ctxt", (C + 2, 2, QN))
        qm = m.sb("qm", (C + 2, 2, 2 * QT, H0 * SEQ))
        stats = m.sb("stats", (P, 2, QT, 6))
        mv = m.sb("mv", (P, 2, QT, 2))
        sd = m.sb("sd", (P, 2, 8, SEQ))
        mx, sm = m.sb("mx", (P, 2, 8)), m.sb("sm", (P, 2, 8))
        pr = m.sb("pr", (P, 2, 8, SEQ))
        pts = m.sb("pts", (P, 2, 4 * P))
        ct = m.sb("ct", (C + 1, 2, H0, P))
        ring = [m.ps(f"ring{i}") for i in range(2)]
        sp_ = [m.ps(f"s{i}") for i in range(2)]
        ptp = m.ps("pt")
        cp = [m.ps(f"c{i}") for i in range(2)]
        op = m.ps("o")
        block = stack.enter_context(nc.Block())
        RING = 10
        pieces = ((0, 1, 2), (3, 4, 5), (6, 7), (8, 9))
        ctx_src = a["ctx_768"].rearrange("b s c -> (b s) c").rearrange("(q t p) c -> q p t c", p=P, t=QT)
        mask_src = g.mask_rows.rearrange("m (q n) -> q m n", q=QUADS)

        @block.sync
        def _(sp):
            def load(j, u):
                q = 2 * j + u
                wait(sp, c_ready, 8 * (q - 1))
                sp.dma_start(ctxn[:, u, :, :], at_quad(ctx_src, q)).then_inc(ctx_in[u], 16)
                sp.dma_start(ctxt[C:C + 2, u, :], at_quad(mask_src, q)).then_inc(ctx_in[u], 16)
            over_pairs(sp, load)

        def front_pe(pe, j, u, ks):
            q = 2 * j + u
            for k in ks:
                n = RING * q + k
                slot = ring[k % 2]
                if k == 9:
                    pe.wait_ge(ctx_in[u], 32 * (j + 1))
                if k == 0:
                    pe.wait_ge(xn_ready, q + 1)
                wait(pe, ring_evac, n - 1 if k != 1 else n)
                if k == 9:
                    for t in range(QT):
                        last = pe.transpose(slot[0:C, t * P:t * P + P], ctxn[:, u, t, :], g.ident[:, :])
                elif k == 0:
                    for t in range(QT):
                        last = pe.transpose(slot[:, t * P:t * P + P], xn[:, u, t, :], g.ident[:, :])
                else:
                    last = pe.matmul(slot[0:C, :], g.m0[:, k - 1, :], xnt[:, u, :], start=True, stop=True)
                last.then_inc(ring_ready, 1)

        def front_act(act, j, u, ks):
            q = 2 * j + u
            for k in ks:
                act.wait_ge(ring_ready, RING * q + k + 1)
                slot = ring[k % 2]
                if k == 9:
                    ins = act.copy(ctxt[0:C, u, :], slot[0:C, :])
                elif k == 0:
                    ins = act.copy(xnt[:, u, :], slot[:, :])
                else:
                    ins = act.copy(qm[0:C, u, :, (k - 1) * SEQ:k * SEQ],
                                   slot[0:C, :].rearrange("c (b s) -> c b s", s=SEQ))
                ins.then_inc(ring_evac, 1)

        @block.tensor
        def _(pe):
            def scores(j, u, t):
                q, n = 2 * j + u, 8 * j + 4 * u + t
                wait(pe, ring_evac, RING * (q + 1))
                wait(pe, shifted, n - 1)
                for b in range(2):
                    tok = slice(t * P + b * SEQ, t * P + b * SEQ + SEQ)
                    for p in range(4):
                        c0 = (2 * p + b) * SEQ
                        last = pe.matmul(sp_[t % 2][:, c0:c0 + SEQ], qm[:, u, 2 * t + b, 2 * p * SEQ:2 * (p + 1) * SEQ],
                                         ctxt[:, u, tok], start=True, stop=True)
                last.then_inc(s_ready, 1)

            def turn(n, t):
                pe.wait_ge(prob_ready, n + 1)
                wait(pe, pt_evac, n)
                for p in range(4):
                    last = pe.transpose(ptp[:, p * P:p * P + P],
                                        pr[:, t % 2, 2 * p:2 * p + 2, :].rearrange("p a s -> p (a s)"), g.ident[:, :])
                last.then_inc(pt_ready, 1)

            def attend(n, u, t):
                pe.wait_ge(pt_evac, n + 1)
                for b in range(2):
                    wait(pe, c_evac, 2 * n - 1 + b)
                    r = slice(b * SEQ, b * SEQ + SEQ)
                    pe.matmul(cp[b][0:C, :], ctxn[r, u, t, :], pts[r, t % 2, :],
                              start=True, stop=True).then_inc(c_ready, 1)

            def project(n, q, t):
                pe.wait_ge(c_evac, 2 * n + 2)
                if t == 0:
                    wait(pe, x_added, q)
                for h in range(H0):
                    last = pe.matmul(op[:, t * P:t * P + P], ct[:, t % 2, h, :], g.n0[:, h, :],
                                     start=(h == 0), stop=(h == H0 - 1))
                last.then_inc(o_ready, 1)

            def body(j, u):
                for t in range(QT):
                    n, q = 8 * j + 4 * u + t, 2 * j + u
                    more = not (isinstance(q, int) and q == QUADS - 1)
                    if more:
                        front_pe(pe, j + (u == 1), 1 - u, pieces[t])
                    if t < 3:
                        scores(j, u, t + 1)
                    turn(n, t)
                    if t == 3 and more:
                        scores(j + (u == 1), 1 - u, 0)
                    if t > 0:
                        project(n - 1, q, t - 1)
                    elif not (isinstance(q, int) and q == 0):
                        project(n - 1, q - 1, 3)
                    attend(n, u, t)

            pe.wait_ge(pool_st, 3)
            front_pe(pe, 0, 0, range(RING))
            scores(0, 0, 0)
            over_pairs(pe, body)
            project(TILES - 1, QUADS - 1, 3)

        @block.scalar
        def _(act):
            def exps(n, t):
                act.wait_ge(shifted, n + 1)
                act.activation(sd[:, t % 2, :, :], sd[:, t % 2, :, :], ACT.Exp, scale=DH0 ** -0.5).then_inc(exp_ready, 1)

            def body(j, u):
                for t in range(QT):
                    n, q = 8 * j + 4 * u + t, 2 * j + u
                    more = not (isinstance(q, int) and q == QUADS - 1)
                    if more:
                        front_act(act, j + (u == 1), 1 - u, pieces[t])
                    act.wait_ge(pt_ready, n + 1)
                    act.copy(pts[:, t % 2, :], ptp[:, :]).then_inc(pt_evac, 1)
                    if more or t < 3:
                        exps(n + 1, t + 1)
                    for b in range(2):
                        act.wait_ge(c_ready, 2 * n + 1 + b)
                        act.copy(ct[0:C, t % 2, :, b * SEQ:b * SEQ + SEQ],
                                 cp[b][0:C, :].rearrange("p (h s) -> p h s", s=SEQ)).then_inc(c_evac, 1)

            front_act(act, 0, 0, range(RING))
            exps(0, 0)
            over_pairs(act, body)

        @block.gpsimd
        def _(pool):
            st = Steps(pool, pool_st)
            st.then(pool.memset(qm[C:C + 2, :, :, :], 0.0))
            st.then(pool.memset(qm[C:C + 1, :, :, :], 1.0))
            st.then(pool.memset(ct[C:C + 1, :, :, :], 1.0))

            def rstd(j, u):
                rstd_steps(pool, g, mv[:, u, :, :], stats_ready, rstd_ready, st, 2 * j + u)

            def body(j, u):
                for t in range(QT):
                    n, q = 8 * j + 4 * u + t, 2 * j + u
                    if t == 2 and not (isinstance(q, int) and q >= QUADS - 2):
                        rstd(j + 1, u)
                    pool.wait_ge(inv_ready, n + 1)
                    wait(pool, pt_ready, n - 1)
                    pool.tensor_tensor(pr[:, t % 2, :, :], sd[:, t % 2, :, :],
                                       sm[:, t % 2, :].unsqueeze(2).to_broadcast([P, 8, SEQ]),
                                       ALU.mult).then_inc(prob_ready, 1)

            rstd(0, 0)
            rstd(0, 1)
            over_pairs(pool, body, [st])

        @block.vector
        def _(dve):
            st = Steps(dve, dve_st)

            def stats_of(j, u):
                q = 2 * j + u
                wait(dve, xn_ready, q - 1)
                norm_stats(dve, g.carry, st, [g.xt(q, t) for t in range(QT)], stats[:, u, :, :], mv[:, u, :, :],
                           stats_ready)

            def norm(j, u):
                q = 2 * j + u
                wait(dve, ring_ready, RING * (q - 2) + 1)
                dve.wait_ge(rstd_ready, q + 1)
                norm_apply(dve, [g.xt(q, t) for t in range(QT)], mv[:, u, :, :],
                           [xn[:, u, t, :] for t in range(QT)]).then_inc(xn_ready, 1)

            def shift(n, t):
                dve.wait_ge(s_ready, n + 1)
                src = sp_[t % 2][:, :].rearrange("p (k s) -> p k s", s=SEQ)
                st.then(dve.tensor_reduce(mx[:, t % 2, :], src, X, ALU.max))
                wait(dve, prob_ready, n - 1)
                dve.tensor_tensor(sd[:, t % 2, :, :], src, mx[:, t % 2, :].unsqueeze(2).to_broadcast([P, 8, SEQ]),
                                  ALU.subtract).then_inc(shifted, 1)

            def sums(n, t):
                dve.wait_ge(exp_ready, n + 1)
                st.then(dve.tensor_reduce(sm[:, t % 2, :], sd[:, t % 2, :, :], X, ALU.add))
                dve.reciprocal(sm[:, t % 2, :], sm[:, t % 2, :]).then_inc(inv_ready, 1)

            def add(q):
                dve.wait_ge(o_ready, 4 * (q + 1))
                xs = g.xq(q)
                dve.tensor_tensor(xs, xs, op[:, :], ALU.add).then_inc(x_added, 1)

            def body(j, u):
                for t in range(QT):
                    n, q = 8 * j + 4 * u + t, 2 * j + u
                    sums(n, t)
                    if t < 3 or not (isinstance(q, int) and q == QUADS - 1):
                        shift(n + 1, t + 1)
                    if t == 0 and not (isinstance(q, int) and q == 0):
                        add(q - 1)
                    if t == 1 and not (isinstance(q, int) and q >= QUADS - 2):
                        stats_of(j + 1, u)
                    if t == 2 and not (isinstance(q, int) and q >= QUADS - 2):
                        norm(j + 1, u)

            for u in range(2):
                stats_of(0, u)
                norm(0, u)
            shift(0, 0)
            over_pairs(dve, body, [st])
            add(QUADS - 1)


class Quantised:

    def __init__(self, nc, stack):
        m = Memory(nc, stack, "ffn")
        self.h_t = m.sb("h_t", (P, TOK))
        self.act = m.sb("act", (P, IC, TOK))
        self.peak = m.sb("peak", (P, 2, QUADS))
        self.top = m.sb("top", (P, 2))
        self.scale = m.sb("scale", (P, 5))
        self.inv = m.sb("inv", (P, 5))

    def piece(self, q):
        return self.h_t[:, bass.ds(q * QN, QN)]

    def act_piece(self, q):
        return self.act[:, :, bass.ds(q * QN, QN)]


H_IN, H_UP, H_GATE, H_GATED, H_OUT = range(5)


def scale_dve(dve, st, f, kinds, peak_ready, top_ready):
    n = len(kinds)
    dve.tensor_reduce(f.top[:, 0:n], f.peak[:, 0:n, :], X, ALU.max).then_inc(peak_ready, 1)
    dve.wait_ge(top_ready, 1)
    k = slice(kinds[0], kinds[0] + n)
    st.then(dve.tensor_scalar(f.scale[:, k], f.top[:, 0:n], 1.0 / QMAX, 1e-12, ALU.mult, ALU.max))
    st.then(dve.reciprocal(f.inv[:, k], f.scale[:, k]))


def scale_pool(pool, f, n, peak_ready, top_ready):
    pool.wait_ge(peak_ready, 1)
    pool.partition_all_reduce(f.top[:, 0:n], f.top[:, 0:n], P, RMAX).then_inc(top_ready, 1)


def act_quant(nc, a, g):
    f = g.f
    with ExitStack() as stack:
        m = Memory(nc, stack, "aq")
        stats_ready, rstd_ready, xn_ready = m.sem("stats_ready"), m.sem("rstd_ready"), m.sem("xn_ready")
        turned, evac, peaked = m.sem("turned"), m.sem("evac"), m.sem("peaked")
        peak_ready, top_ready = m.sem("peak_ready"), m.sem("top_ready")
        dve_st, pool_st = m.sem("dve_st"), m.sem("pool_st")
        xn = m.sb("xn", (P, 2, QT, P))
        stats = m.sb("stats", (P, 2, QT, 6))
        mv = m.sb("mv", (P, 2, QT, 2))
        bank = [m.ps(f"t{i}") for i in range(2)]
        block = stack.enter_context(nc.Block())

        @block.tensor
        def _(pe):
            def body(j, u):
                q = 2 * j + u
                pe.wait_ge(xn_ready, q + 1)
                wait(pe, evac, q - 1)
                for t in range(QT):
                    last = pe.transpose(bank[u][:, t * P:t * P + P], xn[:, u, t, :], g.ident[:, :])
                last.then_inc(turned, 1)
            over_pairs(pe, body)

        @block.scalar
        def _(act):
            def body(j, u):
                q = 2 * j + u
                act.wait_ge(turned, q + 1)
                act.copy(f.piece(q), bank[u][:, :]).then_inc(evac, 1)
            over_pairs(act, body)

        @block.gpsimd
        def _(pool):
            st = Steps(pool, pool_st)
            over_pairs(pool, lambda j, u: rstd_steps(pool, g, mv[:, u, :, :], stats_ready, rstd_ready, st, 2 * j + u),
                       [st])
            scale_pool(pool, f, 1, peak_ready, top_ready)

        @block.vector
        def _(dve):
            st = Steps(dve, dve_st)

            def norm(j, u):
                q = 2 * j + u
                wait(dve, turned, q - 1)
                norm_steps(dve, g.carry, rstd_ready, st, [g.xt(q, t) for t in range(QT)], stats[:, u, :, :],
                           mv[:, u, :, :], [xn[:, u, t, :] for t in range(QT)], stats_ready, q).then_inc(xn_ready, 1)

            def body(j, u):
                q = 2 * j + u
                if not (isinstance(q, int) and q == QUADS - 1):
                    norm(j + u, 1 - u)
                dve.wait_ge(evac, q + 1)
                dve.tensor_reduce(f.peak[:, 0, bass.ds(q, 1)], f.piece(q), X, ALU.max,
                                  apply_absolute_value=True).then_inc(peaked, 1)

            norm(0, 0)
            over_pairs(dve, body, [st])
            dve.wait_ge(peaked, QUADS)
            scale_dve(dve, st, f, [H_IN], peak_ready, top_ready)
            dve.wait_ge(evac, QUADS)
            for i in range(4):
                h = f.h_t[:, i * TOK // 4:(i + 1) * TOK // 4]
                st.then(dve.tensor_scalar(h, h, f.inv[:, H_IN:H_IN + 1], MAGIC, ALU.mult, ALU.add))
                st.then(dve.tensor_scalar(h, h, MAGIC, f.scale[:, H_IN:H_IN + 1], ALU.subtract, ALU.mult))


def gate_up_max(nc, a, g):
    f = g.f
    with ExitStack() as stack:
        m = Memory(nc, stack, "gum")
        made, peaked, peak_ready, top_ready, dve_st = (
            m.sem(n) for n in ("made", "peaked", "peak_ready", "top_ready", "dve_st"))
        group = [m.ps(f"p{i}", (P, IC, 512)) for i in range(2)]
        block = stack.enter_context(nc.Block())

        @block.tensor
        def _(pe):
            def body(j, u):
                q = 2 * j + u
                for k, w in enumerate((g.up_t, g.gate_t)):
                    wait(pe, peaked, 2 * q + k - 1)
                    for c in range(IC):
                        last = pe.matmul(group[k][:, c, :], w[:, c * P:c * P + P], f.piece(q), start=True, stop=True)
                    last.then_inc(made, 1)
            over_pairs(pe, body)

        @block.gpsimd
        def _(pool):
            scale_pool(pool, f, 2, peak_ready, top_ready)

        @block.vector
        def _(dve):
            st = Steps(dve, dve_st)

            def body(j, u):
                q = 2 * j + u
                for k in range(2):
                    dve.wait_ge(made, 2 * q + k + 1)
                    dve.tensor_reduce(f.peak[:, k, bass.ds(q, 1)], group[k][:, :, :], XY, ALU.max,
                                      apply_absolute_value=True).then_inc(peaked, 1)
            over_pairs(dve, body)
            dve.wait_ge(peaked, 2 * QUADS)
            scale_dve(dve, st, f, [H_UP, H_GATE], peak_ready, top_ready)


def gate(nc, a, g):
    f = g.f
    with ExitStack() as stack:
        m = Memory(nc, stack, "gate")
        made, shifted, rounded, sig_ready, peaked, peak_ready, top_ready, dve_st = (
            m.sem(n) for n in ("made", "shifted", "rounded", "sig_ready", "peaked", "peak_ready", "top_ready", "dve_st"))
        group = [m.ps(f"p{i}", (P, IC, 512)) for i in range(2)]
        gt = m.sb("gt", (P, 2, IC, QN))
        sg = m.sb("sg", (P, 2, IC, QN))
        magic = m.sb("magic", (P, 1))
        block = stack.enter_context(nc.Block())

        @block.tensor
        def _(pe):
            def body(j, u):
                q = 2 * j + u
                wait(pe, shifted, q - 1)
                for c in range(IC):
                    last = pe.matmul(group[u][:, c, :], g.gate_t[:, c * P:c * P + P], f.piece(q), start=True, stop=True)
                last.then_inc(made, 1)
            over_pairs(pe, body)

        @block.scalar
        def _(act):
            def shift(j, u):
                q = 2 * j + u
                act.wait_ge(made, q + 1)
                wait(act, peaked, q - 1)
                act.activation(gt[:, u, :, :], group[u][:, :, :], ACT.Identity, scale=f.inv[:, H_GATE:H_GATE + 1],
                               bias=magic[:, 0:1]).then_inc(shifted, 1)

            def body(j, u):
                q = 2 * j + u
                if not (isinstance(q, int) and q == QUADS - 1):
                    shift(j + u, 1 - u)
                act.wait_ge(rounded, q + 1)
                act.activation(sg[:, u, :, :], gt[:, u, :, :], ACT.Sigmoid).then_inc(sig_ready, 1)
            act.wait_ge(dve_st, 1)
            shift(0, 0)
            over_pairs(act, body)

        @block.gpsimd
        def _(pool):
            scale_pool(pool, f, 1, peak_ready, top_ready)

        @block.vector
        def _(dve):
            st = Steps(dve, dve_st)

            def grid(j, u):
                q = 2 * j + u
                dve.wait_ge(shifted, q + 1)
                dve.tensor_scalar(gt[:, u, :, :], gt[:, u, :, :], MAGIC, f.scale[:, H_GATE:H_GATE + 1],
                                  ALU.subtract, ALU.mult).then_inc(rounded, 1)

            def body(j, u):
                q = 2 * j + u
                if not (isinstance(q, int) and q == QUADS - 1):
                    grid(j + u, 1 - u)
                dve.wait_ge(sig_ready, q + 1)
                s = sg[:, u, :, :]
                st.then(dve.tensor_scalar(s, s, 65536.0, MAGIC, ALU.mult, ALU.add))
                st.then(dve.tensor_scalar(s, s, MAGIC + 65535.0, MAGIC, ALU.min, ALU.subtract))
                st.then(dve.scalar_tensor_tensor(out=f.act_piece(q), in0=s, scalar=1.0 / 65536, in1=gt[:, u, :, :],
                                                 op0=ALU.mult, op1=ALU.mult))
                dve.tensor_reduce(f.peak[:, 0, bass.ds(q, 1)], f.act_piece(q), XY, ALU.max,
                                  apply_absolute_value=True).then_inc(peaked, 1)
            st.then(dve.memset(magic[:, :], MAGIC))
            grid(0, 0)
            over_pairs(dve, body, [st])
            dve.wait_ge(peaked, QUADS)
            scale_dve(dve, st, f, [H_GATED], peak_ready, top_ready)


def up(nc, a, g):
    f = g.f
    with ExitStack() as stack:
        m = Memory(nc, stack, "up")
        made, shifted, again, peaked, peak_ready, top_ready, dve_st = (
            m.sem(n) for n in ("made", "shifted", "again", "peaked", "peak_ready", "top_ready", "dve_st"))
        group = [m.ps(f"p{i}", (P, IC, 512)) for i in range(2)]
        ut = m.sb("ut", (P, 2, IC, QN))
        gt = m.sb("gt", (P, 2, IC, QN))
        magic = m.sb("magic", (P, 1))
        block = stack.enter_context(nc.Block())

        @block.tensor
        def _(pe):
            def body(j, u):
                q = 2 * j + u
                wait(pe, shifted, q - 1)
                for c in range(IC):
                    last = pe.matmul(group[u][:, c, :], g.up_t[:, c * P:c * P + P], f.piece(q), start=True, stop=True)
                last.then_inc(made, 1)
            over_pairs(pe, body)

        @block.scalar
        def _(act):
            def body(j, u):
                q = 2 * j + u
                wait(act, peaked, q - 1)
                act.activation(gt[:, u, :, :], f.act_piece(q), ACT.Identity, scale=f.inv[:, H_GATED:H_GATED + 1],
                               bias=magic[:, 0:1]).then_inc(again, 1)
                act.wait_ge(made, q + 1)
                act.activation(ut[:, u, :, :], group[u][:, :, :], ACT.Identity, scale=f.inv[:, H_UP:H_UP + 1],
                               bias=magic[:, 0:1]).then_inc(shifted, 1)
            act.wait_ge(dve_st, 1)
            over_pairs(act, body)

        @block.gpsimd
        def _(pool):
            scale_pool(pool, f, 1, peak_ready, top_ready)

        @block.vector
        def _(dve):
            st = Steps(dve, dve_st)

            def body(j, u):
                q = 2 * j + u
                gv, uv = gt[:, u, :, :], ut[:, u, :, :]
                dve.wait_ge(again, q + 1)
                st.done(dve.tensor_scalar(gv, gv, MAGIC, f.scale[:, H_GATED:H_GATED + 1], ALU.subtract, ALU.mult))
                dve.wait_ge(shifted, q + 1)
                st.then(dve.tensor_scalar(uv, uv, MAGIC, f.scale[:, H_UP:H_UP + 1], ALU.subtract, ALU.mult))
                st.then(dve.tensor_tensor(f.act_piece(q), gv, uv, ALU.mult))
                dve.tensor_reduce(f.peak[:, 0, bass.ds(q, 1)], f.act_piece(q), XY, ALU.max,
                                  apply_absolute_value=True).then_inc(peaked, 1)
            st.then(dve.memset(magic[:, :], MAGIC))
            over_pairs(dve, body, [st])
            dve.wait_ge(peaked, QUADS)
            scale_dve(dve, st, f, [H_OUT], peak_ready, top_ready)


def down(nc, a, g):
    f = g.f
    with ExitStack() as stack:
        m = Memory(nc, stack, "down")
        shifted, rounded, made, added, dve_st = (m.sem(n) for n in ("shifted", "rounded", "made", "added", "dve_st"))
        ot = m.sb("ot", (P, 2, IC, QN))
        magic = m.sb("magic", (P, 1))
        bank = [m.ps(f"o{i}") for i in range(2)]
        block = stack.enter_context(nc.Block())

        @block.scalar
        def _(act):
            def body(j, u):
                q = 2 * j + u
                wait(act, made, q - 1)
                act.activation(ot[:, u, :, :], f.act_piece(q), ACT.Identity, scale=f.inv[:, H_OUT:H_OUT + 1],
                               bias=magic[:, 0:1]).then_inc(shifted, 1)
            act.wait_ge(dve_st, 1)
            over_pairs(act, body)

        @block.tensor
        def _(pe):
            def body(j, u):
                q = 2 * j + u
                pe.wait_ge(rounded, q + 1)
                wait(pe, added, q - 1)
                for t in range(QT):
                    for c in range(IC):
                        last = pe.matmul(bank[u][:, t * P:t * P + P], ot[:, u, c, t * P:t * P + P], g.down_t[:, c, :],
                                         start=(c == 0), stop=(c == IC - 1))
                last.then_inc(made, 1)
            over_pairs(pe, body)

        @block.vector
        def _(dve):
            st = Steps(dve, dve_st)

            def grid(j, u):
                q = 2 * j + u
                dve.wait_ge(shifted, q + 1)
                dve.tensor_scalar(ot[:, u, :, :], ot[:, u, :, :], MAGIC, f.scale[:, H_OUT:H_OUT + 1],
                                  ALU.subtract, ALU.mult).then_inc(rounded, 1)

            def body(j, u):
                q = 2 * j + u
                if not (isinstance(q, int) and q == QUADS - 1):
                    grid(j + u, 1 - u)
                dve.wait_ge(made, q + 1)
                dve.tensor_tensor(g.xq(q), g.xq(q), bank[u][:, :], ALU.add).then_inc(added, 1)
            st.then(dve.memset(magic[:, :], MAGIC))
            grid(0, 0)
            over_pairs(dve, body)


class Half:
    PER = 4

    def __init__(self, j, k):
        self.j, self.k, self.u, self.par = j, k, k // 2, k % 2
        self.n, self.q = 4 * j + k, 2 * j + k // 2

    def shift(self, by):
        dj, k = divmod(self.k + by, self.PER)
        return Half(self.j + dj if dj else self.j, k)

    def outside(self):
        return isinstance(self.n, int) and not 0 <= self.n < 2 * QUADS


def over_halves(eng, body, lead=0, lag=0):
    for n in range(-lead, 0):
        body(Half(*divmod(n, Half.PER)))

    def quad(j, u):
        for par in range(2):
            body(Half(j, 2 * u + par))
    over_pairs(eng, quad)
    for n in range(2 * QUADS, 2 * QUADS + lag):
        body(Half(*divmod(n, Half.PER)))


class Mixer:

    def __init__(self, nc, stack):
        m = Memory(nc, stack, "mix")
        self.xc = m.sb("xc", (P, TILES, D))
        self.mv = m.sb("mv", (P, TILES, 2))


def attention1(nc, a, g):
    v = g.v
    scale = float(1 / np.sqrt(DH1).astype(np.float32))
    GROUPS = 8
    with ExitStack() as stack:
        m = Memory(nc, stack, "at1")
        ctx_in = [m.sem(f"ctx_in{u}") for u in range(2)]
        stats_ready, rstd_ready, h_ready, hn_ready = (
            m.sem(n) for n in ("stats_ready", "rstd_ready", "h_ready", "hn_ready"))
        ring_ready, ring_evac = m.sem("ring_ready"), m.sem("ring_evac")
        s_ready, s_evac, top_ready, bias_ready = (m.sem(n) for n in ("s_ready", "s_evac", "top_ready", "bias_ready"))
        e_ready, d_ready, inv_ready, prob_ready = (m.sem(n) for n in ("e_ready", "d_ready", "inv_ready", "prob_ready"))
        am_ready, am_evac, u_ready, u_evac = (m.sem(n) for n in ("am_ready", "am_evac", "u_ready", "u_evac"))
        film_ready, fin_done = m.sem("film_ready"), m.sem("fin_done")
        u_out = [m.sem(f"u_out{u}") for u in range(2)]
        pool_st, top_steps = m.sem("pool_st"), m.sem("top_steps")
        TOP_STEPS, FIRST_ROUND = 7, 2

        hq = m.sb("hq", (P, 2, QT, P))
        hn = m.sb("hn", (P, 2, QT, P))
        ht = m.sb("ht", (P, 2, QN))
        ctxn = m.sb("ctxn", (P, 2, QT, C))
        ctxt = m.sb("ctxt", (C + 2, 2, QN))
        qm = m.sb("qm", (C + 2, 2, 2 * QT, H1 * SEQ))
        stats = m.sb("stats", (P, 2, QT, 6))
        mv = m.sb("mv", (P, 2, QT, 2))
        r1 = m.sb("r1", (P, 2, QT, 1))
        again = m.sb("again", (P, 2, QT, 1))
        so = m.sb("so", (P, 2, GROUPS, SEQ))
        rest = m.sb("rest", (P, 2, GROUPS, SEQ))
        df = m.sb("df", (P, 2, GROUPS, SEQ))
        m8 = m.sb("m8", (P, 2, GROUPS, 4, 8))
        bias = m.sb("bias", (P, 2, GROUPS))
        minus_scale = m.sb("minus_scale", (P, GROUPS))
        sm = m.sb("sm", (P, 2, GROUPS))
        pr = m.sb("pr", (P, 2, GROUPS, SEQ))
        amb = m.sb("amb", (P, 2, 2, P))
        ut = m.sb("ut", (C + 1, 2, QN))
        xt = m.sb("xt", (P, 2, 2, D))
        ring = [m.ps(f"ring{i}") for i in range(2)]
        sps = [m.ps(f"s{i}") for i in range(2)]
        amp = m.ps("am")
        up_ = m.ps("u")
        fip = [m.ps(f"f{i}") for i in range(2)]
        block = stack.enter_context(nc.Block())
        RING = 6
        pieces = ((0, 1, 2), (3, 4, 5))
        POOL_CONSTS = 5
        ctx_src = a["ctx_768"].rearrange("b s c -> (b s) c").rearrange("(q t p) c -> q p t c", p=P, t=QT)
        mask_src = g.mask_rows.rearrange("m (q n) -> q m n", q=QUADS)

        @block.sync
        def _(sp):
            def load(j, u):
                q = 2 * j + u
                wait(sp, u_ready, 2 * (q - 1))
                sp.dma_start(ctxn[:, u, :, :], at_quad(ctx_src, q)).then_inc(ctx_in[u], 16)
                sp.dma_start(ctxt[C:C + 2, u, :], at_quad(mask_src, q)).then_inc(ctx_in[u], 16)
            over_pairs(sp, load)
            sp.wait_ge(u_out[0], 16 * QUADS // 2)
            sp.wait_ge(u_out[1], 16 * QUADS // 2)

        @block.tensor
        def _(pe):
            def front(x):
                if x.outside():
                    return
                for k in pieces[x.par]:
                    n = RING * x.q + k
                    slot = ring[k % 2]
                    if k == 0:
                        pe.wait_ge(h_ready, x.q + 1)
                    if k == 5:
                        pe.wait_ge(ctx_in[x.u], 32 * (x.j + 1))
                    wait(pe, ring_evac, n - 1 if k != 1 else n)
                    if k == 0:
                        for t in range(QT):
                            last = pe.transpose(slot[:, t * P:t * P + P], hq[:, x.u, t, :], g.ident[:, :])
                    elif k == 5:
                        for t in range(QT):
                            last = pe.transpose(slot[0:C, t * P:t * P + P], ctxn[:, x.u, t, :], g.ident[:, :])
                    else:
                        last = pe.matmul(slot[0:C, :], g.m1[:, k - 1, :], ht[:, x.u, :], start=True, stop=True)
                    last.then_inc(ring_ready, 1)

            def scores(x):
                if x.outside():
                    return
                wait(pe, ring_evac, RING * (x.q + 1))
                wait(pe, s_evac, x.n - 1)
                for i in range(2):
                    t = 2 * x.par + i
                    for b in range(2):
                        tok = slice(t * P + b * SEQ, t * P + b * SEQ + SEQ)
                        for p in range(2):
                            c0 = (4 * i + 2 * p + b) * SEQ
                            last = pe.matmul(sps[x.par][:, c0:c0 + SEQ], qm[:, x.u, 2 * t + b, p * P:p * P + P],
                                             ctxt[:, x.u, tok], start=True, stop=True)
                last.then_inc(s_ready, 1)

            def mean(x):
                if x.outside():
                    return
                pe.wait_ge(prob_ready, x.n + 1)
                wait(pe, am_evac, x.n)
                for i in range(2):
                    for p in range(2):
                        k = 4 * i + 2 * p
                        last = pe.matmul(amp[:, i * SEQ:i * SEQ + SEQ],
                                         pr[:, x.par, k:k + 2, :].rearrange("p a s -> p (a s)"),
                                         g.pairsum[:, :], start=(p == 0), stop=(p == 1))
                last.then_inc(am_ready, 1)

            def attend(x):
                if x.outside():
                    return
                pe.wait_ge(am_evac, x.n + 1)
                wait(pe, u_evac, x.n)
                for i in range(2):
                    last = pe.matmul(up_[0:C, i * P:i * P + P], ctxn[:, x.u, 2 * x.par + i, :], amb[:, x.par, i, :],
                                     start=True, stop=True)
                last.then_inc(u_ready, 1)

            def film(x):
                if x.outside():
                    return
                pe.wait_ge(u_evac, x.n + 1)
                wait(pe, fin_done, x.n - 1)
                for i in range(2):
                    t = 2 * x.par + i
                    last = pe.matmul(fip[x.par][:, 2 * D * i:2 * D * i + 2 * D], ut[:, x.u, t * P:t * P + P],
                                     g.film[:, 0:2 * D], start=True, stop=True)
                last.then_inc(film_ready, 1)

            def body(x):
                front(x.shift(2))
                scores(x.shift(1))
                mean(x.shift(-1))
                attend(x.shift(-1))
                film(x.shift(-1))
            pe.wait_ge(pool_st, POOL_CONSTS)
            over_halves(pe, body, lead=2, lag=1)

        @block.scalar
        def _(act):
            def front(x):
                if x.outside():
                    return
                for k in pieces[x.par]:
                    act.wait_ge(ring_ready, RING * x.q + k + 1)
                    slot = ring[k % 2]
                    if k == 0:
                        ins = act.copy(ht[:, x.u, :], slot[:, :])
                    elif k == 5:
                        ins = act.copy(ctxt[0:C, x.u, :], slot[0:C, :])
                    else:
                        ins = act.copy(qm[0:C, x.u, :, (k - 1) * SEQ:k * SEQ],
                                       slot[0:C, :].rearrange("c (b s) -> c b s", s=SEQ))
                    ins.then_inc(ring_evac, 1)

            def take(x):
                if x.outside():
                    return
                act.wait_ge(s_ready, x.n + 1)
                wait(act, d_ready, x.n - 1)
                act.copy(so[:, x.par, :, :], sps[x.par][:, :].rearrange("p (k s) -> p k s", s=SEQ)).then_inc(s_evac, 1)

            def exps(x, of, ready, value):
                if x.outside():
                    return
                act.wait_ge(bias_ready, x.n + 1)
                act.wait_ge(ready, value)
                for k in range(GROUPS):
                    ins = act.activation(of[:, x.par, k, :], of[:, x.par, k, :], ACT.Exp, scale=scale,
                                         bias=bias[:, x.par, k:k + 1])
                ins.then_inc(e_ready, 1)

            def attend(x):
                if x.outside():
                    return
                act.wait_ge(am_ready, x.n + 1)
                am = amp[:, 0:2 * SEQ].rearrange("p (i s) -> p i s", s=SEQ)
                act.copy(amb[0:SEQ, x.par, :, 0:SEQ], am[0:SEQ, :, :])
                act.copy(amb[SEQ:P, x.par, :, SEQ:P], am[SEQ:P, :, :]).then_inc(am_evac, 1)
                act.wait_ge(u_ready, x.n + 1)
                if x.par == 0:
                    wait(act, u_out[x.u], 16 * x.j)
                act.copy(ut[0:C, x.u, x.par * 2 * P:(x.par + 1) * 2 * P], up_[0:C, 0:2 * P]).then_inc(u_evac, 1)
                if x.par == 1:
                    act.wait_ge(u_evac, x.n + 1)
                    act.dma_start(g.u_t[:, bass.ds(x.q * QN, QN)], ut[:, x.u, :]).then_inc(u_out[x.u], 16)

            def body(x):
                front(x.shift(2))
                take(x.shift(1))
                exps(x, so, top_steps, TOP_STEPS * x.n + FIRST_ROUND)
                attend(x.shift(-1))
                exps(x, rest, top_ready, x.n + 1)
            over_halves(act, body, lead=2, lag=1)

        @block.gpsimd
        def _(pool):
            st = Steps(pool, pool_st)
            st.then(pool.memset(qm[C:C + 2, :, :, :], 1.0))
            st.then(pool.memset(qm[C:C + 1, :, :, :], 0.0))
            st.then(pool.memset(ut[C:C + 1, :, :], 1.0))
            st.then(pool.memset(amb[:, :, :, :], 0.0))
            st.then(pool.memset(minus_scale[:, :], -scale))
            assert st.n == POOL_CONSTS
            st_rstd, st_prob, st_hn = (Each(pool, m.sem(n), k) for n, k in (("st_rstd", 5), ("st_prob", 1), ("st_hn", 2)))

            def rstds(x):
                if x.outside() or x.par:
                    return
                eps, power = g.eps[:, 0:QT].unsqueeze(2), g.minus_half[:, 0:QT].unsqueeze(2)
                var, r = mv[:, x.u, :, 1:2], r1[:, x.u, :, :]
                pool.wait_ge(stats_ready, x.q + 1)
                link = st_rstd.at(x.q)
                link.then(pool.tensor_tensor(r, var, eps, ALU.add))
                pool.tensor_tensor(r, r, power, ALU.pow).then_inc(rstd_ready, 1)
                pool.wait_ge(rstd_ready, x.q + 1)
                link.then(pool.tensor_tensor(var, var, r, ALU.mult))
                link.then(pool.tensor_tensor(var, var, r, ALU.mult))
                link.then(pool.tensor_tensor(var, var, eps, ALU.add))
                link.then(pool.tensor_tensor(again[:, x.u, :, :], var, power, ALU.pow))

            def norm_in(x):
                if x.outside() or x.par:
                    return
                wait(pool, h_ready, x.q + 1)
                wait(pool, fin_done, 2 * (x.q - 1))
                n = hn[:, x.u, :, :]
                link = st_hn.at(x.q)
                link.then(pool.tensor_tensor(n, hq[:, x.u, :, :], again[:, x.u, :, :].to_broadcast([P, QT, D]), ALU.mult))
                link.then(pool.tensor_tensor(n, n, g.wide[:, 0:1, :].to_broadcast([P, QT, D]), ALU.mult))
                pool.tensor_tensor(n, n, g.wide[:, 1:2, :].to_broadcast([P, QT, D]), ALU.add).then_inc(hn_ready, 1)

            def biases(x):
                if x.outside():
                    return
                pool.wait_ge(top_steps, TOP_STEPS * x.n + FIRST_ROUND)
                pool.tensor_tensor(bias[:, x.par, :], m8[:, x.par, :, 0, 0:1].rearrange("p a b -> p (a b)"),
                                   minus_scale[:, :], ALU.mult).then_inc(bias_ready, 1)

            def probs(x):
                if x.outside():
                    return
                pool.wait_ge(inv_ready, x.n + 1)
                s = sm[:, x.par, :].rearrange("p (i a b) -> p i a b", a=2, b=2)
                tm = g.tmask[:, bass.ds(4 * x.n, 4)].rearrange("p (i b) -> p i b", b=2).unsqueeze(2)
                st_prob.at(x.n).then(pool.tensor_tensor(s, s, tm.to_broadcast([P, 2, 2, 2]), ALU.mult))
                wait(pool, am_ready, x.n - 1)
                pool.tensor_tensor(pr[:, x.par, :, :], df[:, x.par, :, :],
                                   sm[:, x.par, :].unsqueeze(2).to_broadcast([P, GROUPS, SEQ]), ALU.mult).then_inc(prob_ready, 1)

            def differences(x):
                if x.outside():
                    return
                pool.wait_ge(e_ready, 2 * x.n + 2)
                pool.tensor_tensor(df[:, x.par, :, :], so[:, x.par, :, :], rest[:, x.par, :, :],
                                   ALU.subtract).then_inc(d_ready, 1)

            def body(x):
                biases(x)
                rstds(x.shift(3))
                norm_in(x)
                probs(x.shift(-1))
                differences(x)
            over_halves(pool, body, lead=3, lag=1)

        @block.vector
        def _(dve):
            st_top = Each(dve, top_steps, TOP_STEPS)
            st_stat, st_sum, st_fin = (
                Each(dve, m.sem(n), k) for n, k in (("st_stat", 1), ("st_sum", 1), ("st_fin", 1)))

            def carry(cell):
                dve.memset(g.carry[:, cell:cell + 1], 0.0)

            def stats_of(x):
                if x.outside() or x.par:
                    return
                for t in range(QT):
                    last = dve.bn_stats(stats[:, x.u, t, :], g.xt(x.q, t))
                st_stat.at(x.q).done(last)

            def means_of(x):
                if x.outside() or x.par:
                    return
                wait(dve, hn_ready, x.q - 1)
                dve.wait_ge(st_stat.sem, x.q + 1)
                carry(2)
                for t in range(QT):
                    last = dve.bn_aggr(mv[:, x.u, t, :], stats[:, x.u, t, :])
                last.then_inc(stats_ready, 1)

            def norm(x):
                if x.outside() or x.par:
                    return
                wait(dve, ring_ready, RING * (x.q - 2) + 1)
                dve.wait_ge(rstd_ready, x.q + 1)
                for t in range(QT):
                    last = dve.tensor_scalar(hq[:, x.u, t, :], g.xt(x.q, t), mv[:, x.u, t, 0:1], r1[:, x.u, t, :],
                                             ALU.subtract, ALU.mult)
                last.then_inc(h_ready, 1)
                dve.tensor_copy(v.mv[:, bass.ds(QT * x.q, QT), 0:1], mv[:, x.u, :, 0:1])
                dve.tensor_copy(v.mv[:, bass.ds(QT * x.q, QT), 1:2], r1[:, x.u, :, :])

            def total(x):
                if x.outside():
                    return
                dve.wait_ge(d_ready, x.n + 1)
                st_sum.at(x.n).done(dve.tensor_reduce(sm[:, x.par, :], df[:, x.par, :, :], X, ALU.add))

            def inverse(x):
                if x.outside():
                    return
                dve.wait_ge(st_sum.sem, x.n + 1)
                dve.reciprocal(sm[:, x.par, :], sm[:, x.par, :]).then_inc(inv_ready, 1)

            def out_scale(x):
                if x.outside():
                    return
                dve.wait_ge(hn_ready, x.q + 1)
                dve.wait_ge(film_ready, x.n + 1)
                fi = fip[x.par][:, :].rearrange("p (i c d) -> p i c d", i=2, c=2)
                st_fin.at(x.n).done(dve.tensor_tensor(xt[:, x.par, :, :], fi[:, :, 0, :],
                                                      hn[:, x.u, 2 * x.par:2 * x.par + 2, :], ALU.mult))

            def out_shift(x):
                if x.outside():
                    return
                dve.wait_ge(st_fin.sem, x.n + 1)
                fi = fip[x.par][:, :].rearrange("p (i c d) -> p i c d", i=2, c=2)
                dve.tensor_tensor(v.xc[:, bass.ds(2 * x.n, 2), :], fi[:, :, 1, :], xt[:, x.par, :, :],
                                  ALU.add).then_inc(fin_done, 1)

            def body(x):
                fill = ((stats_of, 3), (means_of, 3), (total, -1), (inverse, -1),
                        (out_scale, -2), (out_shift, -2), (norm, 3))
                if x.outside():
                    for step, by in fill:
                        step(x.shift(by))
                    return
                wait(dve, d_ready, x.n - 1)
                dve.wait_ge(s_evac, x.n + 1)
                carry(0)
                link = st_top.at(x.n)
                for i in range(8):
                    r = i // 2
                    src = so if r == 0 else rest
                    for k in range(GROUPS):
                        if i % 2 == 0:
                            last = dve.max(m8[:, x.par, k, r, :], src[:, x.par, k, :])
                        else:
                            last = dve.match_replace(rest[:, x.par, k, :], m8[:, x.par, k, r, :], src[:, x.par, k, :], -3.0e38)
                    if i < 7:
                        link.done(last)
                        step, by = fill[i]
                        step(x.shift(by))
                        dve.wait_ge(link.sem, link.now())
                        carry(1)
                last.then_inc(top_ready, 1)
            over_halves(dve, body, lead=3, lag=2)


def at_quad(src, q):
    if isinstance(q, int):
        return src[q]
    s = src[bass.ds(q, 1)]
    return s.rearrange("a p t c -> (a p) t c") if len(s.shape) == 4 else s.rearrange("a m n -> (a m) n")


def filter_tokens(nc, a, g):
    v = g.v
    GR = 8
    with ExitStack() as stack:
        m = Memory(nc, stack, "fil")
        t_in = [m.sem(f"t_in{u}") for u in range(2)]
        made, moved, zeroed = m.sem("made"), m.sem("moved"), m.sem("zeroed")
        tb = m.sb("tb", (P, 2, GR, P))
        bank = [m.ps(f"y{i}") for i in range(2)]
        block = stack.enter_context(nc.Block())
        groups = D // GR

        @block.gpsimd
        def _(pool):
            pool.memset(tb[:, :, :, :], 0.0).then_inc(zeroed, 1)

        @block.sync
        def _(sp):
            sp.wait_ge(g.taps_stored, 16)
            sp.wait_ge(zeroed, 1)

            def load(j, u):
                i = 2 * j + u
                wait(sp, made, i - 1)
                for b in range(2):
                    sp.dma_start(tb[b * SEQ:b * SEQ + SEQ, u, :, b * SEQ:b * SEQ + SEQ],
                                 g.toeplitz[:, bass.ds(i * GR, GR), :]).then_inc(t_in[u], 16)
            over_pairs(sp, load, pairs=groups // 2)

        @block.tensor
        def _(pe):
            def body(j, u):
                i = 2 * j + u
                pe.wait_ge(t_in[u], 32 * (j + 1))
                wait(pe, moved, i - 1)
                for k in range(GR):
                    last = pe.matmul(bank[u][:, k * TILES:k * TILES + TILES], tb[:, u, k, :],
                                     v.xc[:, :, bass.ds(i * GR + k, 1)].rearrange("p t a -> p (t a)"),
                                     start=True, stop=True)
                last.then_inc(made, 1)
            over_pairs(pe, body, pairs=groups // 2)

        @block.scalar
        def _(act):
            def body(j, u):
                i = 2 * j + u
                act.wait_ge(made, i + 1)
                act.copy(v.xc[:, :, bass.ds(i * GR, GR)].rearrange("p t c -> p c t"),
                         bank[u][:, :].rearrange("p (c t) -> p c t", t=TILES)).then_inc(moved, 1)
            over_pairs(act, body, pairs=groups // 2)


def mix(nc, a, g):
    v = g.v
    with ExitStack() as stack:
        m = Memory(nc, stack, "mx")
        u_in = [m.sem(f"u_in{u}") for u in range(2)]
        out_done = m.sem("out_done")
        film_ready, film_used, stats_ready, rstd_ready, n_ready, turned, turn_evac = (
            m.sem(n) for n in ("film_ready", "film_used", "stats_ready", "rstd_ready", "n_ready", "turned", "turn_evac"))
        hid_ready, hid_done, back_ready, back_used, resid_ready, last_ready, x_ready = (
            m.sem(n) for n in ("hid_ready", "hid_done", "back_ready", "back_used", "resid_ready", "last_ready", "x_ready"))
        ut = m.sb("ut", (C + 1, 2, QN))
        mvs = m.sb("mvs", (P, 2, QT, 2))
        hq = m.sb("hq", (P, QT, D))
        yq = m.sb("yq", (P, QT, D))
        xq = m.sb("xq", (P, 2, QT, D))
        xb = m.sb("xb", (P, 2, QT, D))
        nq = m.sb("nq", (P, 2, QT, D))
        lq = m.sb("lq", (P, 2, QT, D))
        nt = m.sb("nt", (P, 2, QN))
        hid = m.sb("hid", (P, 2, 4, QN))
        stats = m.sb("stats", (P, 2, QT, 6))
        stats2 = m.sb("stats2", (P, 2, QT, 6))
        mv = m.sb("mv", (P, 2, QT, 2))
        mv2 = m.sb("mv2", (P, 2, QT, 2))
        fop = m.ps("fo", (P, 2, 512))
        tp = m.ps("t")
        hp = [m.ps(f"h{i}") for i in range(4)]
        bp = m.ps("b")
        block = stack.enter_context(nc.Block())
        out = g.out.rearrange("b s d -> (b s) d").rearrange("(q t p) d -> q p t d", p=P, t=QT)

        def last_quad(q):
            return isinstance(q, int) and q == QUADS - 1

        def norm_count(q):
            return 0 if isinstance(q, int) and q == 0 else 2 * q - 1

        def last_count(q):
            return 2 * q + 1 if last_quad(q) else 2 * q + 2

        @block.sync
        def _(sp):
            def load(j, u):
                q = 2 * j + u
                wait(sp, film_ready, q - 1)
                sp.dma_start(ut[:, u, :], g.u_t[:, bass.ds(q * QN, QN)]).then_inc(u_in[u], 16)
                if not (isinstance(q, int) and q < 2):
                    store(q - 2)

            def store(q):
                sp.wait_ge(x_ready, q + 1)
                sp.dma_start(at_quad(out, q), g.xq(q).rearrange("p (t d) -> p t d", d=D)).then_inc(out_done, 16)
            over_pairs(sp, load)
            for q in range(QUADS - 2, QUADS):
                store(q)
            sp.wait_ge(out_done, 16 * QUADS)

        @block.tensor
        def _(pe):
            def film(j, u):
                q = 2 * j + u
                pe.wait_ge(u_in[u], 16 * (j + 1))
                wait(pe, film_used, q)
                for t in range(QT):
                    last = pe.matmul(fop[:, t // 2, 256 * (t % 2):256 * (t % 2) + 256], ut[:, u, t * P:t * P + P],
                                     g.film[:, 2 * D:], start=True, stop=True)
                last.then_inc(film_ready, 1)

            def back(q, u):
                wait(pe, back_used, q)
                pe.wait_ge(hid_done, 4 * (q + 1))
                for t in range(QT):
                    for c in range(4):
                        last = pe.matmul(bp[:, t * P:t * P + P], hid[:, u, c, t * P:t * P + P], g.w2[:, c, :],
                                         start=(c == 0), stop=(c == 3))
                last.then_inc(back_ready, 1)

            def body(j, u):
                q = 2 * j + u
                if not last_quad(q):
                    film(j + u, 1 - u)
                if not (isinstance(q, int) and q == 0):
                    back(q - 1, 1 - u)
                pe.wait_ge(n_ready, q + 1)
                wait(pe, turn_evac, q)
                for t in range(QT):
                    last = pe.transpose(tp[:, t * P:t * P + P], nq[:, u, t, :], g.ident[:, :])
                last.then_inc(turned, 1)
                pe.wait_ge(turn_evac, q + 1)
                for c in range(4):
                    wait(pe, hid_done, 4 * (q - 1) + c + 1)
                    pe.matmul(hp[c][:, :], g.w1[:, c * P:c * P + P], nt[:, u, :], start=True, stop=True).then_inc(hid_ready, 1)
            film(0, 0)
            over_pairs(pe, body)
            back(QUADS - 1, 1)

        @block.scalar
        def _(act):
            def body(j, u):
                q = 2 * j + u
                act.wait_ge(turned, q + 1)
                act.activation(nt[:, u, :], tp[:, :], ACT.Identity, scale=g.ffn_g[:, 0:1],
                               bias=g.ffn_b[:, 0:1]).then_inc(turn_evac, 1)
                wait(act, back_ready, q - 1)
                for c in range(4):
                    act.wait_ge(hid_ready, 4 * q + c + 1)
                    act.activation(hid[:, u, c, :], hp[c][:, :], ACT.Gelu, bias=g.b1[:, c:c + 1]).then_inc(hid_done, 1)
            over_pairs(act, body)

        @block.gpsimd
        def _(pool):
            st_first, st_last = Each(pool, m.sem("pool_first"), 1), Each(pool, m.sem("pool_last"), 3)

            def finish(j, u):
                q = 2 * j + u
                st = st_last.at(q)
                rstd_steps(pool, g, mv2[:, u, :, :], stats_ready, rstd_ready, st, last_count(q))
                pool.wait_ge(last_ready, q + 1)
                n = lq[:, u, :, :]
                st.then(pool.tensor_tensor(n, n, g.wide[:, 3:4, :].to_broadcast([P, QT, D]), ALU.mult))
                xs = g.xq(q).rearrange("p (t d) -> p t d", d=D)
                st.then(pool.tensor_tensor(n, n, g.wide[:, 4:5, :].to_broadcast([P, QT, D]), ALU.add))
                pool.tensor_tensor(xs, xs, n, ALU.add).then_inc(x_ready, 1)

            def body(j, u):
                q = 2 * j + u
                rstd_steps(pool, g, mv[:, u, :, :], stats_ready, rstd_ready, st_first.at(q), norm_count(q))
                pool.tensor_tensor(xb[:, u, :, :], xq[:, u, :, :], g.wide[:, 2:3, :].to_broadcast([P, QT, D]),
                                   ALU.add).then_inc(resid_ready, 1)
                if not (isinstance(q, int) and q == 0):
                    finish(j + u - 1, 1 - u)
            over_pairs(pool, body)
            finish(QUADS // 2 - 1, 1)


        @block.vector
        def _(dve):
            st_first, st_last = Each(dve, m.sem("dve_first"), 4), Each(dve, m.sem("dve_last"), 1)

            def first(j, u):
                q = 2 * j + u
                st = st_first.at(q)
                st.then(dve.tensor_copy(mvs[:, u, :, :], v.mv[:, bass.ds(QT * q, QT), :]))
                for t in range(QT):
                    dve.tensor_scalar(hq[:, t, :], g.xt(q, t), mvs[:, u, t, 0:1], mvs[:, u, t, 1:2],
                                      ALU.subtract, ALU.mult)
                dve.wait_ge(film_ready, q + 1)
                fo = fop[:, :, :].rearrange("p a (b n) -> p (a b) n", n=2 * D)
                y = v.xc[:, bass.ds(QT * q, QT), :]
                st.then(dve.tensor_tensor(yq[:, :, :], fo[:, :, 0:D], y, ALU.mult))
                ins = dve.tensor_tensor(yq[:, :, :], fo[:, :, D:2 * D], yq[:, :, :], ALU.add)
                ins.then_inc(film_used, 1)
                dve.wait_ge(film_used, q + 1)
                wait(dve, resid_ready, q - 1)
                st.then(dve.tensor_tensor(xq[:, u, :, :], yq[:, :, :], hq[:, :, :], ALU.add))
                wait(dve, turned, q - 1)
                norm_steps(dve, g.carry, rstd_ready, st, [xq[:, u, t, :] for t in range(QT)], stats[:, u, :, :],
                           mv[:, u, :, :], [nq[:, u, t, :] for t in range(QT)], stats_ready,
                           norm_count(q)).then_inc(n_ready, 1)

            def second(j, u):
                q = 2 * j + u
                st = st_last.at(q)
                dve.wait_ge(back_ready, q + 1)
                dve.wait_ge(resid_ready, q + 1)
                b = xb[:, u, :, :]
                dve.tensor_tensor(b, bp[:, :].rearrange("p (t d) -> p t d", d=D), b, ALU.add).then_inc(back_used, 1)
                dve.wait_ge(back_used, q + 1)
                wait(dve, x_ready, q - 1)
                norm_steps(dve, g.carry, rstd_ready, st, [xb[:, u, t, :] for t in range(QT)], stats2[:, u, :, :],
                           mv2[:, u, :, :], [lq[:, u, t, :] for t in range(QT)], stats_ready,
                           last_count(q)).then_inc(last_ready, 1)

            def body(j, u):
                q = 2 * j + u
                first(j, u)
                if not (isinstance(q, int) and q == 0):
                    second(j + u - 1, 1 - u)
            over_pairs(dve, body)
            second(QUADS // 2 - 1, 1)


def experts(nc, a, g):
    n_tok = a["L1_ffn_router_indices"].shape[0]
    NT = n_tok // P
    with ExitStack() as stack:
        m = Memory(nc, stack, "ex")
        loaded, stats_ready, rstd_ready, xn_ready, dve_st, pool_st, act_st, pe_st, out_done = (
            m.sem(n) for n in ("loaded", "stats_ready", "rstd_ready", "xn_ready", "dve_st", "pool_st", "act_st", "pe_st", "out_done"))
        gu_ready, limited, sig_ready, inter_ready, down_ready, summed = (
            m.sem(n) for n in ("gu_ready", "limited", "sig_ready", "inter_ready", "down_ready", "summed"))
        wgu = m.sb("wgu", (P, EXPERTS, 2 * D))
        wd = m.sb("wd", (P, EXPERTS, D))
        bgu = m.sb("bgu", (P, EXPERTS, 2))
        bd = m.sb("bd", (EXPERTS, D))
        route = m.sb("route", (P, NT, 2), I32)
        routef = m.sb("routef", (P, NT, 2))
        weight = m.sb("weight", (P, NT, EXPERTS))
        iota = m.sb("iota", (P, EXPERTS))
        hit = m.sb("hit", (P, NT, 2, EXPERTS))
        coef = m.sb("coef", (P, NT, EXPERTS))
        coeft = m.sb("coeft", (EXPERTS, NT, P))
        xn = m.sb("xn", (P, NT, D))
        xnt = m.sb("xnt", (P, NT * P))
        stats = m.sb("stats", (P, NT, 6))
        mv = m.sb("mv", (P, NT, 2))
        gu = m.sb("gu", (P, 2, 2, NT * P))
        sg = m.sb("sg", (P, 2, NT * P))
        inter = m.sb("inter", (P, 2, NT * P))
        tp, cp = m.ps("t"), m.ps("c")
        gp = [m.ps(f"g{i}") for i in range(2)]
        dp = [m.ps(f"d{i}") for i in range(2)]
        bp = m.ps("b")
        block = stack.enter_context(nc.Block())
        LOADS = 6
        COEF_AT = 4

        @block.sync
        def _(sp):
            with nc.allow_non_contiguous_dma(reason="small biases, turned"):
                for dst, src in (
                    (wgu[:, :, :], a["L1_ffn_gate_up_proj"].rearrange("e h n -> h e n")),
                    (wd[:, :, :], a["L1_ffn_down_proj"].rearrange("e h n -> h e n")),
                    (bgu[:, :, :], a["L1_ffn_gate_up_proj_bias"].rearrange("e (i k) -> i e k", k=2)),
                    (bd[:, :], a["L1_ffn_down_proj_bias"]),
                    (route[:, :, :], a["L1_ffn_router_indices"].rearrange("(t p) k -> p t k", p=P)),
                    (weight[:, :, :], a["L1_ffn_routing_weights"].rearrange("(t p) e -> p t e", p=P)),
                ):
                    sp.dma_start(dst, src).then_inc(loaded, 16)
            sp.wait_ge(summed, NT * EXPERTS + NT)
            sp.dma_start(g.out.rearrange("b s d -> (b s) d").rearrange("(t p) d -> p t d", p=P)[:, 0:NT, :],
                         g.x[:, 0:NT, :]).then_inc(out_done, 16)
            sp.wait_ge(out_done, 16)

        @block.gpsimd
        def _(pool):
            st = Steps(pool, pool_st)
            for e in range(EXPERTS):
                st.then(pool.memset(iota[:, e:e + 1], float(e)))
            pool.wait_ge(stats_ready, 1)
            st.then(pool.tensor_tensor(mv[:, :, 1:2], mv[:, :, 1:2], g.eps[:, 0:NT].unsqueeze(2), ALU.add))
            pool.tensor_tensor(mv[:, :, 1:2], mv[:, :, 1:2], g.minus_half[:, 0:NT].unsqueeze(2), ALU.pow).then_inc(rstd_ready, 1)

        @block.tensor
        def _(pe):
            pe.wait_ge(xn_ready, NT)
            for t in range(NT):
                last = pe.transpose(tp[:, t * P:t * P + P], xn[:, t, :], g.ident[:, :])
            last.then_inc(pe_st, 1)
            pe.wait_ge(dve_st, COEF_AT)
            for t in range(NT):
                last = pe.transpose(cp[0:EXPERTS, t * P:t * P + P], coef[:, t, :], g.ident[:, :])
            last.then_inc(pe_st, 1)
            pe.wait_ge(loaded, 16 * LOADS)

            def into(e):
                wait(pe, limited, 2 * (e - 1))
                w = wgu[:, e, :].rearrange("p (i k) -> p i k", k=2)
                for k in range(2):
                    last = pe.matmul(gp[e % 2][:, k * NT * P:(k + 1) * NT * P], w[:, :, k], xnt[:, :], start=True, stop=True)
                last.then_inc(gu_ready, 1)

            def outof(e):
                pe.wait_ge(inter_ready, e + 1)
                wait(pe, summed, NT * (e - 1) + NT)
                for t in range(NT):
                    last = pe.matmul(dp[e % 2][:, t * P:t * P + P], inter[:, e % 2, t * P:t * P + P], wd[:, e, :],
                                     start=True, stop=True)
                last.then_inc(down_ready, 1)
            pe.wait_ge(act_st, 2)
            for t in range(NT):
                last = pe.matmul(bp[:, t * P:t * P + P], coeft[:, t, :], bd[:, :], start=True, stop=True)
            last.then_inc(pe_st, 1)
            into(0)
            for e in range(EXPERTS):
                if e + 1 < EXPERTS:
                    into(e + 1)
                outof(e)

        @block.scalar
        def _(act):
            st = Steps(act, act_st)
            act.wait_ge(pe_st, 1)
            st.then(act.copy(xnt[:, :], tp[:, 0:NT * P]))
            act.wait_ge(pe_st, 2)
            st.then(act.copy(coeft[:, :, :], cp[0:EXPERTS, 0:NT * P].rearrange("p (t n) -> p t n", n=P)))
            for e in range(EXPERTS):
                act.wait_ge(limited, 2 * e + 1)
                wait(act, inter_ready, e - 1)
                act.activation(sg[:, e % 2, :], gu[:, e % 2, 0, :], ACT.Sigmoid, scale=1.702).then_inc(sig_ready, 1)

        @block.vector
        def _(dve):
            st = Steps(dve, dve_st)
            dve.wait_ge(loaded, 16 * LOADS)
            dve.wait_ge(pool_st, EXPERTS)
            st.then(dve.tensor_copy(routef[:, :, :], route[:, :, :]))
            for t in range(NT):
                for k in range(2):
                    last = dve.tensor_scalar(hit[:, t, k, :], iota[:, :], routef[:, t, k:k + 1], None, ALU.is_equal)
            st.then(last)
            st.then(dve.tensor_tensor(hit[:, :, 0, :], hit[:, :, 0, :], hit[:, :, 1, :], ALU.add))
            st.then(dve.tensor_tensor(coef[:, :, :], hit[:, :, 0, :], weight[:, :, :], ALU.mult))
            for t in range(NT):
                last = dve.bn_stats(stats[:, t, :], g.x[:, t, :])
            st.then(last)
            assert st.n == COEF_AT + 1
            for t in range(NT):
                last = dve.bn_aggr(mv[:, t, :], stats[:, t, :])
            last.then_inc(stats_ready, 1)
            dve.wait_ge(rstd_ready, 1)
            for t in range(NT):
                dve.tensor_scalar(xn[:, t, :], g.x[:, t, :], mv[:, t, 0:1], mv[:, t, 1:2],
                                  ALU.subtract, ALU.mult).then_inc(xn_ready, 1)
            dve.wait_ge(pe_st, 3)
            dve.wait_ge(xn_ready, NT)
            for t in range(NT):
                dve.tensor_tensor(g.x[:, t, :], g.x[:, t, :], bp[:, t * P:t * P + P], ALU.add).then_inc(summed, 1)

            def limit(e):
                dve.wait_ge(gu_ready, e + 1)
                gv, uv = gu[:, e % 2, 0, :], gu[:, e % 2, 1, :]
                dve.tensor_scalar(gv, gp[e % 2][:, 0:NT * P], bgu[:, e, 0:1], 7.0, ALU.add, ALU.min).then_inc(limited, 1)
                dve.tensor_scalar(uv, gp[e % 2][:, NT * P:], bgu[:, e, 1:2], 7.0, ALU.add, ALU.min).then_inc(limited, 1)
                dve.wait_ge(limited, 2 * e + 2)
                st.then(dve.tensor_scalar(uv, uv, -7.0, 1.0, ALU.max, ALU.add))
                st.then(dve.tensor_tensor(uv, uv, gv, ALU.mult))
                dve.wait_ge(sig_ready, e + 1)
                wait(dve, down_ready, e - 1)
                dve.tensor_tensor(inter[:, e % 2, :], uv, sg[:, e % 2, :], ALU.mult).then_inc(inter_ready, 1)

            def join(e):
                dve.wait_ge(down_ready, e + 1)
                dve.wait_ge(summed, NT * (e + 1))
                for t in range(NT):
                    dve.scalar_tensor_tensor(out=g.x[:, t, :], in0=dp[e % 2][:, t * P:t * P + P],
                                             scalar=coef[:, t, e:e + 1], in1=g.x[:, t, :],
                                             op0=ALU.mult, op1=ALU.add).then_inc(summed, 1)
            for e in range(EXPERTS):
                limit(e)
                if e > 0:
                    join(e - 1)
            join(EXPERTS - 1)


class Resident:

    def __init__(self, nc, stack):
        m = Memory(nc, stack, "g")
        self.x = m.sb("x", (P, TILES, P))
        self.ident = m.sb("ident", (P, P))
        self.pairsum = m.sb("pairsum", (P, SEQ))
        self.minus_half = m.sb("minus_half", (P, 8))
        self.carry = m.sb("carry", (P, 4))
        self.eps = m.sb("eps", (P, 8))
        self.m0 = m.sb("m0", (P, H0, C))
        self.n0 = m.sb("n0", (C + 1, H0, D))
        self.m1 = m.sb("m1", (P, H1, C))
        self.film = m.sb("film", (C + 1, 4 * D))
        self.gate_t = m.sb("gate_t", (P, INTER))
        self.up_t = m.sb("up_t", (P, INTER))
        self.down_t = m.sb("down_t", (P, IC, D))
        self.w1 = m.sb("w1", (P, HID))
        self.w2 = m.sb("w2", (P, 4, D))
        self.b1 = m.sb("b1", (P, 4))
        self.ffn_g = m.sb("ffn_g", (P, 1))
        self.ffn_b = m.sb("ffn_b", (P, 1))
        self.wide = m.sb("wide", (P, 5, D))
        self.tmask = m.sb("tmask", (P, BATCH))
        self.mask_rows = nc.dram_tensor("mask_rows", [2, TOK], F32, kind="Internal").ap()
        self.taps_sb = m.sb("taps_sb", (P, 2 * SEQ))
        self.taps_stored = m.sem("taps_stored")
        SKEW = SEQ * (2 * SEQ + 1)
        skewed = nc.dram_tensor("skewed_taps", [D, SKEW], F32, kind="Internal").ap()
        self.taps_out = skewed.rearrange("d (j m) -> d j m", j=SEQ)[:, :, 0:2 * SEQ]
        self.toeplitz = bass.AP(skewed.tensor, SEQ, [[2 * SEQ, SEQ], [SKEW, D], [1, SEQ]])
        self.u_t = nc.dram_tensor("u_t", [C + 1, TOK], F32, kind="Internal").ap()

    def xt(self, q, t):
        flat = self.x[:, :, :].rearrange("p t d -> p (t d)")
        return flat[:, bass.ds(q * QN + t * P, P)] if not isinstance(q, int) else flat[:, q * QN + t * P:q * QN + t * P + P]

    def xq(self, q):
        flat = self.x[:, :, :].rearrange("p t d -> p (t d)")
        return flat[:, bass.ds(q * QN, QN)] if not isinstance(q, int) else flat[:, q * QN:q * QN + QN]


FFN = [act_quant, gate_up_max, gate, up, down]
ATTENTION1 = [attention1, filter_tokens, mix]


def program(nc, a, out, stages=None):
    with ExitStack() as stack:
        g = Resident(nc, stack)
        g.out = out

        def run(some):
            for stage in some:
                if stages is None or stage in stages:
                    stage(nc, a, g)
        run([prepare, attention0])
        with ExitStack() as ffn:
            g.f = Quantised(nc, ffn)
            run(FFN)
        with ExitStack() as second:
            g.v = Mixer(nc, second)
            run(ATTENTION1)
        run([experts])
        if stages and mix not in stages and experts not in stages:
            dump(nc, a, g, out)


def dump(nc, a, g, out):
    with ExitStack() as stack:
        m = Memory(nc, stack, "dump")
        done = m.sem("done")
        block = stack.enter_context(nc.Block())

        @block.sync
        def _(sp):
            sp.dma_start(out.rearrange("b s d -> (b s) d").rearrange("(t p) d -> p t d", p=P), g.x[:, :, :]).then_inc(done, 16)
            sp.wait_ge(done, 16)


_NAMES = [
    "x", "ctx_768", "mask_BxS2_bk0", "mask_BxS_bf1", "mask_BxS2_bf1",
    "L0_xattn_W_q", "L0_xattn_W_k", "L0_xattn_W_v", "L0_xattn_W_o", "L0_xattn_b_o",
    "L0_ffn_w_gate", "L0_ffn_w_up", "L0_ffn_w_down",
    "L1_xattn_Wq", "L1_xattn_Wk", "L1_xattn_Wv", "L1_xattn_W_film_in", "L1_xattn_b_film_in",
    "L1_xattn_W_film_out", "L1_xattn_b_film_out", "L1_xattn_g_norm_in", "L1_xattn_b_norm_in",
    "L1_xattn_g_norm_out", "L1_xattn_b_norm_out", "L1_xattn_g_ffn", "L1_xattn_b_ffn",
    "L1_xattn_W1", "L1_xattn_b1", "L1_xattn_W2", "L1_xattn_b2", "L1_xattn_log_dt",
    "L1_xattn_A_re", "L1_xattn_A_im", "L1_xattn_C_re", "L1_xattn_C_im", "L1_xattn_D_skip",
    "L1_xattn_mod_gate", "L1_ffn_router_indices", "L1_ffn_routing_weights",
    "L1_ffn_gate_up_proj", "L1_ffn_gate_up_proj_bias", "L1_ffn_down_proj", "L1_ffn_down_proj_bias",
]


def kernel(**inputs):
    import concourse.bacc as bacc
    from concourse.bass_utils import run_bass_kernel_spmd

    nc = bacc.Bacc("TRN2", target_bir_lowering=False, num_devices=1)
    arrays, args = {}, {}
    for name in _NAMES:
        v = np.ascontiguousarray(inputs[name])
        if v.ndim == 0:
            v = v.reshape(1)
        arrays[f"in_{name}"] = v
        args[name] = nc.dram_tensor(f"in_{name}", v.shape, mybir.dt.from_np(v.dtype), kind="ExternalInput").ap()
    out = nc.dram_tensor("out", (BATCH, SEQ, D), F32, kind="ExternalOutput").ap()
    program(nc, args, out)
    return run_bass_kernel_spmd(nc, [arrays], core_ids=[0]).results[0]["out"]
```

```python
from contextlib import ExitStack

import numpy as np

import concourse.bass as bass
from concourse import mybir

F32 = mybir.dt.float32
I32 = mybir.dt.int32
U8 = mybir.dt.uint8
ALU = mybir.AluOpType
ACT = mybir.ActivationFunctionType
X = mybir.AxisListType.X
XY = mybir.AxisListType.XY
RMAX = bass.bass_isa.ReduceOp.max

P = 128
SEQ = 64
BATCH = 128
D = 128
C = 96
TOK = BATCH * SEQ
TILES = TOK // P
QT = 4
QUADS = TILES // QT
QN = QT * P
H0, H1 = 8, 4
DH0, DH1 = 64, 32
INTER = 384
IC = INTER // P
HID = 512
NS = 64
EXPERTS = 8
EPS = 1e-5
MAGIC = 12582912.0
FAR = 2.0 ** 100
QMAX = 32767.0
TWO_PI = 2 * np.pi


class Steps:

    def __init__(self, eng, sem):
        self.eng, self.sem, self.base, self.n = eng, sem, 0, 0

    def done(self, ins):
        ins.then_inc(self.sem, 1)
        self.n += 1

    def now(self):
        return self.base + self.n

    def then(self, ins):
        self.done(ins)
        self.eng.wait_ge(self.sem, self.now())


class Each(Steps):

    def __init__(self, eng, sem, per):
        super().__init__(eng, sem)
        self.per = per

    def at(self, i):
        self.base, self.n = i * self.per, 0
        return self


def wait(eng, sem, value):
    if isinstance(value, int) and value <= 0:
        return
    eng.wait_ge(sem, value)


def over_pairs(eng, body, steps=(), pairs=QUADS // 2):
    before = [s.n for s in steps]
    for u in range(2):
        body(0, u)
    per = [s.n - b for s, b in zip(steps, before)]
    start = [s.n for s in steps]
    with eng.Fori(1, pairs - 1) as j:
        for s, b, k in zip(steps, start, per):
            s.base, s.n = (j - 1) * k + b, 0
        for u in range(2):
            body(j, u)
    for s, b, k in zip(steps, start, per):
        s.base, s.n = 0, b + (pairs - 2) * k
    for u in range(2):
        body(pairs - 1, u)


class Memory:

    def __init__(self, nc, stack, tag):
        self.nc, self.stack, self.tag = nc, stack, tag

    def sb(self, name, shape, dt=F32):
        return self.stack.enter_context(self.nc.sbuf_tensor(f"{self.tag}_{name}", list(shape), dt))

    def ps(self, name, shape=(P, 512)):
        return self.stack.enter_context(self.nc.psum_tensor(f"{self.tag}_{name}", list(shape), F32))

    def sem(self, name):
        return self.stack.enter_context(self.nc.semaphore(f"{self.tag}_{name}"))


def row(ap1d):
    return ap1d.rearrange("(a n) -> a n", a=1)


def col(ap1d):
    return ap1d.rearrange("(n a) -> n a", a=1)


def exp_steps(dve, st, x, out, tmp, k, pw, poly):
    ln2_hi = 0.693359375
    ln2_lo = -2.12194440054690583e-4
    st.then(dve.tensor_scalar(k, x, 1.4426950408889634, MAGIC, ALU.mult, ALU.add))
    st.then(dve.tensor_scalar(k, k, MAGIC, -126.0, ALU.subtract, ALU.max))
    st.then(dve.tensor_scalar(k, k, 127.0, None, ALU.min))
    st.then(dve.scalar_tensor_tensor(out=tmp, in0=k, scalar=-ln2_hi, in1=x, op0=ALU.mult, op1=ALU.add))
    st.then(dve.scalar_tensor_tensor(out=tmp, in0=k, scalar=-ln2_lo, in1=tmp, op0=ALU.mult, op1=ALU.add))
    st.then(dve.tensor_scalar(poly, tmp, 1.0 / 5040, None, ALU.mult))
    for c in (1.0 / 720, 1.0 / 120, 1.0 / 24, 1.0 / 6, 0.5, 1.0):
        st.then(dve.scalar_tensor_tensor(out=poly, in0=poly, scalar=c, in1=tmp, op0=ALU.add, op1=ALU.mult))
    st.then(dve.tensor_scalar(pw, k, 127.0, 8388608.0, ALU.add, ALU.mult))
    st.then(dve.scalar_tensor_tensor(out=out, in0=poly, scalar=1.0, in1=pw.bitcast(F32),
                                     op0=ALU.add, op1=ALU.mult))


class FilterTables:
    PHASES_AT = 14 + 3 + 2 + 3 + 1

    def __init__(self, nc, stack, taps):
        m = Memory(nc, stack, "s4")
        self.logdt, self.dskip, self.dt = (m.sb(n, (P, 1)) for n in ("logdt", "dskip", "dt"))
        self.are, self.aim, self.cre, self.cim = (m.sb(n, (P, NS)) for n in ("are", "aim", "cre", "cim"))
        self.t1k, self.t1t, self.t1p = (m.sb(n, (P, 1)) for n in ("t1k", "t1t", "t1p"))
        self.t1i = m.sb("t1i", (P, 1), I32)
        self.a1, self.b1, self.ea, self.wr, self.wi, self.dr, self.di, self.z1, self.z2, self.z3, self.inv = (
            m.sb(n, (P, NS)) for n in ("a1", "b1", "ea", "wr", "wi", "dr", "di", "z1", "z2", "z3", "inv"))
        self.zi = m.sb("zi", (P, NS), I32)
        self.phase, self.turns, self.decay, self.sine, self.half, self.cosine = (
            m.sb(n, (P, 16, NS)) for n in ("phase", "turns", "decay", "sine", "half", "cosine"))
        self.ur, self.ui, self.prod, self.prod2 = (m.sb(n, (P, 8, NS)) for n in ("ur", "ui", "prod", "prod2"))
        self.qm = m.sb("qm", (C + 2, 2, 2 * QT, H0 * SEQ))
        self.ct = m.sb("ct", (C + 1, 2, H0, P))
        self.taps = taps
        self.steps = m.sem("steps")
        self.tables = m.sem("tables")
        self.built = m.sem("built")

    def start(self, dve):
        self.dve, self.st = dve, Steps(dve, self.steps)

    def step_size(self):
        exp_steps(self.dve, self.st, self.logdt[:, :], self.dt[:, :], self.t1t[:, :], self.t1k[:, :],
                  self.t1i[:, :], self.t1p[:, :])
        self.st.then(self.dve.tensor_scalar(self.a1[:, :], self.are[:, :], self.dt[:, 0:1], None, ALU.mult))
        self.st.then(self.dve.tensor_scalar(self.b1[:, :], self.aim[:, :], self.dt[:, 0:1], None, ALU.mult))

    def multiples(self):
        for k in range(16):
            f = float(k if k < 8 else 8 * (k - 8))
            self.dve.tensor_scalar(self.phase[:, k, :], self.b1[:, :], f, None, ALU.mult)
            last = self.dve.tensor_scalar(self.decay[:, k, :], self.a1[:, :], f, None, ALU.mult)
        self.st.then(last)

    def phases(self):
        dve, st, phase, turns = self.dve, self.st, self.phase[:, :, :], self.turns[:, :, :]
        st.then(dve.tensor_scalar(turns, phase, 1 / TWO_PI, MAGIC, ALU.mult, ALU.add))
        st.then(dve.tensor_scalar(turns, turns, MAGIC, None, ALU.subtract))
        c1 = 6.28125
        c2 = float(np.float32(np.round((TWO_PI - c1) * 2 ** 21) / 2 ** 21))
        c3 = TWO_PI - c1 - c2
        for c in (c1, c2, c3):
            st.then(dve.scalar_tensor_tensor(out=phase, in0=turns, scalar=-c, in1=phase, op0=ALU.mult, op1=ALU.add))
        st.then(dve.tensor_scalar(phase, phase, 3.1415925, -3.1415925, ALU.min, ALU.max))
        assert st.n == self.PHASES_AT, st.n

    def table_functions(self, act):
        act.wait_ge(self.steps, self.PHASES_AT)
        act.activation(self.decay[:, :, :], self.decay[:, :, :], ACT.Exp)
        act.activation(self.sine[:, :, :], self.phase[:, :, :], ACT.Sin)
        act.activation(self.half[:, :, :], self.phase[:, :, :], ACT.Sin, scale=0.5).then_inc(self.tables, 1)

    def first_decay(self):
        exp_steps(self.dve, self.st, self.a1[:, :], self.ea[:, :], self.z1[:, :], self.z2[:, :],
                  self.zi[:, :], self.z3[:, :])

    def cosines(self):
        dve, st, half, cosine = self.dve, self.st, self.half[:, :, :], self.cosine[:, :, :]
        dve.wait_ge(self.tables, 1)
        st.then(dve.tensor_tensor(half, half, half, ALU.mult))
        st.then(dve.tensor_scalar(cosine, half, -2.0, 1.0, ALU.mult, ALU.add))

    def w_minus_one(self):
        dve, st, z1, z2 = self.dve, self.st, self.z1[:, :], self.z2[:, :]
        st.then(dve.scalar_tensor_tensor(out=z1, in0=self.ea[:, :], scalar=-1.0, in1=self.cosine[:, 1, :],
                                         op0=ALU.add, op1=ALU.mult))
        st.then(dve.scalar_tensor_tensor(out=self.wr[:, :], in0=self.half[:, 1, :], scalar=-2.0, in1=z1,
                                         op0=ALU.mult, op1=ALU.add))
        st.then(dve.tensor_tensor(self.wi[:, :], self.ea[:, :], self.sine[:, 1, :], ALU.mult))
        st.then(dve.tensor_tensor(z1, self.are[:, :], self.are[:, :], ALU.mult))
        st.then(dve.tensor_tensor(z2, self.aim[:, :], self.aim[:, :], ALU.mult))
        st.then(dve.tensor_tensor(z1, z1, z2, ALU.add))
        st.then(dve.reciprocal(self.inv[:, :], z1))

    def complex_mult(self, outr, outi, xr, xi, yr, yi, sign, t1, t2):
        dve, st = self.dve, self.st
        st.then(dve.tensor_tensor(t1, xi, yi, ALU.mult))
        st.then(dve.tensor_tensor(t2, xr, yi, ALU.mult))
        st.then(dve.tensor_tensor(outr, xr, yr, ALU.mult))
        st.then(dve.scalar_tensor_tensor(out=outr, in0=t1, scalar=-float(sign), in1=outr, op0=ALU.mult, op1=ALU.add))
        st.then(dve.tensor_tensor(outi, xi, yr, ALU.mult))
        st.then(dve.scalar_tensor_tensor(out=outi, in0=t2, scalar=float(sign), in1=outi, op0=ALU.mult, op1=ALU.add))

    def gains(self):
        dve, st = self.dve, self.st
        wr, wi, dr, di, z1, z2 = (t[:, :] for t in (self.wr, self.wi, self.dr, self.di, self.z1, self.z2))
        self.complex_mult(dr, di, wr, wi, self.are[:, :], self.aim[:, :], -1, z1, z2)
        st.then(dve.tensor_tensor(dr, dr, self.inv[:, :], ALU.mult))
        st.then(dve.tensor_tensor(di, di, self.inv[:, :], ALU.mult))
        self.complex_mult(wr, wi, dr, di, self.cre[:, :], self.cim[:, :], 1, z1, z2)
        st.then(dve.tensor_scalar(wr, wr, 2.0, None, ALU.mult))
        st.then(dve.tensor_scalar(wi, wi, 2.0, None, ALU.mult))

    def powers(self):
        dve, st = self.dve, self.st
        for t in (self.cosine, self.sine):
            st.then(dve.tensor_tensor(t[:, :, :], t[:, :, :], self.decay[:, :, :], ALU.mult))
        st.then(dve.memset(self.taps[:, 0:SEQ], 0.0))

    def scaled_powers(self):
        wrb = self.wr[:, :].unsqueeze(1).to_broadcast([P, 8, NS])
        wib = self.wi[:, :].unsqueeze(1).to_broadcast([P, 8, NS])
        self.complex_mult(self.ur[:, :, :], self.ui[:, :, :], self.cosine[:, 8:16, :], self.sine[:, 8:16, :],
                          wrb, wib, 1, self.prod[:, :, :], self.prod2[:, :, :])

    def taps_of(self, l1):
        dve, st, prod, prod2 = self.dve, self.st, self.prod[:, :, :], self.prod2[:, :, :]
        st.then(dve.tensor_tensor(prod, self.cosine[:, 0:8, :], self.ur[:, l1, :].unsqueeze(1).to_broadcast([P, 8, NS]),
                                  ALU.mult))
        st.then(dve.tensor_tensor(prod2, self.sine[:, 0:8, :], self.ui[:, l1, :].unsqueeze(1).to_broadcast([P, 8, NS]),
                                  ALU.mult))
        st.then(dve.tensor_tensor(prod, prod, prod2, ALU.subtract))
        st.then(dve.tensor_reduce(self.taps[:, SEQ + 8 * l1:SEQ + 8 * l1 + 8], prod, X, ALU.add))
        if l1 == 7:
            dve.tensor_tensor(self.taps[:, SEQ:SEQ + 1], self.taps[:, SEQ:SEQ + 1], self.dskip[:, :],
                              ALU.add).then_inc(self.built, 1)

    def dve_part(self, tile):
        if tile < 8:
            (self.step_size, self.multiples, self.phases, self.first_decay, self.cosines, self.w_minus_one,
             self.gains, self.powers)[tile]()
        elif tile == TILES - 8:
            self.scaled_powers()
        elif tile > TILES - 8:
            self.taps_of(tile - (TILES - 7))
            if tile == TILES - 1:
                self.taps_of(7)

    ACT_TILE = 3


def prepare(nc, a, g):
    with ExitStack() as stack:
        m = Memory(nc, stack, "pre")
        loaded, quant_in, others_in, built, pe_ready, act_st, dve_st, pool_st, stored = (
            m.sem(n) for n in ("loaded", "quant_in", "others_in", "built", "pe", "act", "dve", "pool", "stored"))
        wq = m.sb("wq", (P, H0 * DH0))
        wk = m.sb("wk", (C, H0 * DH0))
        wv = m.sb("wv", (C, H0 * DH0))
        wo = m.sb("wo", (P, 4, D))
        wq1 = m.sb("wq1", (P, P))
        wk1 = m.sb("wk1", (C, P))
        wv1 = m.sb("wv1", (C, P))
        film = m.sb("film", (P, 4 * D))
        bfilm = m.sb("bfilm", (C + 1, 4 * D))
        qraw = m.sb("qraw", (P, 3, INTER))
        gate_raw = qraw[:, 0, :].rearrange("p (c n) -> p c n", c=IC)
        up_raw = qraw[:, 1, :].rearrange("p (c n) -> p c n", c=IC)
        down_raw = qraw[:, 2, :].rearrange("p (c n) -> p c n", c=IC)
        blocks = qraw[:, :, :].rearrange("p w (b n) -> p (w b) n", n=32)
        bamax = m.sb("bamax", (P, 36))
        binv = m.sb("binv", (P, 36))
        masks = m.sb("masks", (P, 3, SEQ), U8)
        mrows = m.sb("mrows", (P, 2, SEQ))
        tmb = m.sb("tmb", (P, 2, SEQ))
        gate_s = m.sb("gate_s", (P, 1))
        one_col = m.sb("one_col", (P, 1))
        turned = m.sb("turned", (P, 16, P))
        pt = [m.ps(f"t{i}") for i in range(8)]

        s4 = g.s4
        LOADS, QUANT_LOADS = 13, 6
        block = stack.enter_context(nc.Block())

        @block.sync
        def _(sp):
            def load(sem, pairs):
                with nc.allow_non_contiguous_dma(reason="small constants"):
                    for dst, src in pairs:
                        sp.dma_start(dst, src).then_inc(sem, 16)

            def spread_row(name):
                return bass.AP(a[name].tensor, 0, [[0, P], [1, D]])

            attention_weights = (
                (wq[:, :], a["L0_xattn_W_q"]), (wk[:, :], a["L0_xattn_W_k"]), (wv[:, :], a["L0_xattn_W_v"]),
                (wq1[:, :], a["L1_xattn_Wq"]), (wk1[:, :], a["L1_xattn_Wk"]), (wv1[:, :], a["L1_xattn_Wv"]),
                (wo[:, :, :], a["L0_xattn_W_o"].rearrange("(c p) n -> p c n", p=P)),
                (g.n0[C:C + 1, 0, :], row(a["L0_xattn_b_o"])),
                (film[:, 0:2 * D], a["L1_xattn_W_film_in"]), (film[:, 2 * D:], a["L1_xattn_W_film_out"]),
                (bfilm[C:C + 1, 0:2 * D], row(a["L1_xattn_b_film_in"])),
                (bfilm[C:C + 1, 2 * D:], row(a["L1_xattn_b_film_out"])),
                (gate_s[:, :], bass.AP(a["L1_xattn_mod_gate"].tensor, 0, [[0, P], [1, 1]])))
            quantised_weights = (
                (gate_raw, a["L0_ffn_w_gate"].rearrange("(c p) n -> p c n", p=P)),
                (up_raw, a["L0_ffn_w_up"].rearrange("(c p) n -> p c n", p=P)),
                (qraw[:, 2, :], a["L0_ffn_w_down"]),
                (masks[:, 0, :], a["mask_BxS2_bk0"]), (masks[:, 1, :], a["mask_BxS2_bf1"]),
                (masks[:, 2, :], a["mask_BxS_bf1"]))
            others = (
                (s4.logdt[:, :], col(a["L1_xattn_log_dt"])), (s4.dskip[:, :], col(a["L1_xattn_D_skip"])),
                (s4.are[:, :], a["L1_xattn_A_re"]), (s4.aim[:, :], a["L1_xattn_A_im"]),
                (s4.cre[:, :], a["L1_xattn_C_re"]), (s4.cim[:, :], a["L1_xattn_C_im"]),
                (g.w1[:, :], a["L1_xattn_W1"]),
                (g.w2[:, :, :], a["L1_xattn_W2"].rearrange("(c p) n -> p c n", p=P)),
                (g.b1[:, :], a["L1_xattn_b1"].rearrange("(c p) -> p c", p=P)),
                (g.ffn_g[:, :], col(a["L1_xattn_g_ffn"])), (g.ffn_b[:, :], col(a["L1_xattn_b_ffn"])),
                *((g.wide[:, k, :], spread_row(f"L1_xattn_{name}"))
                  for k, name in enumerate(("g_norm_in", "b_norm_in", "b2", "g_norm_out", "b_norm_out"))))
            load(loaded, attention_weights)
            load(quant_in, quantised_weights)
            x_src = a["x"].rearrange("b s d -> (b s) d").rearrange("(t p) d -> p t d", p=P)
            assert (len(attention_weights), len(quantised_weights)) == (LOADS, QUANT_LOADS)

            def load_x(part, first, last):
                sp.dma_start(g.x[:, first:last, :], x_src[:, first:last, :]).then_inc(g.x_in[part], 16)
            load_x(0, 0, 8)
            load(others_in, others)
            load_x(1, 8, 16)
            load_x(2, 16, TILES)
            sp.wait_ge(built, 1)
            sp.dma_start(g.mask_rows.rearrange("m (b s) -> b m s", b=BATCH), mrows[:, :, :]).then_inc(stored, 16)
            sp.wait_ge(stored, 16)
            sp.wait_ge(others_in, 16 * len(others))
        QUANT_AT = 7
        TMASK_AT = 10

        @block.gpsimd
        def _(pool):
            st = Steps(pool, pool_st)
            st.then(pool.memset(g.ident[:, :], 0.0))
            st.then(pool.affine_select(out=g.ident[:, :], in_=g.ident[:, :], compare_op=ALU.not_equal, fill=1.0,
                                       base=0, pattern=[[-1, P]], channel_multiplier=1))
            st.then(pool.memset(g.pairsum[:, :], 0.0))
            for base in (0, -SEQ):
                st.then(pool.affine_select(out=g.pairsum[:, :], in_=g.pairsum[:, :], compare_op=ALU.not_equal,
                                           fill=0.25, base=base, pattern=[[-1, SEQ]], channel_multiplier=1))
            st.then(pool.memset(g.minus_half[:, :], -0.5))
            st.then(pool.memset(g.eps[:, :], EPS))
            st.then(pool.memset(one_col[:, :], 1.0))
            st.then(pool.memset(s4.qm[C:C + 2, :, :, :], 0.0))
            st.then(pool.memset(s4.qm[C:C + 1, :, :, :], 1.0))
            st.then(pool.memset(s4.ct[C:C + 1, :, :, :], 1.0))
            st.then(pool.memset(g.minus_one[:, :], -1.0))
            pool.wait_ge(loaded, 16 * LOADS)
            st.then(pool.memset(g.n0[C:C + 1, 1:H0, :], 0.0))

        turns_of = ([(wq[:, 128 * i:128 * i + 128], P, P) for i in range(4)]
                    + [(wk[:, 128 * i:128 * i + 128], C, P) for i in range(4)]
                    + [(wv[:, 128 * i:128 * i + 128], C, P) for i in range(4)]
                    + [(wq1[:, :], P, P), (wk1[:, :], C, P), (wv1[:, :], C, P)])
        quant_of = ([gate_raw[:, i, :] for i in range(IC)] + [up_raw[:, i, :] for i in range(IC)]
                    + [down_raw[:, i, :] for i in range(IC)])

        @block.tensor
        def _(pe):
            pe.wait_ge(loaded, 16 * LOADS)
            pe.wait_ge(pool_st, 2)
            for i, (src, rows, cols) in enumerate(turns_of):
                pe.transpose(pt[i // 4][0:cols, 128 * (i % 4):128 * (i % 4) + rows], src,
                             g.ident[0:rows, 0:rows]).then_inc(pe_ready, 1)
            pe.wait_ge(act_st, 1)
            n = len(turns_of)
            for h in range(H0):
                r = DH0 * (h % 2)
                pe.matmul(pt[4 + h % 2][:, 128 * (h // 2):128 * (h // 2) + C], turned[r:r + DH0, h // 2, 0:P],
                          turned[r:r + DH0, 4 + h // 2, 0:C], start=True, stop=True).then_inc(pe_ready, 1)
            for h in range(H0):
                r = DH0 * (h % 2)
                pe.matmul(pt[6 + h % 2][0:C, 128 * (h // 2):128 * (h // 2) + D], turned[r:r + DH0, 8 + h // 2, 0:C],
                          wo[r:r + DH0, h // 2, :], start=True, stop=True).then_inc(pe_ready, 1)
            n += 16
            pe.wait_ge(act_st, 2)
            for h in range(H1):
                r = DH1 * h
                pe.matmul(pt[h][:, 0:C], turned[r:r + DH1, 12, 0:P],
                          turned[r:r + DH1, 13, 0:C], start=True, stop=True).then_inc(pe_ready, 1)
            pe.matmul(pt[4][0:C, :], turned[:, 14, 0:C], film[:, :], start=True, stop=True).then_inc(pe_ready, 1)
            pe.wait_ge(dve_st, QUANT_AT)
            for i, src in enumerate(quant_of):
                pe.transpose(pt[5 + i // 4][:, 128 * (i % 4):128 * (i % 4) + 128], src,
                             g.ident[:, :]).then_inc(pe_ready, 1)
            pe.wait_ge(dve_st, TMASK_AT)
            pe.wait_ge(act_st, 3)
            pe.transpose(pt[0][:, 0:P], tmb[:, :, :].rearrange("p a s -> p (a s)"), g.ident[:, :]).then_inc(pe_ready, 1)

        @block.scalar
        def _(act):
            act.wait_ge(pe_ready, 15)
            st = Steps(act, act_st)
            for b in range(4):
                k = 4 if b < 3 else 3
                rows = P if b in (0, 3) else C
                src = pt[b][:, 0:128 * k].rearrange("p (i n) -> p i n", n=128)
                if b == 3:
                    act.copy(turned[:, 12:13, :], src[:, 0:1, :])
                    ins = act.copy(turned[:, 13:15, 0:C], src[:, 1:3, 0:C])
                else:
                    ins = act.copy(turned[:, 4 * b:4 * b + k, 0:rows], src[:, :, 0:rows])
            st.then(ins)
            act.wait_ge(pe_ready, 31)
            for b in range(2):
                act.copy(g.m0[:, b::2, :],
                         pt[4 + b][:, :].rearrange("p (i n) -> p i n", n=128)[:, :, 0:C])
                ins = act.copy(g.n0[0:C, b::2, :],
                               pt[6 + b][0:C, :].rearrange("p (i n) -> p i n", n=128))
            st.then(ins)
            act.wait_ge(pe_ready, 36)
            for h in range(H1):
                act.copy(g.m1[:, h, :], pt[h][:, 0:C])
            act.mul(g.film[0:C, :], pt[4][0:C, :], gate_s[0:C, 0:1])
            ins = act.mul(g.film[C:C + 1, :], bfilm[C:C + 1, :], gate_s[C:C + 1, 0:1])
            st.then(ins)
            fr = g.film[C:C + 1, :].rearrange("p (a b n) -> p a b n", a=2, b=2)
            act.wait_ge(pool_st, 8)
            st.then(act.activation(fr[:, :, 0, :], fr[:, :, 0, :], ACT.Identity, bias=one_col[C:C + 1, 0:1]))
            act.wait_ge(pe_ready, 45)
            act.copy(g.gate_t[:, 0:3 * P], pt[5][:, 0:3 * P])
            act.copy(g.up_t[:, 0:P], pt[5][:, 3 * P:])
            act.copy(g.up_t[:, P:3 * P], pt[6][:, 0:2 * P])
            act.copy(g.down_t[:, 0:2, :], pt[6][:, 2 * P:].rearrange("p (i n) -> p i n", n=P))
            ins = act.copy(g.down_t[:, 2, :], pt[7][:, 0:P])
            act.wait_ge(pe_ready, 46)
            ins = act.copy(g.tmask[:, :], pt[0][:, 0:P])
            st.then(ins)

        @block.vector
        def _(dve):
            st = Steps(dve, dve_st)
            dve.wait_ge(quant_in, 16 * QUANT_LOADS)
            st.then(dve.tensor_reduce(bamax[:, :], blocks, X, ALU.max, apply_absolute_value=True))
            st.then(dve.tensor_scalar(bamax[:, :], bamax[:, :], 1.0 / 7.0, 1e-12, ALU.mult, ALU.max))
            st.then(dve.reciprocal(binv[:, :], bamax[:, :]))
            st.then(dve.tensor_tensor(blocks, blocks, binv[:, :].unsqueeze(2).to_broadcast([P, 36, 32]), ALU.mult))
            st.then(dve.tensor_scalar(blocks, blocks, MAGIC, MAGIC, ALU.add, ALU.subtract))
            st.then(dve.tensor_scalar(blocks, blocks, 7.0, -8.0, ALU.min, ALU.max))
            st.then(dve.tensor_tensor(blocks, blocks, bamax[:, :].unsqueeze(2).to_broadcast([P, 36, 32]), ALU.mult))
            assert st.n == QUANT_AT
            st.then(dve.tensor_scalar(mrows[:, :, :], masks[:, 0:2, :], -1.0, FAR, ALU.add, ALU.mult))
            dve.sem_inc(built, 1)
            st.then(dve.tensor_copy(tmb[:, 0, :], masks[:, 2, :]))
            st.then(dve.tensor_copy(tmb[:, 1, :], masks[:, 2, :]))
            assert st.n == TMASK_AT


def norm_steps(dve, carry, pool_done, st, x_tiles, stats, mv, out_tiles, pool_ready, count):
    norm_stats(dve, carry, st, x_tiles, stats, mv, pool_ready)
    dve.wait_ge(pool_done, count + 1)
    return norm_apply(dve, x_tiles, mv, out_tiles)


def norm_stats(dve, carry, st, x_tiles, stats, mv, pool_ready):
    for t in range(QT):
        last = dve.bn_stats(stats[:, t, :], x_tiles[t])
    st.then(last)
    dve.memset(carry[:, 0:1], 0.0)
    for t in range(QT):
        last = dve.bn_aggr(mv[:, t, :], stats[:, t, :])
    last.then_inc(pool_ready, 1)


def norm_apply(dve, x_tiles, mv, out_tiles):
    for t in range(QT):
        last = dve.tensor_scalar(out_tiles[t], x_tiles[t], mv[:, t, 0:1], mv[:, t, 1:2], ALU.subtract, ALU.mult)
    return last


def rstd_steps(pool, g, mv, stats_ready, rstd_ready, link, count):
    pool.wait_ge(stats_ready, count + 1)
    link.then(pool.tensor_tensor(mv[:, :, 1:2], mv[:, :, 1:2], g.eps[:, 0:QT].unsqueeze(2), ALU.add))
    pool.tensor_tensor(mv[:, :, 1:2], mv[:, :, 1:2], g.minus_half[:, 0:QT].unsqueeze(2), ALU.pow).then_inc(rstd_ready, 1)


def attention0(nc, a, g):
    f, s4 = g.f, g.s4
    with ExitStack() as stack:
        m = Memory(nc, stack, "at0")
        ctx_in = [m.sem(f"ctx_in{u}") for u in range(2)]
        stats_ready, rstd_ready = m.sem("stats_ready"), m.sem("rstd_ready")
        xn_ready = m.sem("xn_ready")
        ring_ready, ring_evac = m.sem("ring_ready"), m.sem("ring_evac")
        s_ready, shifted, exp_ready = m.sem("s_ready"), m.sem("shifted"), m.sem("exp_ready")
        inv_ready, prob_ready = m.sem("inv_ready"), m.sem("prob_ready")
        pt_ready, pt_evac = m.sem("pt_ready"), m.sem("pt_evac")
        c_ready, c_evac = m.sem("c_ready"), m.sem("c_evac")
        o_ready, x_added = m.sem("o_ready"), m.sem("x_added")
        next_stats, next_rstd, next_ready, peaked = (
            m.sem(n) for n in ("next_stats", "next_rstd", "next_ready", "peaked"))
        dve_st, pool_st = m.sem("dve_st"), m.sem("pool_st")

        xn = m.sb("xn", (P, 2, QT, P))
        nx = m.sb("nx", (P, QT, P))
        nstats = m.sb("nstats", (P, 2, QT, 6))
        nmv = m.sb("nmv", (P, 2, QT, 2))
        xnt = m.sb("xnt", (P, 2, QN))
        ctxn = m.sb("ctxn", (P, 2, QT, C))
        ctxt = m.sb("ctxt", (C + 2, 2, QN))
        qm, ct = s4.qm, s4.ct
        stats = m.sb("stats", (P, 2, QT, 6))
        mv = m.sb("mv", (P, 2, QT, 2))
        sd = m.sb("sd", (P, 2, 8, SEQ))
        mx, sm = m.sb("mx", (P, 2, 8)), m.sb("sm", (P, 2, 8))
        pr = m.sb("pr", (P, 2, 8, SEQ))
        pts = m.sb("pts", (P, 2, 4 * P))
        ring = [m.ps(f"ring{i}") for i in range(2)]
        sp_ = [m.ps(f"s{i}") for i in range(2)]
        ptp = m.ps("pt")
        cp = [m.ps(f"c{i}") for i in range(2)]
        op = m.ps("o")
        block = stack.enter_context(nc.Block())
        NORM, NEXT, CTX = "norm", "next", "context"
        after_two = (NORM, 0, 1, 2, 3, 4, 5, 6, NEXT, 7, CTX)
        spread = ((0, 1, 2), (3, 4, 5), (6, 7, 8), (9, 10))

        def early(q):
            return isinstance(q, int) and q < 2

        def start(q):
            return 10 * q if early(q) else 11 * q - 2

        def uses(q, t=None):
            kinds = [k for k in after_two if not (early(q) and k == NEXT)]
            found = []
            for i, kind in enumerate(kinds):
                if t is None or after_two.index(kind) in spread[t]:
                    found.append((start(q) + i, i, kind))
            return found

        def turned_next(q):
            if isinstance(q, int) and q >= QUADS - 2:
                return start(QUADS) + q - (QUADS - 2) + 1
            return start(q + 2) + 9

        ctx_src = a["ctx_768"].rearrange("b s c -> (b s) c").rearrange("(q t p) c -> q p t c", p=P, t=QT)
        mask_src = g.mask_rows.rearrange("m (q n) -> q m n", q=QUADS)

        @block.sync
        def _(sp):
            def load(j, u):
                q = 2 * j + u
                wait(sp, c_ready, 8 * (q - 1))
                sp.dma_start(ctxn[:, u, :, :], at_quad(ctx_src, q)).then_inc(ctx_in[u], 16)
                sp.dma_start(ctxt[C:C + 2, u, :], at_quad(mask_src, q)).then_inc(ctx_in[u], 16)
            over_pairs(sp, load)
            sp.wait_ge(s4.built, 1)
            sp.dma_start(g.taps_out, s4.taps[:, :].unsqueeze(1).to_broadcast([D, SEQ, 2 * SEQ])).then_inc(g.taps_stored, 16)

        def slot_of(q, u, i):
            return ring[i % 2 if early(q) else (u + i) % 2]

        def turn_next(pe, q, number, slot):
            pe.wait_ge(next_ready, q + 1)
            pe.wait_ge(ring_evac, number - 1)
            for t in range(QT):
                last = pe.transpose(slot[:, t * P:t * P + P], nx[:, t, :], g.ident[:, :])
            last.then_inc(ring_ready, 1)

        def keep_next(act, q, number, slot):
            act.wait_ge(ring_ready, number + 1)
            act.copy(f.piece(q), slot[:, :]).then_inc(ring_evac, 1)

        def front_pe(pe, j, u, t=None):
            q = 2 * j + u
            for n, i, kind in uses(q, t):
                slot = slot_of(q, u, i)
                if kind == NEXT:
                    turn_next(pe, q - 2, n, slot)
                    continue
                if kind == CTX:
                    pe.wait_ge(ctx_in[u], 32 * (j + 1))
                if kind == NORM:
                    pe.wait_ge(xn_ready, q + 1)
                wait(pe, ring_evac, n - 1 if kind != 0 else n)
                if kind == CTX:
                    for tt in range(QT):
                        last = pe.transpose(slot[0:C, tt * P:tt * P + P], ctxn[:, u, tt, :], g.ident[:, :])
                elif kind == NORM:
                    for tt in range(QT):
                        last = pe.transpose(slot[:, tt * P:tt * P + P], xn[:, u, tt, :], g.ident[:, :])
                else:
                    last = pe.matmul(slot[0:C, :], g.m0[:, kind, :], xnt[:, u, :], start=True, stop=True)
                last.then_inc(ring_ready, 1)

        def front_act(act, j, u, t=None):
            q = 2 * j + u
            for n, i, kind in uses(q, t):
                slot = slot_of(q, u, i)
                if kind == NEXT:
                    keep_next(act, q - 2, n, slot)
                    continue
                act.wait_ge(ring_ready, n + 1)
                if kind == CTX:
                    ins = act.copy(ctxt[0:C, u, :], slot[0:C, :])
                elif kind == NORM:
                    ins = act.copy(xnt[:, u, :], slot[:, :])
                else:
                    ins = act.copy(qm[0:C, u, :, kind * SEQ:(kind + 1) * SEQ],
                                   slot[0:C, :].rearrange("c (b s) -> c b s", s=SEQ))
                ins.then_inc(ring_evac, 1)

        @block.tensor
        def _(pe):
            def scores(j, u, t):
                q, n = 2 * j + u, 8 * j + 4 * u + t
                wait(pe, ring_evac, start(q + 1))
                wait(pe, shifted, n - 1)
                for b in range(2):
                    tok = slice(t * P + b * SEQ, t * P + b * SEQ + SEQ)
                    for p in range(4):
                        c0 = (2 * p + b) * SEQ
                        last = pe.matmul(sp_[t % 2][:, c0:c0 + SEQ], qm[:, u, 2 * t + b, 2 * p * SEQ:2 * (p + 1) * SEQ],
                                         ctxt[:, u, tok], start=True, stop=True)
                last.then_inc(s_ready, 1)

            def turn(n, t):
                pe.wait_ge(prob_ready, n + 1)
                wait(pe, pt_evac, n)
                for p in range(4):
                    last = pe.transpose(ptp[:, p * P:p * P + P],
                                        pr[:, t % 2, 2 * p:2 * p + 2, :].rearrange("p a s -> p (a s)"), g.ident[:, :])
                last.then_inc(pt_ready, 1)

            def attend(n, u, t):
                pe.wait_ge(pt_evac, n + 1)
                for b in range(2):
                    wait(pe, c_evac, 2 * n - 1 + b)
                    r = slice(b * SEQ, b * SEQ + SEQ)
                    pe.matmul(cp[b][0:C, :], ctxn[r, u, t, :], pts[r, t % 2, :],
                              start=True, stop=True).then_inc(c_ready, 1)

            def project(n, q, t):
                pe.wait_ge(c_evac, 2 * n + 2)
                if t == 0:
                    wait(pe, x_added, q)
                for h in range(H0):
                    last = pe.matmul(op[:, t * P:t * P + P], ct[:, t % 2, h, :], g.n0[:, h, :],
                                     start=(h == 0), stop=(h == H0 - 1))
                last.then_inc(o_ready, 1)

            def body(j, u):
                for t in range(QT):
                    n, q = 8 * j + 4 * u + t, 2 * j + u
                    more = not (isinstance(q, int) and q == QUADS - 1)
                    if more:
                        front_pe(pe, j + (u == 1), 1 - u, t)
                    if t < 3:
                        scores(j, u, t + 1)
                    turn(n, t)
                    if t == 3 and more:
                        scores(j + (u == 1), 1 - u, 0)
                    if t > 0:
                        project(n - 1, q, t - 1)
                    elif not (isinstance(q, int) and q == 0):
                        project(n - 1, q - 1, 3)
                    attend(n, u, t)

            front_pe(pe, 0, 0)
            scores(0, 0, 0)
            over_pairs(pe, body)
            project(TILES - 1, QUADS - 1, 3)
            for q in (QUADS - 2, QUADS - 1):
                turn_next(pe, q, turned_next(q) - 1, ring[q % 2])

        @block.scalar
        def _(act):
            def exps(n, t):
                act.wait_ge(shifted, n + 1)
                act.activation(sd[:, t % 2, :, :], sd[:, t % 2, :, :], ACT.Exp, scale=DH0 ** -0.5).then_inc(exp_ready, 1)

            def body(j, u):
                for t in range(QT):
                    n, q = 8 * j + 4 * u + t, 2 * j + u
                    more = not (isinstance(q, int) and q == QUADS - 1)
                    if more:
                        front_act(act, j + (u == 1), 1 - u, t)
                    act.wait_ge(pt_ready, n + 1)
                    act.copy(pts[:, t % 2, :], ptp[:, :]).then_inc(pt_evac, 1)
                    if more or t < 3:
                        exps(n + 1, t + 1)
                    if isinstance(n, int) and n == s4.ACT_TILE:
                        s4.table_functions(act)
                    for b in range(2):
                        act.wait_ge(c_ready, 2 * n + 1 + b)
                        act.copy(ct[0:C, t % 2, :, b * SEQ:b * SEQ + SEQ],
                                 cp[b][0:C, :].rearrange("p (h s) -> p h s", s=SEQ)).then_inc(c_evac, 1)

            front_act(act, 0, 0)
            exps(0, 0)
            over_pairs(act, body)
            for q in (QUADS - 2, QUADS - 1):
                keep_next(act, q, turned_next(q) - 1, ring[q % 2])

        @block.gpsimd
        def _(pool):
            st = Steps(pool, pool_st)

            def rstd(j, u):
                rstd_steps(pool, g, mv[:, u, :, :], stats_ready, rstd_ready, st, 2 * j + u)

            def body(j, u):
                for t in range(QT):
                    n, q = 8 * j + 4 * u + t, 2 * j + u
                    if t == 2 and not (isinstance(q, int) and q >= QUADS - 2):
                        rstd(j + 1, u)
                    if t == 1 and not (isinstance(q, int) and q == 0):
                        next_rstds(j + u - 1, 1 - u)
                    pool.wait_ge(inv_ready, n + 1)
                    wait(pool, pt_ready, n - 1)
                    pool.tensor_tensor(pr[:, t % 2, :, :], sd[:, t % 2, :, :],
                                       sm[:, t % 2, :].unsqueeze(2).to_broadcast([P, 8, SEQ]),
                                       ALU.mult).then_inc(prob_ready, 1)

            st_next = Each(pool, m.sem("pool_next"), 1)

            def next_rstds(j, u):
                q = 2 * j + u
                rstd_steps(pool, g, nmv[:, u, :, :], next_stats, next_rstd, st_next.at(q), q)

            rstd(0, 0)
            rstd(0, 1)
            over_pairs(pool, body, [st])
            next_rstds(QUADS // 2 - 1, 1)

        @block.vector
        def _(dve):
            st = Steps(dve, dve_st)

            def stats_of(j, u):
                q = 2 * j + u
                wait(dve, xn_ready, q - 1)
                norm_stats(dve, g.carry, st, [g.xt(q, t) for t in range(QT)], stats[:, u, :, :], mv[:, u, :, :],
                           stats_ready)

            def norm(j, u):
                q = 2 * j + u
                wait(dve, ring_ready, start(q - 2) + 1)
                dve.wait_ge(rstd_ready, q + 1)
                norm_apply(dve, [g.xt(q, t) for t in range(QT)], mv[:, u, :, :],
                           [xn[:, u, t, :] for t in range(QT)]).then_inc(xn_ready, 1)

            def shift(n, t):
                dve.wait_ge(s_ready, n + 1)
                src = sp_[t % 2][:, :].rearrange("p (k s) -> p k s", s=SEQ)
                st.then(dve.tensor_reduce(mx[:, t % 2, :], src, X, ALU.max))
                wait(dve, prob_ready, n - 1)
                dve.tensor_tensor(sd[:, t % 2, :, :], src, mx[:, t % 2, :].unsqueeze(2).to_broadcast([P, 8, SEQ]),
                                  ALU.subtract).then_inc(shifted, 1)

            def sums(n, t):
                dve.wait_ge(exp_ready, n + 1)
                st.then(dve.tensor_reduce(sm[:, t % 2, :], sd[:, t % 2, :, :], X, ALU.add))
                dve.reciprocal(sm[:, t % 2, :], sm[:, t % 2, :]).then_inc(inv_ready, 1)

            def add(q):
                dve.wait_ge(o_ready, 4 * (q + 1))
                xs = g.xq(q)
                dve.tensor_tensor(xs, xs, op[:, :], ALU.add).then_inc(x_added, 1)

            st_next = Each(dve, m.sem("dve_next"), 1)

            def next_stats_of(j, u):
                q = 2 * j + u
                wait(dve, next_ready, q - 1)
                dve.wait_ge(x_added, q + 1)
                dve.memset(g.carry[:, 2:3], 0.0)
                norm_stats(dve, g.carry[:, 1:2], st_next.at(q), [g.xt(q, t) for t in range(QT)], nstats[:, u, :, :],
                           nmv[:, u, :, :], next_stats)

            def next_norm(j, u):
                q = 2 * j + u
                if not (isinstance(q, int) and q == 0):
                    dve.wait_ge(ring_ready, turned_next(q - 1))
                dve.wait_ge(next_rstd, q + 1)
                norm_apply(dve, [g.xt(q, t) for t in range(QT)], nmv[:, u, :, :],
                           [nx[:, t, :] for t in range(QT)]).then_inc(next_ready, 1)

            def peak(q):
                dve.wait_ge(ring_evac, turned_next(q))
                dve.tensor_reduce(f.peak[:, 0, bass.ds(q, 1)], f.piece(q), X, ALU.max,
                                  apply_absolute_value=True).then_inc(peaked, 1)

            def body(j, u):
                for t in range(QT):
                    n, q = 8 * j + 4 * u + t, 2 * j + u
                    sums(n, t)
                    if t < 3 or not (isinstance(q, int) and q == QUADS - 1):
                        shift(n + 1, t + 1)
                    if t == 0 and not (isinstance(q, int) and q == 0):
                        add(q - 1)
                        next_stats_of(j + u - 1, 1 - u)
                    if t == 1 and not (isinstance(q, int) and q >= QUADS - 2):
                        if isinstance(q, int) and q < 2:
                            dve.wait_ge(g.x_in[1 + q], 16)
                        stats_of(j + 1, u)
                    if t == 2 and not (isinstance(q, int) and q >= QUADS - 2):
                        norm(j + 1, u)
                    if t == 1 and not (isinstance(q, int) and q == 0):
                        next_norm(j + u - 1, 1 - u)
                    if t == 3 and not (isinstance(q, int) and q < 2):
                        peak(q - 2)
                    if isinstance(n, int):
                        s4.dve_part(n)

            s4.start(dve)
            dve.wait_ge(g.x_in[0], 16)
            for u in range(2):
                stats_of(0, u)
                norm(0, u)
            shift(0, 0)
            over_pairs(dve, body, [st])
            add(QUADS - 1)
            next_stats_of(QUADS // 2 - 1, 1)
            next_norm(QUADS // 2 - 1, 1)
            peak(QUADS - 2)
            peak(QUADS - 1)


class Quantised:

    def __init__(self, nc, stack):
        m = Memory(nc, stack, "ffn")
        self.h_t = m.sb("h_t", (P, TOK))
        self.peak = m.sb("peak", (P, 2, QUADS))
        self.top = m.sb("top", (P, 2))
        self.scale = m.sb("scale", (P, 5))
        self.inv = m.sb("inv", (P, 5))
        self.unit = m.sb("unit", (P, 5))

    def hold_act(self, nc, stack):
        self.act = Memory(nc, stack, "ffn").sb("act", (P, IC, TOK))

    def piece(self, q):
        return self.h_t[:, bass.ds(q * QN, QN)]

    def act_piece(self, q):
        return self.act[:, :, bass.ds(q * QN, QN)]


H_IN, H_UP, H_GATE, H_GATED, H_OUT = range(5)


def scale_dve(dve, st, f, kinds, peak_ready, top_ready, unit_of=(), row=0):
    n = len(kinds)
    dve.tensor_reduce(f.top[:, 0:n], f.peak[:, row:row + n, :], X, ALU.max).then_inc(peak_ready, 1)
    k = slice(kinds[0], kinds[0] + n)
    st.then(dve.memset(f.unit[:, k], 1.0))
    for other in unit_of:
        st.then(dve.tensor_tensor(f.unit[:, k], f.unit[:, k], f.scale[:, other:other + 1], ALU.mult))
    dve.wait_ge(top_ready, 1)
    st.then(dve.tensor_tensor(f.top[:, 0:n], f.top[:, 0:n], f.unit[:, k], ALU.mult))
    st.then(dve.tensor_scalar(f.scale[:, k], f.top[:, 0:n], 1.0 / QMAX, 1e-12, ALU.mult, ALU.max))
    st.then(dve.reciprocal(f.inv[:, k], f.scale[:, k]))
    st.then(dve.tensor_tensor(f.inv[:, k], f.inv[:, k], f.unit[:, k], ALU.mult))


def scale_pool(pool, f, n, peak_ready, top_ready):
    pool.wait_ge(peak_ready, 1)
    pool.partition_all_reduce(f.top[:, 0:n], f.top[:, 0:n], P, RMAX).then_inc(top_ready, 1)


def gate_max(nc, a, g):
    f = g.f
    with ExitStack() as stack:
        m = Memory(nc, stack, "gm")
        in_peak, in_top, rounded = m.sem("in_peak"), m.sem("in_top"), m.sem("rounded")
        made, kept, peaked, peak_ready, top_ready, dve_st = (
            m.sem(n) for n in ("made", "kept", "peaked", "peak_ready", "top_ready", "dve_st"))
        group = [m.ps(f"p{i}", (P, IC, 512)) for i in range(2)]
        block = stack.enter_context(nc.Block())

        @block.tensor
        def _(pe):
            def body(j, u):
                q = 2 * j + u
                pe.wait_ge(rounded, q + 1)
                wait(pe, kept, q - 1)
                for c in range(IC):
                    last = pe.matmul(group[u][:, c, :], g.gate_t[:, c * P:c * P + P], f.piece(q), start=True, stop=True)
                last.then_inc(made, 1)
            over_pairs(pe, body)

        @block.scalar
        def _(act):
            def body(j, u):
                q = 2 * j + u
                act.wait_ge(made, q + 1)
                act.copy(f.act_piece(q), group[u][:, :, :]).then_inc(kept, 1)
            over_pairs(act, body)

        @block.gpsimd
        def _(pool):
            scale_pool(pool, f, 1, in_peak, in_top)
            scale_pool(pool, f, 1, peak_ready, top_ready)

        @block.vector
        def _(dve):
            st = Steps(dve, dve_st)
            st_grid = Each(dve, m.sem("st_grid"), 1)

            def grid(q):
                h = f.piece(q)
                st_grid.at(q).then(dve.tensor_scalar(h, h, f.inv[:, H_IN:H_IN + 1], MAGIC, ALU.mult, ALU.add))
                dve.tensor_scalar(h, h, MAGIC, f.scale[:, H_IN:H_IN + 1], ALU.subtract, ALU.mult).then_inc(rounded, 1)

            def body(j, u):
                q = 2 * j + u
                if not (isinstance(q, int) and q == QUADS - 1):
                    grid(q + 1)
                dve.wait_ge(kept, q + 1)
                dve.tensor_reduce(f.peak[:, 0, bass.ds(q, 1)], f.act_piece(q), XY, ALU.max,
                                  apply_absolute_value=True).then_inc(peaked, 1)
            scale_dve(dve, st, f, [H_IN], in_peak, in_top)
            grid(0)
            over_pairs(dve, body)
            dve.wait_ge(peaked, QUADS)
            scale_dve(dve, st, f, [H_GATE], peak_ready, top_ready)


def gate(nc, a, g):
    f = g.f
    with ExitStack() as stack:
        m = Memory(nc, stack, "gate")
        made, shifted, gridded, sig_ready, rounded, gated, up_peaked, peaked, peak_ready, top_ready, dve_st = (
            m.sem(n) for n in ("made", "shifted", "gridded", "sig_ready", "rounded", "gated", "up_peaked", "peaked",
                               "peak_ready", "top_ready", "dve_st"))
        up_peak_ready, up_top_ready = m.sem("up_peak_ready"), m.sem("up_top_ready")
        group = [m.ps(f"p{i}", (P, IC, 512)) for i in range(2)]
        gt = m.sb("gt", (P, 2, IC, QN))
        sg = m.sb("sg", (P, 2, IC, QN))
        magic = m.sb("magic", (P, 2))
        block = stack.enter_context(nc.Block())

        @block.tensor
        def _(pe):
            def body(j, u):
                q = 2 * j + u
                wait(pe, up_peaked, q - 1)
                for c in range(IC):
                    last = pe.matmul(group[u][:, c, :], g.up_t[:, c * P:c * P + P], f.piece(q), start=True, stop=True)
                last.then_inc(made, 1)
            over_pairs(pe, body)

        @block.scalar
        def _(act):
            def shift(j, u):
                q = 2 * j + u
                wait(act, gated, q - 1)
                act.activation(gt[:, u, :, :], f.act_piece(q), ACT.Identity, scale=f.inv[:, H_GATE:H_GATE + 1],
                               bias=magic[:, 0:1]).then_inc(shifted, 1)

            def grid(j, u):
                act.wait_ge(shifted, 2 * j + u + 1)
                act.activation(gt[:, u, :, :], gt[:, u, :, :], ACT.Identity, bias=magic[:, 1:2]).then_inc(gridded, 1)

            def body(j, u):
                q = 2 * j + u
                more = not (isinstance(q, int) and q == QUADS - 1)
                act.wait_ge(gridded, q + 1)
                act.activation(sg[:, u, :, :], gt[:, u, :, :], ACT.Sigmoid,
                               scale=f.scale[:, H_GATE:H_GATE + 1]).then_inc(sig_ready, 1)
                if more:
                    shift(j + u, 1 - u)
                    grid(j + u, 1 - u)
            act.wait_ge(dve_st, 2)
            shift(0, 0)
            grid(0, 0)
            over_pairs(act, body)

        @block.gpsimd
        def _(pool):
            scale_pool(pool, f, 1, up_peak_ready, up_top_ready)
            scale_pool(pool, f, 1, peak_ready, top_ready)

        @block.vector
        def _(dve):
            st = Steps(dve, dve_st)

            def peak(q):
                dve.wait_ge(gated, q + 1)
                dve.tensor_reduce(f.peak[:, 1, bass.ds(q, 1)], f.act_piece(q), XY, ALU.max,
                                  apply_absolute_value=True).then_inc(peaked, 1)

            def body(j, u):
                q = 2 * j + u
                dve.wait_ge(sig_ready, q + 1)
                s = sg[:, u, :, :]
                dve.tensor_scalar(s, s, 65535.0 / 65536, 192.0, ALU.min, ALU.add).then_inc(rounded, 1)
                dve.wait_ge(made, q + 1)
                dve.tensor_reduce(f.peak[:, 0, bass.ds(q, 1)], group[u][:, :, :], XY, ALU.max,
                                  apply_absolute_value=True).then_inc(up_peaked, 1)
                dve.wait_ge(rounded, q + 1)
                dve.scalar_tensor_tensor(out=f.act_piece(q), in0=s, scalar=192.0, in1=gt[:, u, :, :],
                                         op0=ALU.subtract, op1=ALU.mult).then_inc(gated, 1)
                if not (isinstance(q, int) and q == 0):
                    peak(q - 1)
            st.then(dve.memset(magic[:, 0:1], MAGIC))
            st.then(dve.memset(magic[:, 1:2], -MAGIC))
            over_pairs(dve, body)
            peak(QUADS - 1)
            dve.wait_ge(peaked, QUADS)
            dve.wait_ge(up_peaked, QUADS)
            scale_dve(dve, st, f, [H_UP], up_peak_ready, up_top_ready)
            scale_dve(dve, st, f, [H_GATED], peak_ready, top_ready, unit_of=(H_GATE,), row=1)


def up(nc, a, g):
    f = g.f
    with ExitStack() as stack:
        m = Memory(nc, stack, "up")
        made, shifted, again, gridded, multiplied, peaked, peak_ready, top_ready, dve_st = (
            m.sem(n) for n in ("made", "shifted", "again", "gridded", "multiplied", "peaked", "peak_ready", "top_ready",
                               "dve_st"))
        group = [m.ps(f"p{i}", (P, IC, 512)) for i in range(2)]
        ut = m.sb("ut", (P, 2, IC, QN))
        gt = m.sb("gt", (P, 2, IC, QN))
        magic = m.sb("magic", (P, 1))
        block = stack.enter_context(nc.Block())

        @block.tensor
        def _(pe):
            def body(j, u):
                q = 2 * j + u
                wait(pe, shifted, q - 1)
                for c in range(IC):
                    last = pe.matmul(group[u][:, c, :], g.up_t[:, c * P:c * P + P], f.piece(q), start=True, stop=True)
                last.then_inc(made, 1)
            over_pairs(pe, body)

        @block.scalar
        def _(act):
            def body(j, u):
                q = 2 * j + u
                wait(act, multiplied, q - 1)
                act.activation(gt[:, u, :, :], f.act_piece(q), ACT.Identity, scale=f.inv[:, H_GATED:H_GATED + 1],
                               bias=magic[:, 0:1]).then_inc(again, 1)
                act.wait_ge(made, q + 1)
                act.activation(ut[:, u, :, :], group[u][:, :, :], ACT.Identity, scale=f.inv[:, H_UP:H_UP + 1],
                               bias=magic[:, 0:1]).then_inc(shifted, 1)
            act.wait_ge(dve_st, 1)
            over_pairs(act, body)

        @block.gpsimd
        def _(pool):
            scale_pool(pool, f, 1, peak_ready, top_ready)

        @block.vector
        def _(dve):
            st = Steps(dve, dve_st)

            def peak(q):
                dve.wait_ge(multiplied, q + 1)
                dve.tensor_reduce(f.peak[:, 0, bass.ds(q, 1)], f.act_piece(q), XY, ALU.max,
                                  apply_absolute_value=True).then_inc(peaked, 1)

            def body(j, u):
                q = 2 * j + u
                gv, uv = gt[:, u, :, :], ut[:, u, :, :]
                dve.wait_ge(shifted, q + 1)
                dve.tensor_scalar(uv, uv, MAGIC, None, ALU.subtract).then_inc(gridded, 1)
                if not (isinstance(q, int) and q == 0):
                    peak(q - 1)
                dve.wait_ge(again, q + 1)
                dve.wait_ge(gridded, q + 1)
                dve.scalar_tensor_tensor(out=f.act_piece(q), in0=gv, scalar=MAGIC, in1=uv,
                                         op0=ALU.subtract, op1=ALU.mult).then_inc(multiplied, 1)
            st.then(dve.memset(magic[:, :], MAGIC))
            over_pairs(dve, body)
            peak(QUADS - 1)
            dve.wait_ge(peaked, QUADS)
            scale_dve(dve, st, f, [H_OUT], peak_ready, top_ready, unit_of=(H_GATED, H_UP))


def down(nc, a, g):
    f = g.f
    with ExitStack() as stack:
        m = Memory(nc, stack, "down")
        shifted, rounded, made, added, dve_st = (m.sem(n) for n in ("shifted", "rounded", "made", "added", "dve_st"))
        ot = m.sb("ot", (P, 2, IC, QN))
        magic = m.sb("magic", (P, 1))
        bank = [m.ps(f"o{i}") for i in range(2)]
        block = stack.enter_context(nc.Block())

        @block.scalar
        def _(act):
            def body(j, u):
                q = 2 * j + u
                wait(act, made, q - 1)
                act.activation(ot[:, u, :, :], f.act_piece(q), ACT.Identity, scale=f.inv[:, H_OUT:H_OUT + 1],
                               bias=magic[:, 0:1]).then_inc(shifted, 1)
            act.wait_ge(dve_st, 1)
            over_pairs(act, body)

        @block.tensor
        def _(pe):
            def body(j, u):
                q = 2 * j + u
                pe.wait_ge(rounded, q + 1)
                wait(pe, added, q - 1)
                for t in range(QT):
                    for c in range(IC):
                        last = pe.matmul(bank[u][:, t * P:t * P + P], ot[:, u, c, t * P:t * P + P], g.down_t[:, c, :],
                                         start=(c == 0), stop=(c == IC - 1))
                last.then_inc(made, 1)
            over_pairs(pe, body)

        @block.vector
        def _(dve):
            st = Steps(dve, dve_st)

            def grid(j, u):
                q = 2 * j + u
                dve.wait_ge(shifted, q + 1)
                dve.tensor_scalar(ot[:, u, :, :], ot[:, u, :, :], MAGIC, None, ALU.subtract).then_inc(rounded, 1)

            def body(j, u):
                q = 2 * j + u
                if not (isinstance(q, int) and q == QUADS - 1):
                    grid(j + u, 1 - u)
                dve.wait_ge(made, q + 1)
                dve.scalar_tensor_tensor(out=g.xq(q), in0=bank[u][:, :], scalar=f.scale[:, H_OUT:H_OUT + 1],
                                         in1=g.xq(q), op0=ALU.mult, op1=ALU.add).then_inc(added, 1)
            st.then(dve.memset(magic[:, :], MAGIC))
            grid(0, 0)
            over_pairs(dve, body)


class Half:
    PER = 4

    def __init__(self, j, k):
        self.j, self.k, self.u, self.par = j, k, k // 2, k % 2
        self.n, self.q = 4 * j + k, 2 * j + k // 2

    def shift(self, by):
        dj, k = divmod(self.k + by, self.PER)
        return Half(self.j + dj if dj else self.j, k)

    def outside(self):
        return isinstance(self.n, int) and not 0 <= self.n < 2 * QUADS


def over_halves(eng, body, lead=0, lag=0):
    for n in range(-lead, 0):
        body(Half(*divmod(n, Half.PER)))

    def quad(j, u):
        for par in range(2):
            body(Half(j, 2 * u + par))
    over_pairs(eng, quad)
    for n in range(2 * QUADS, 2 * QUADS + lag):
        body(Half(*divmod(n, Half.PER)))


class Mixer:
    CHANNELS = 16

    def __init__(self, nc, stack):
        m = Memory(nc, stack, "mix")
        self.xc = m.sb("xc", (P, TILES, D))
        self.mv = m.sb("mv", (P, TILES, 2))
        self.tb = m.sb("tb", (P, 2, self.CHANNELS, P))
        self.t_in = [m.sem(f"t_in{u}") for u in range(2)]
        self.wgu = m.sb("wgu", (P, EXPERTS, 2 * D))
        self.wd = m.sb("wd", (P, EXPERTS, D))
        self.bgu = m.sb("bgu", (P, EXPERTS, 2))
        self.bd = m.sb("bd", (EXPERTS, D))
        self.experts_in = m.sem("experts_in")

    def load_blocks(self, sp, g, i, u):
        for b in range(2):
            sp.dma_start(self.tb[b * SEQ:b * SEQ + SEQ, u, :, b * SEQ:b * SEQ + SEQ],
                         g.toeplitz[:, bass.ds(i * self.CHANNELS, self.CHANNELS), :]).then_inc(self.t_in[u], 16)


def attention1(nc, a, g):
    v = g.v
    scale = float(1 / np.sqrt(DH1).astype(np.float32))
    GROUPS = 8
    with ExitStack() as stack:
        m = Memory(nc, stack, "at1")
        ctx_in = [m.sem(f"ctx_in{u}") for u in range(2)]
        stats_ready, rstd_ready, h_ready, hn_ready = (
            m.sem(n) for n in ("stats_ready", "rstd_ready", "h_ready", "hn_ready"))
        ring_ready, ring_evac = m.sem("ring_ready"), m.sem("ring_evac")
        s_ready, s_evac, top_ready, bias_ready = (m.sem(n) for n in ("s_ready", "s_evac", "top_ready", "bias_ready"))
        e_ready, d_ready, inv_ready, prob_ready = (m.sem(n) for n in ("e_ready", "d_ready", "inv_ready", "prob_ready"))
        am_ready, am_evac, u_ready, u_evac = (m.sem(n) for n in ("am_ready", "am_evac", "u_ready", "u_evac"))
        film_ready, fin_done = m.sem("film_ready"), m.sem("fin_done")
        u_out = [m.sem(f"u_out{u}") for u in range(2)]
        pool_st, top_steps = m.sem("pool_st"), m.sem("top_steps")
        TOP_STEPS, FIRST_ROUND = 7, 2

        hq = m.sb("hq", (P, 2, QT, P))
        hn = m.sb("hn", (P, 2, QT, P))
        ht = m.sb("ht", (P, 2, QN))
        ctxn = m.sb("ctxn", (P, 2, QT, C))
        ctxt = m.sb("ctxt", (C + 2, 2, QN))
        qm = m.sb("qm", (C + 2, 2, 2 * QT, H1 * SEQ))
        stats = m.sb("stats", (P, 2, QT, 6))
        mv = m.sb("mv", (P, 2, QT, 2))
        r1 = m.sb("r1", (P, 2, QT, 1))
        again = m.sb("again", (P, 2, QT, 1))
        so = m.sb("so", (P, 2, GROUPS, SEQ))
        rest = m.sb("rest", (P, 2, GROUPS, SEQ))
        df = m.sb("df", (P, 2, GROUPS, SEQ))
        m8 = m.sb("m8", (P, 2, GROUPS, 4, 8))
        bias = m.sb("bias", (P, 2, GROUPS))
        minus_scale = m.sb("minus_scale", (P, GROUPS))
        sm = m.sb("sm", (P, 2, GROUPS))
        pr = m.sb("pr", (P, 2, GROUPS, SEQ))
        amb = m.sb("amb", (P, 2, 2, P))
        ut = m.sb("ut", (C + 1, 2, QN))
        xt = m.sb("xt", (P, 2, 2, D))
        ring = [m.ps(f"ring{i}") for i in range(2)]
        sps = [m.ps(f"s{i}") for i in range(2)]
        amp = m.ps("am")
        up_ = m.ps("u")
        fip = [m.ps(f"f{i}") for i in range(2)]
        block = stack.enter_context(nc.Block())
        RING = 6
        pieces = ((0, 1, 2), (3, 4, 5))
        POOL_CONSTS = 5
        zeroed = m.sem("zeroed")
        ctx_src = a["ctx_768"].rearrange("b s c -> (b s) c").rearrange("(q t p) c -> q p t c", p=P, t=QT)
        mask_src = g.mask_rows.rearrange("m (q n) -> q m n", q=QUADS)

        @block.sync
        def _(sp):
            def load(j, u):
                q = 2 * j + u
                wait(sp, u_ready, 2 * (q - 1))
                sp.dma_start(ctxn[:, u, :, :], at_quad(ctx_src, q)).then_inc(ctx_in[u], 16)
                sp.dma_start(ctxt[C:C + 2, u, :], at_quad(mask_src, q)).then_inc(ctx_in[u], 16)
            over_pairs(sp, load)
            sp.wait_ge(g.taps_stored, 16)
            sp.wait_ge(zeroed, 1)
            for u in range(2):
                v.load_blocks(sp, g, u, u)
            with nc.allow_non_contiguous_dma(reason="small biases, turned"):
                for dst, src in (
                    (v.wgu[:, :, :], a["L1_ffn_gate_up_proj"].rearrange("e h n -> h e n")),
                    (v.wd[:, :, :], a["L1_ffn_down_proj"].rearrange("e h n -> h e n")),
                    (v.bgu[:, :, :], a["L1_ffn_gate_up_proj_bias"].rearrange("e (i k) -> i e k", k=2)),
                    (v.bd[:, :], a["L1_ffn_down_proj_bias"]),
                ):
                    sp.dma_start(dst, src).then_inc(v.experts_in, 16)
            sp.wait_ge(u_out[0], 16 * QUADS // 2)
            sp.wait_ge(u_out[1], 16 * QUADS // 2)

        @block.tensor
        def _(pe):
            def front(x):
                if x.outside():
                    return
                for k in pieces[x.par]:
                    n = RING * x.q + k
                    slot = ring[k % 2]
                    if k == 0:
                        pe.wait_ge(h_ready, x.q + 1)
                    if k == 5:
                        pe.wait_ge(ctx_in[x.u], 32 * (x.j + 1))
                    wait(pe, ring_evac, n - 1 if k != 1 else n)
                    if k == 0:
                        for t in range(QT):
                            last = pe.transpose(slot[:, t * P:t * P + P], hq[:, x.u, t, :], g.ident[:, :])
                    elif k == 5:
                        for t in range(QT):
                            last = pe.transpose(slot[0:C, t * P:t * P + P], ctxn[:, x.u, t, :], g.ident[:, :])
                    else:
                        last = pe.matmul(slot[0:C, :], g.m1[:, k - 1, :], ht[:, x.u, :], start=True, stop=True)
                    last.then_inc(ring_ready, 1)

            def scores(x):
                if x.outside():
                    return
                wait(pe, ring_evac, RING * (x.q + 1))
                wait(pe, s_evac, x.n - 1)
                for i in range(2):
                    t = 2 * x.par + i
                    for b in range(2):
                        tok = slice(t * P + b * SEQ, t * P + b * SEQ + SEQ)
                        for p in range(2):
                            c0 = (4 * i + 2 * p + b) * SEQ
                            last = pe.matmul(sps[x.par][:, c0:c0 + SEQ], qm[:, x.u, 2 * t + b, p * P:p * P + P],
                                             ctxt[:, x.u, tok], start=True, stop=True)
                last.then_inc(s_ready, 1)

            def mean(x):
                if x.outside():
                    return
                pe.wait_ge(prob_ready, x.n + 1)
                wait(pe, am_evac, x.n)
                for i in range(2):
                    for p in range(2):
                        k = 4 * i + 2 * p
                        last = pe.matmul(amp[:, i * SEQ:i * SEQ + SEQ],
                                         pr[:, x.par, k:k + 2, :].rearrange("p a s -> p (a s)"),
                                         g.pairsum[:, :], start=(p == 0), stop=(p == 1))
                last.then_inc(am_ready, 1)

            def attend(x):
                if x.outside():
                    return
                pe.wait_ge(am_evac, x.n + 1)
                wait(pe, u_evac, x.n)
                for i in range(2):
                    last = pe.matmul(up_[0:C, i * P:i * P + P], ctxn[:, x.u, 2 * x.par + i, :], amb[:, x.par, i, :],
                                     start=True, stop=True)
                last.then_inc(u_ready, 1)

            def film(x):
                if x.outside():
                    return
                pe.wait_ge(u_evac, x.n + 1)
                wait(pe, fin_done, x.n - 1)
                for i in range(2):
                    t = 2 * x.par + i
                    last = pe.matmul(fip[x.par][:, 2 * D * i:2 * D * i + 2 * D], ut[:, x.u, t * P:t * P + P],
                                     g.film[:, 0:2 * D], start=True, stop=True)
                last.then_inc(film_ready, 1)

            def body(x):
                front(x.shift(2))
                if isinstance(x.n, int) and x.n == -1:
                    pe.wait_ge(pool_st, POOL_CONSTS)
                scores(x.shift(1))
                mean(x.shift(-1))
                attend(x.shift(-1))
                film(x.shift(-1))
            over_halves(pe, body, lead=2, lag=1)

        @block.scalar
        def _(act):
            def front(x):
                if x.outside():
                    return
                for k in pieces[x.par]:
                    act.wait_ge(ring_ready, RING * x.q + k + 1)
                    slot = ring[k % 2]
                    if k == 0:
                        ins = act.copy(ht[:, x.u, :], slot[:, :])
                    elif k == 5:
                        ins = act.copy(ctxt[0:C, x.u, :], slot[0:C, :])
                    else:
                        ins = act.copy(qm[0:C, x.u, :, (k - 1) * SEQ:k * SEQ],
                                       slot[0:C, :].rearrange("c (b s) -> c b s", s=SEQ))
                    ins.then_inc(ring_evac, 1)

            def take(x):
                if x.outside():
                    return
                act.wait_ge(s_ready, x.n + 1)
                wait(act, d_ready, x.n - 1)
                act.copy(so[:, x.par, :, :], sps[x.par][:, :].rearrange("p (k s) -> p k s", s=SEQ)).then_inc(s_evac, 1)

            def exps(x, of, ready, value):
                if x.outside():
                    return
                act.wait_ge(bias_ready, x.n + 1)
                act.wait_ge(ready, value)
                for k in range(GROUPS):
                    ins = act.activation(of[:, x.par, k, :], of[:, x.par, k, :], ACT.Exp, scale=scale,
                                         bias=bias[:, x.par, k:k + 1])
                ins.then_inc(e_ready, 1)

            def keep_mean(x):
                if x.outside():
                    return
                act.wait_ge(am_ready, x.n + 1)
                am = amp[:, 0:2 * SEQ].rearrange("p (i s) -> p i s", s=SEQ)
                act.copy(amb[0:SEQ, x.par, :, 0:SEQ], am[0:SEQ, :, :])
                act.copy(amb[SEQ:P, x.par, :, SEQ:P], am[SEQ:P, :, :]).then_inc(am_evac, 1)

            def keep_attended(x):
                if x.outside():
                    return
                act.wait_ge(u_ready, x.n + 1)
                if x.par == 0:
                    wait(act, u_out[x.u], 16 * x.j)
                act.copy(ut[0:C, x.u, x.par * 2 * P:(x.par + 1) * 2 * P], up_[0:C, 0:2 * P]).then_inc(u_evac, 1)
                if x.par == 1:
                    act.wait_ge(u_evac, x.n + 1)
                    act.dma_start(g.u_t[:, bass.ds(x.q * QN, QN)], ut[:, x.u, :]).then_inc(u_out[x.u], 16)

            def body(x):
                front(x.shift(2))
                take(x.shift(1))
                keep_mean(x.shift(-1))
                exps(x, so, top_steps, TOP_STEPS * x.n + FIRST_ROUND)
                keep_attended(x.shift(-1))
                exps(x, rest, top_ready, x.n + 1)
            over_halves(act, body, lead=2, lag=1)

        @block.gpsimd
        def _(pool):
            st_rstd, st_prob, st_hn = (Each(pool, m.sem(n), k) for n, k in (("st_rstd", 5), ("st_prob", 1), ("st_hn", 2)))

            def rstds(x):
                if x.outside() or x.par:
                    return
                eps, power = g.eps[:, 0:QT].unsqueeze(2), g.minus_half[:, 0:QT].unsqueeze(2)
                var, r = mv[:, x.u, :, 1:2], r1[:, x.u, :, :]
                pool.wait_ge(stats_ready, x.q + 1)
                link = st_rstd.at(x.q)
                link.then(pool.tensor_tensor(r, var, eps, ALU.add))
                pool.tensor_tensor(r, r, power, ALU.pow).then_inc(rstd_ready, 1)
                pool.wait_ge(rstd_ready, x.q + 1)
                link.then(pool.tensor_tensor(var, var, r, ALU.mult))
                link.then(pool.tensor_tensor(var, var, r, ALU.mult))
                link.then(pool.tensor_tensor(var, var, eps, ALU.add))
                link.then(pool.tensor_tensor(again[:, x.u, :, :], var, power, ALU.pow))

            def norm_in(x):
                if x.outside() or x.par:
                    return
                wait(pool, h_ready, x.q + 1)
                wait(pool, fin_done, 2 * (x.q - 1))
                n = hn[:, x.u, :, :]
                link = st_hn.at(x.q)
                link.then(pool.tensor_tensor(n, hq[:, x.u, :, :], again[:, x.u, :, :].to_broadcast([P, QT, D]), ALU.mult))
                link.then(pool.tensor_tensor(n, n, g.wide[:, 0:1, :].to_broadcast([P, QT, D]), ALU.mult))
                pool.tensor_tensor(n, n, g.wide[:, 1:2, :].to_broadcast([P, QT, D]), ALU.add).then_inc(hn_ready, 1)

            def biases(x):
                if x.outside():
                    return
                pool.wait_ge(top_steps, TOP_STEPS * x.n + FIRST_ROUND)
                pool.tensor_tensor(bias[:, x.par, :], m8[:, x.par, :, 0, 0:1].rearrange("p a b -> p (a b)"),
                                   minus_scale[:, :], ALU.mult).then_inc(bias_ready, 1)

            def probs(x):
                if x.outside():
                    return
                pool.wait_ge(inv_ready, x.n + 1)
                s = sm[:, x.par, :].rearrange("p (i a b) -> p i a b", a=2, b=2)
                tm = g.tmask[:, bass.ds(4 * x.n, 4)].rearrange("p (i b) -> p i b", b=2).unsqueeze(2)
                st_prob.at(x.n).then(pool.tensor_tensor(s, s, tm.to_broadcast([P, 2, 2, 2]), ALU.mult))
                wait(pool, am_ready, x.n - 1)
                pool.tensor_tensor(pr[:, x.par, :, :], df[:, x.par, :, :],
                                   sm[:, x.par, :].unsqueeze(2).to_broadcast([P, GROUPS, SEQ]), ALU.mult).then_inc(prob_ready, 1)

            def differences(x):
                if x.outside():
                    return
                pool.wait_ge(e_ready, 2 * x.n + 2)
                pool.tensor_tensor(df[:, x.par, :, :], so[:, x.par, :, :], rest[:, x.par, :, :],
                                   ALU.subtract).then_inc(d_ready, 1)

            def body(x):
                biases(x)
                rstds(x.shift(3))
                probs(x.shift(-1))
                norm_in(x)
                differences(x)
            body(Half(*divmod(-3, Half.PER)))
            st = Steps(pool, pool_st)
            st.then(pool.memset(qm[C:C + 2, :, :, :], 1.0))
            st.then(pool.memset(qm[C:C + 1, :, :, :], 0.0))
            st.then(pool.memset(ut[C:C + 1, :, :], 1.0))
            st.then(pool.memset(amb[:, :, :, :], 0.0))
            st.then(pool.memset(minus_scale[:, :], -scale))
            assert st.n == POOL_CONSTS
            pool.memset(v.tb[:, :, :, :], 0.0).then_inc(zeroed, 1)
            over_halves(pool, body, lead=2, lag=1)

        @block.vector
        def _(dve):
            st_top = Each(dve, top_steps, TOP_STEPS)
            st_stat, st_sum, st_fin = (
                Each(dve, m.sem(n), k) for n, k in (("st_stat", 1), ("st_sum", 1), ("st_fin", 1)))

            def carry(cell):
                dve.memset(g.carry[:, cell:cell + 1], 0.0)

            def stats_of(x):
                if x.outside() or x.par:
                    return
                for t in range(QT):
                    last = dve.bn_stats(stats[:, x.u, t, :], g.xt(x.q, t))
                st_stat.at(x.q).done(last)

            def means_of(x):
                if x.outside() or x.par:
                    return
                wait(dve, hn_ready, x.q - 1)
                dve.wait_ge(st_stat.sem, x.q + 1)
                carry(2)
                for t in range(QT):
                    last = dve.bn_aggr(mv[:, x.u, t, :], stats[:, x.u, t, :])
                last.then_inc(stats_ready, 1)

            def norm(x):
                if x.outside() or x.par:
                    return
                wait(dve, ring_ready, RING * (x.q - 2) + 1)
                dve.wait_ge(rstd_ready, x.q + 1)
                for t in range(QT):
                    last = dve.tensor_scalar(hq[:, x.u, t, :], g.xt(x.q, t), mv[:, x.u, t, 0:1], r1[:, x.u, t, :],
                                             ALU.subtract, ALU.mult)
                last.then_inc(h_ready, 1)
                dve.scalar_tensor_tensor(out=v.mv[:, bass.ds(QT * x.q, QT), 0:1], in0=mv[:, x.u, :, 0:1], scalar=-1.0,
                                         in1=r1[:, x.u, :, :], op0=ALU.mult, op1=ALU.mult)
                dve.tensor_copy(v.mv[:, bass.ds(QT * x.q, QT), 1:2], r1[:, x.u, :, :])

            def total(x):
                if x.outside():
                    return
                dve.wait_ge(d_ready, x.n + 1)
                st_sum.at(x.n).done(dve.tensor_reduce(sm[:, x.par, :], df[:, x.par, :, :], X, ALU.add))

            def inverse(x):
                if x.outside():
                    return
                dve.wait_ge(st_sum.sem, x.n + 1)
                dve.reciprocal(sm[:, x.par, :], sm[:, x.par, :]).then_inc(inv_ready, 1)

            def out_scale(x):
                if x.outside():
                    return
                dve.wait_ge(hn_ready, x.q + 1)
                dve.wait_ge(film_ready, x.n + 1)
                fi = fip[x.par][:, :].rearrange("p (i c d) -> p i c d", i=2, c=2)
                st_fin.at(x.n).done(dve.tensor_tensor(xt[:, x.par, :, :], fi[:, :, 0, :],
                                                      hn[:, x.u, 2 * x.par:2 * x.par + 2, :], ALU.mult))

            def out_shift(x):
                if x.outside():
                    return
                dve.wait_ge(st_fin.sem, x.n + 1)
                fi = fip[x.par][:, :].rearrange("p (i c d) -> p i c d", i=2, c=2)
                dve.tensor_tensor(v.xc[:, bass.ds(2 * x.n, 2), :], fi[:, :, 1, :], xt[:, x.par, :, :],
                                  ALU.add).then_inc(fin_done, 1)

            def body(x):
                fill = ((stats_of, 3), (means_of, 3), (total, -1), (inverse, -1),
                        (out_scale, -2), (out_shift, -2), (norm, 3))
                if x.outside():
                    for step, by in fill:
                        step(x.shift(by))
                    return
                wait(dve, d_ready, x.n - 1)
                dve.wait_ge(s_evac, x.n + 1)
                carry(0)
                link = st_top.at(x.n)
                for i in range(8):
                    r = i // 2
                    src = so if r == 0 else rest
                    for k in range(GROUPS):
                        if i % 2 == 0:
                            last = dve.max(m8[:, x.par, k, r, :], src[:, x.par, k, :])
                        else:
                            last = dve.match_replace(rest[:, x.par, k, :], m8[:, x.par, k, r, :], src[:, x.par, k, :], -3.0e38)
                    if i < 7:
                        link.done(last)
                        step, by = fill[i]
                        step(x.shift(by))
                        dve.wait_ge(link.sem, link.now())
                        carry(1)
                last.then_inc(top_ready, 1)
            over_halves(dve, body, lead=3, lag=2)


def at_quad(src, q):
    if isinstance(q, int):
        return src[q]
    s = src[bass.ds(q, 1)]
    return s.rearrange("a p t c -> (a p) t c") if len(s.shape) == 4 else s.rearrange("a m n -> (a m) n")


def filter_tokens(nc, a, g):
    v = g.v
    GR = v.CHANNELS
    with ExitStack() as stack:
        m = Memory(nc, stack, "fil")
        made, moved = m.sem("made"), m.sem("moved")
        bank = [m.ps(f"y{i}", (P, GR * TILES)) for i in range(2)]
        block = stack.enter_context(nc.Block())
        groups = D // GR

        @block.sync
        def _(sp):
            def load(j, u):
                i = 2 * j + u
                if isinstance(i, int) and i < 2:
                    return
                sp.wait_ge(made, i - 1)
                v.load_blocks(sp, g, i, u)
            over_pairs(sp, load, pairs=groups // 2)

        @block.tensor
        def _(pe):
            def body(j, u):
                i = 2 * j + u
                pe.wait_ge(v.t_in[u], 32 * (j + 1))
                wait(pe, moved, i - 1)
                for k in range(GR):
                    last = pe.matmul(bank[u][:, k * TILES:k * TILES + TILES], v.tb[:, u, k, :],
                                     v.xc[:, :, bass.ds(i * GR + k, 1)].rearrange("p t a -> p (t a)"),
                                     start=True, stop=True)
                last.then_inc(made, 1)
            over_pairs(pe, body, pairs=groups // 2)

        @block.scalar
        def _(act):
            def body(j, u):
                i = 2 * j + u
                act.wait_ge(made, i + 1)
                act.copy(v.xc[:, :, bass.ds(i * GR, GR)].rearrange("p t c -> p c t"),
                         bank[u][:, :].rearrange("p (c t) -> p c t", t=TILES)).then_inc(moved, 1)
            over_pairs(act, body, pairs=groups // 2)


def mix(nc, a, g):
    v = g.v
    with ExitStack() as stack:
        m = Memory(nc, stack, "mx")
        u_in = [m.sem(f"u_in{u}") for u in range(2)]
        out_done = m.sem("out_done")
        film_ready, film_used, stats_ready, rstd_ready, n_ready, turned, turn_evac = (
            m.sem(n) for n in ("film_ready", "film_used", "stats_ready", "rstd_ready", "n_ready", "turned", "turn_evac"))
        hid_ready, hid_done, back_ready, back_used, resid_ready, last_ready, x_ready = (
            m.sem(n) for n in ("hid_ready", "hid_done", "back_ready", "back_used", "resid_ready", "last_ready", "x_ready"))
        h_ready = m.sem("h_ready")
        first_steps = m.sem("dve_first")
        nb = m.sb("nb", (P, 2, QT, 1))
        nb2 = m.sb("nb2", (P, 2, QT, 1))
        ut = m.sb("ut", (C + 1, 2, QN))
        mvs = m.sb("mvs", (P, 2, QT, 2))
        hq = m.sb("hq", (P, 2, QT, D))
        yq = m.sb("yq", (P, 2, QT, D))
        xq = m.sb("xq", (P, 2, QT, D))
        xb = m.sb("xb", (P, 2, QT, D))
        total = m.sb("total", (P, 2, QT, D))
        nq = m.sb("nq", (P, 2, QT, D))
        lq = m.sb("lq", (P, 2, QT, D))
        nt = m.sb("nt", (P, 2, QN))
        hid = m.sb("hid", (P, 2, 4, QN))
        stats = m.sb("stats", (P, 2, QT, 6))
        stats2 = m.sb("stats2", (P, 2, QT, 6))
        mv = m.sb("mv", (P, 2, QT, 2))
        mv2 = m.sb("mv2", (P, 2, QT, 2))
        fop = m.ps("fo", (P, 2, 512))
        tp = m.ps("t")
        hp = [m.ps(f"h{i}") for i in range(4)]
        bp = m.ps("b")
        block = stack.enter_context(nc.Block())
        out = g.out.rearrange("b s d -> (b s) d").rearrange("(q t p) d -> q p t d", p=P, t=QT)

        def last_quad(q):
            return isinstance(q, int) and q == QUADS - 1

        def norm_count(q):
            return q if isinstance(q, int) and q < 2 else 2 * q - 2

        def last_count(q):
            return QUADS + q if isinstance(q, int) and q >= QUADS - 3 else 2 * q + 3

        AHEAD = 2

        @block.sync
        def _(sp):
            def store(j, u):
                q = 2 * j + u
                sp.wait_ge(x_ready, AHEAD + q + 1)
                sp.dma_start(at_quad(out, q), g.xq(q).rearrange("p (t d) -> p t d", d=D)).then_inc(out_done, 16)
            over_pairs(sp, store)
            sp.wait_ge(out_done, 16 * QUADS)

        @block.tensor
        def _(pe):
            def film(j, u):
                q = 2 * j + u
                pe.wait_ge(u_in[u], 16 * (j + 1))
                wait(pe, film_used, q)
                for t in range(QT):
                    last = pe.matmul(fop[:, t // 2, 256 * (t % 2):256 * (t % 2) + 256], ut[:, u, t * P:t * P + P],
                                     g.film[:, 2 * D:], start=True, stop=True)
                last.then_inc(film_ready, 1)

            def back(q, u):
                wait(pe, back_used, q)
                pe.wait_ge(hid_done, 4 * (q + 1))
                for t in range(QT):
                    for c in range(4):
                        last = pe.matmul(bp[:, t * P:t * P + P], hid[:, u, c, t * P:t * P + P], g.w2[:, c, :],
                                         start=(c == 0), stop=(c == 3))
                last.then_inc(back_ready, 1)

            def body(j, u):
                q = 2 * j + u
                if not last_quad(q):
                    film(j + u, 1 - u)
                pe.wait_ge(n_ready, q + 1)
                wait(pe, turn_evac, q)
                for t in range(QT):
                    last = pe.transpose(tp[:, t * P:t * P + P], nq[:, u, t, :], g.ident[:, :])
                last.then_inc(turned, 1)
                if not (isinstance(q, int) and q == 0):
                    back(q - 1, 1 - u)
                pe.wait_ge(turn_evac, q + 1)
                for c in range(4):
                    wait(pe, hid_done, 4 * (q - 1) + c + 1)
                    pe.matmul(hp[c][:, :], g.w1[:, c * P:c * P + P], nt[:, u, :], start=True, stop=True).then_inc(hid_ready, 1)
            film(0, 0)
            over_pairs(pe, body)
            back(QUADS - 1, 1)

        @block.scalar
        def _(act):
            st_mv = Each(act, m.sem("act_mv"), 1)

            def apply(out, x, r, bias):
                for t in range(QT):
                    last = act.activation(out[:, t, :], x[t], ACT.Identity, scale=r[:, t, :], bias=bias[:, t, :])
                return last

            def normed_x(j, u):
                q = 2 * j + u
                if not (isinstance(q, int) and q < 2):
                    act.wait_ge(first_steps, 2 * (q - 2) + 1)
                st_mv.at(q).then(act.copy(mvs[:, u, :, :], v.mv[:, bass.ds(QT * q, QT), :]))
                apply(hq[:, u, :, :], [g.xt(q, t) for t in range(QT)], mvs[:, u, :, 1:2],
                      mvs[:, u, :, 0:1]).then_inc(h_ready, 1)

            def load_context(j, u):
                q = 2 * j + u
                wait(act, film_ready, q - 1)
                act.dma_start(ut[:, u, :], g.u_t[:, bass.ds(q * QN, QN)]).then_inc(u_in[u], 16)

            def norm(j, u):
                q = 2 * j + u
                act.wait_ge(rstd_ready, norm_count(q) + 1)
                apply(nq[:, u, :, :], [xq[:, u, t, :] for t in range(QT)], mv[:, u, :, 1:2], nb[:, u, :, :]).then_inc(n_ready, 1)

            def last_norm(j, u):
                q = 2 * j + u
                act.wait_ge(rstd_ready, last_count(q) + 1)
                act.wait_ge(x_ready, AHEAD + q - 1)
                apply(lq[:, u, :, :], [total[:, u, t, :] for t in range(QT)], mv2[:, u, :, 1:2],
                      nb2[:, u, :, :]).then_inc(last_ready, 1)

            def body(j, u):
                q = 2 * j + u
                norm(j, u)
                act.wait_ge(turned, q + 1)
                act.activation(nt[:, u, :], tp[:, :], ACT.Identity, scale=g.ffn_g[:, 0:1],
                               bias=g.ffn_b[:, 0:1]).then_inc(turn_evac, 1)
                if not (isinstance(q, int) and q < 2):
                    last_norm(j - 1, u)
                if not last_quad(q):
                    normed_x(j + u, 1 - u)
                if not (isinstance(q, int) and q >= QUADS - 2):
                    load_context(j + 1, u)
                wait(act, back_ready, q - 1)
                for c in range(4):
                    act.wait_ge(hid_ready, 4 * q + c + 1)
                    act.activation(hid[:, u, c, :], hp[c][:, :], ACT.Gelu, bias=g.b1[:, c:c + 1]).then_inc(hid_done, 1)
            act.sem_inc(last_ready, AHEAD)
            load_context(0, 0)
            load_context(0, 1)
            normed_x(0, 0)
            over_pairs(act, body)
            last_norm(QUADS // 2 - 1, 0)
            last_norm(QUADS // 2 - 1, 1)

        @block.gpsimd
        def _(pool):
            st_first, st_last = Each(pool, m.sem("pool_first"), 3), Each(pool, m.sem("pool_last"), 5)

            def rstd_and_bias(mv, nb, link, count):
                pool.wait_ge(stats_ready, count + 1)
                link.done(pool.tensor_tensor(nb, mv[:, :, 0:1], g.minus_one[:, :].unsqueeze(2), ALU.mult))
                link.then(pool.tensor_tensor(mv[:, :, 1:2], mv[:, :, 1:2], g.eps[:, 0:QT].unsqueeze(2), ALU.add))
                link.then(pool.tensor_tensor(mv[:, :, 1:2], mv[:, :, 1:2], g.minus_half[:, 0:QT].unsqueeze(2), ALU.pow))
                pool.tensor_tensor(nb, nb, mv[:, :, 1:2], ALU.mult).then_inc(rstd_ready, 1)

            def weigh(j, u):
                q = 2 * j + u
                st = st_last.at(q)
                rstd_and_bias(mv2[:, u, :, :], nb2[:, u, :, :], st, last_count(q))
                pool.wait_ge(last_ready, AHEAD + q + 1)
                n = lq[:, u, :, :]
                st.then(pool.tensor_tensor(n, n, g.wide[:, 3:4, :].to_broadcast([P, QT, D]), ALU.mult))
                st.done(pool.tensor_tensor(n, n, g.wide[:, 4:5, :].to_broadcast([P, QT, D]), ALU.add))

            def join(j, u):
                q = 2 * j + u
                pool.wait_ge(st_last.sem, 5 * (q + 1))
                xs = g.xq(q).rearrange("p (t d) -> p t d", d=D)
                pool.tensor_tensor(xs, xs, lq[:, u, :, :], ALU.add).then_inc(x_ready, 1)

            def body(j, u):
                q = 2 * j + u
                rstd_and_bias(mv[:, u, :, :], nb[:, u, :, :], st_first.at(q), norm_count(q))
                if not (isinstance(q, int) and q < 2):
                    weigh(j - 1, u)
                if not (isinstance(q, int) and q < 2):
                    join(j - 1, u)
            pool.sem_inc(x_ready, AHEAD)
            over_pairs(pool, body)
            j = QUADS // 2 - 1
            for u in range(2):
                weigh(j, u)
                join(j, u)

        @block.vector
        def _(dve):
            st_first = Each(dve, first_steps, 2)
            st_y, st_last = Each(dve, m.sem("dve_y"), 1), Each(dve, m.sem("dve_last"), 1)

            def filtered(j, u):
                q = 2 * j + u
                dve.wait_ge(film_ready, q + 1)
                fo = fop[:, :, :].rearrange("p a (b n) -> p (a b) n", n=2 * D)
                st_y.at(q).then(dve.tensor_tensor(yq[:, u, :, :], fo[:, :, 0:D], v.xc[:, bass.ds(QT * q, QT), :], ALU.mult))
                dve.tensor_tensor(yq[:, u, :, :], fo[:, :, D:2 * D], yq[:, u, :, :], ALU.add).then_inc(film_used, 1)

            def first(j, u):
                q = 2 * j + u
                st = st_first.at(q)
                dve.wait_ge(h_ready, q + 1)
                wait(dve, n_ready, q - 1)
                dve.wait_ge(film_used, q + 1)
                st.then(dve.tensor_tensor(xq[:, u, :, :], yq[:, u, :, :], hq[:, u, :, :], ALU.add))
                tiles = [xq[:, u, t, :] for t in range(QT)]
                norm_stats(dve, g.carry[:, 0:1], st, tiles, stats[:, u, :, :], mv[:, u, :, :], stats_ready)

            def second(j, u):
                q = 2 * j + u
                st = st_last.at(q)
                dve.wait_ge(last_ready, AHEAD + q - 1)
                dve.wait_ge(back_ready, q + 1)
                dve.wait_ge(resid_ready, q + 1)
                dve.tensor_tensor(total[:, u, :, :], bp[:, :].rearrange("p (t d) -> p t d", d=D), xb[:, u, :, :],
                                  ALU.add).then_inc(back_used, 1)
                dve.wait_ge(back_used, q + 1)
                tiles = [total[:, u, t, :] for t in range(QT)]
                norm_stats(dve, g.carry[:, 2:3], st, tiles, stats2[:, u, :, :], mv2[:, u, :, :], stats_ready)

            def residual(j, u):
                q = 2 * j + u
                wait(dve, back_used, q - 1)
                dve.wait_ge(first_steps, 2 * q + 1)
                dve.tensor_tensor(xb[:, u, :, :], xq[:, u, :, :], g.wide[:, 2:3, :].to_broadcast([P, QT, D]),
                                  ALU.add).then_inc(resid_ready, 1)

            def body(j, u):
                q = 2 * j + u
                first(j, u)
                if not last_quad(q):
                    filtered(j + u, 1 - u)
                if not (isinstance(q, int) and q < 2):
                    second(j - 1, u)
                residual(j, u)
            filtered(0, 0)
            over_pairs(dve, body)
            for u in range(2):
                second(QUADS // 2 - 1, u)


def experts(nc, a, g):
    n_tok = a["L1_ffn_router_indices"].shape[0]
    NT = n_tok // P
    with ExitStack() as stack:
        m = Memory(nc, stack, "ex")
        loaded, stats_ready, rstd_ready, xn_ready, dve_st, pool_st, act_st, pe_st, out_done = (
            m.sem(n) for n in ("loaded", "stats_ready", "rstd_ready", "xn_ready", "dve_st", "pool_st", "act_st", "pe_st", "out_done"))
        gu_ready, limited, sig_ready, inter_ready, down_ready, summed = (
            m.sem(n) for n in ("gu_ready", "limited", "sig_ready", "inter_ready", "down_ready", "summed"))
        wgu, wd, bgu, bd = g.v.wgu, g.v.wd, g.v.bgu, g.v.bd
        route = m.sb("route", (P, NT, 2), I32)
        routef = m.sb("routef", (P, NT, 2))
        weight = m.sb("weight", (P, NT, EXPERTS))
        iota = m.sb("iota", (P, EXPERTS))
        hit = m.sb("hit", (P, NT, 2, EXPERTS))
        coef = m.sb("coef", (P, NT, EXPERTS))
        coeft = m.sb("coeft", (EXPERTS, NT, P))
        xn = m.sb("xn", (P, NT, D))
        xnt = m.sb("xnt", (P, NT * P))
        stats = m.sb("stats", (P, NT, 6))
        mv = m.sb("mv", (P, NT, 2))
        gu = m.sb("gu", (P, 2, 2, NT * P))
        sg = m.sb("sg", (P, 2, NT * P))
        inter = m.sb("inter", (P, 2, NT * P))
        tp, cp = m.ps("t"), m.ps("c")
        gp = [m.ps(f"g{i}") for i in range(2)]
        dp = [m.ps(f"d{i}") for i in range(2)]
        bp = m.ps("b")
        block = stack.enter_context(nc.Block())
        LOADS, WEIGHT_LOADS = 2, 4
        COEF_AT = 4

        @block.sync
        def _(sp):
            for dst, src in (
                (route[:, :, :], a["L1_ffn_router_indices"].rearrange("(t p) k -> p t k", p=P)),
                (weight[:, :, :], a["L1_ffn_routing_weights"].rearrange("(t p) e -> p t e", p=P)),
            ):
                sp.dma_start(dst, src).then_inc(loaded, 16)
            sp.wait_ge(summed, NT * EXPERTS + NT)
            sp.dma_start(g.out.rearrange("b s d -> (b s) d").rearrange("(t p) d -> p t d", p=P)[:, 0:NT, :],
                         g.x[:, 0:NT, :]).then_inc(out_done, 16)
            sp.wait_ge(out_done, 16)

        @block.gpsimd
        def _(pool):
            st = Steps(pool, pool_st)
            for e in range(EXPERTS):
                st.then(pool.memset(iota[:, e:e + 1], float(e)))
            pool.wait_ge(stats_ready, 1)
            st.then(pool.tensor_tensor(mv[:, :, 1:2], mv[:, :, 1:2], g.eps[:, 0:NT].unsqueeze(2), ALU.add))
            pool.tensor_tensor(mv[:, :, 1:2], mv[:, :, 1:2], g.minus_half[:, 0:NT].unsqueeze(2), ALU.pow).then_inc(rstd_ready, 1)

        @block.tensor
        def _(pe):
            pe.wait_ge(xn_ready, NT)
            for t in range(NT):
                last = pe.transpose(tp[:, t * P:t * P + P], xn[:, t, :], g.ident[:, :])
            last.then_inc(pe_st, 1)
            pe.wait_ge(dve_st, COEF_AT)
            for t in range(NT):
                last = pe.transpose(cp[0:EXPERTS, t * P:t * P + P], coef[:, t, :], g.ident[:, :])
            last.then_inc(pe_st, 1)
            pe.wait_ge(g.v.experts_in, 16 * WEIGHT_LOADS)

            def into(e):
                wait(pe, limited, 2 * (e - 1))
                w = wgu[:, e, :].rearrange("p (i k) -> p i k", k=2)
                for k in range(2):
                    last = pe.matmul(gp[e % 2][:, k * NT * P:(k + 1) * NT * P], w[:, :, k], xnt[:, :], start=True, stop=True)
                last.then_inc(gu_ready, 1)

            def outof(e):
                pe.wait_ge(inter_ready, e + 1)
                wait(pe, summed, NT * (e - 1) + NT)
                for t in range(NT):
                    last = pe.matmul(dp[e % 2][:, t * P:t * P + P], inter[:, e % 2, t * P:t * P + P], wd[:, e, :],
                                     start=True, stop=True)
                last.then_inc(down_ready, 1)
            pe.wait_ge(act_st, 2)
            for t in range(NT):
                last = pe.matmul(bp[:, t * P:t * P + P], coeft[:, t, :], bd[:, :], start=True, stop=True)
            last.then_inc(pe_st, 1)
            into(0)
            for e in range(EXPERTS):
                if e + 1 < EXPERTS:
                    into(e + 1)
                outof(e)

        @block.scalar
        def _(act):
            st = Steps(act, act_st)
            act.wait_ge(pe_st, 1)
            st.then(act.copy(xnt[:, :], tp[:, 0:NT * P]))
            act.wait_ge(pe_st, 2)
            st.then(act.copy(coeft[:, :, :], cp[0:EXPERTS, 0:NT * P].rearrange("p (t n) -> p t n", n=P)))
            for e in range(EXPERTS):
                act.wait_ge(limited, 2 * e + 1)
                wait(act, inter_ready, e - 1)
                act.activation(sg[:, e % 2, :], gu[:, e % 2, 0, :], ACT.Sigmoid, scale=1.702).then_inc(sig_ready, 1)

        @block.vector
        def _(dve):
            st = Steps(dve, dve_st)
            dve.wait_ge(loaded, 16 * LOADS)
            dve.wait_ge(pool_st, EXPERTS)
            st.then(dve.tensor_copy(routef[:, :, :], route[:, :, :]))
            for t in range(NT):
                for k in range(2):
                    last = dve.tensor_scalar(hit[:, t, k, :], iota[:, :], routef[:, t, k:k + 1], None, ALU.is_equal)
            st.then(last)
            st.then(dve.tensor_tensor(hit[:, :, 0, :], hit[:, :, 0, :], hit[:, :, 1, :], ALU.add))
            st.then(dve.tensor_tensor(coef[:, :, :], hit[:, :, 0, :], weight[:, :, :], ALU.mult))
            for t in range(NT):
                last = dve.bn_stats(stats[:, t, :], g.x[:, t, :])
            st.then(last)
            assert st.n == COEF_AT + 1
            for t in range(NT):
                last = dve.bn_aggr(mv[:, t, :], stats[:, t, :])
            last.then_inc(stats_ready, 1)
            dve.wait_ge(rstd_ready, 1)
            for t in range(NT):
                dve.tensor_scalar(xn[:, t, :], g.x[:, t, :], mv[:, t, 0:1], mv[:, t, 1:2],
                                  ALU.subtract, ALU.mult).then_inc(xn_ready, 1)
            dve.wait_ge(pe_st, 3)
            dve.wait_ge(xn_ready, NT)
            for t in range(NT):
                dve.tensor_tensor(g.x[:, t, :], g.x[:, t, :], bp[:, t * P:t * P + P], ALU.add).then_inc(summed, 1)

            dve.wait_ge(g.v.experts_in, 16 * WEIGHT_LOADS)

            def limit(e):
                dve.wait_ge(gu_ready, e + 1)
                gv, uv = gu[:, e % 2, 0, :], gu[:, e % 2, 1, :]
                dve.tensor_scalar(gv, gp[e % 2][:, 0:NT * P], bgu[:, e, 0:1], 7.0, ALU.add, ALU.min).then_inc(limited, 1)
                dve.tensor_scalar(uv, gp[e % 2][:, NT * P:], bgu[:, e, 1:2], 7.0, ALU.add, ALU.min).then_inc(limited, 1)
                dve.wait_ge(limited, 2 * e + 2)
                st.then(dve.tensor_scalar(uv, uv, -7.0, 1.0, ALU.max, ALU.add))
                st.then(dve.tensor_tensor(uv, uv, gv, ALU.mult))
                dve.wait_ge(sig_ready, e + 1)
                wait(dve, down_ready, e - 1)
                dve.tensor_tensor(inter[:, e % 2, :], uv, sg[:, e % 2, :], ALU.mult).then_inc(inter_ready, 1)

            def join(e):
                dve.wait_ge(down_ready, e + 1)
                dve.wait_ge(summed, NT * (e + 1))
                for t in range(NT):
                    dve.scalar_tensor_tensor(out=g.x[:, t, :], in0=dp[e % 2][:, t * P:t * P + P],
                                             scalar=coef[:, t, e:e + 1], in1=g.x[:, t, :],
                                             op0=ALU.mult, op1=ALU.add).then_inc(summed, 1)
            for e in range(EXPERTS):
                limit(e)
                if e > 0:
                    join(e - 1)
            join(EXPERTS - 1)


class Resident:

    def __init__(self, nc, stack):
        m = Memory(nc, stack, "g")
        self.x = m.sb("x", (P, TILES, P))
        self.ident = m.sb("ident", (P, P))
        self.pairsum = m.sb("pairsum", (P, SEQ))
        self.minus_half = m.sb("minus_half", (P, 8))
        self.carry = m.sb("carry", (P, 4))
        self.eps = m.sb("eps", (P, 8))
        self.minus_one = m.sb("minus_one", (P, 4))
        self.m0 = m.sb("m0", (P, H0, C))
        self.n0 = m.sb("n0", (C + 1, H0, D))
        self.m1 = m.sb("m1", (P, H1, C))
        self.film = m.sb("film", (C + 1, 4 * D))
        self.gate_t = m.sb("gate_t", (P, INTER))
        self.up_t = m.sb("up_t", (P, INTER))
        self.down_t = m.sb("down_t", (P, IC, D))
        self.w1 = m.sb("w1", (P, HID))
        self.w2 = m.sb("w2", (P, 4, D))
        self.b1 = m.sb("b1", (P, 4))
        self.ffn_g = m.sb("ffn_g", (P, 1))
        self.ffn_b = m.sb("ffn_b", (P, 1))
        self.wide = m.sb("wide", (P, 5, D))
        self.tmask = m.sb("tmask", (P, BATCH))
        self.mask_rows = nc.dram_tensor("mask_rows", [2, TOK], F32, kind="Internal").ap()
        self.taps_sb = m.sb("taps_sb", (P, 2 * SEQ))
        self.taps_stored = m.sem("taps_stored")
        self.x_in = [m.sem(f"x_in{i}") for i in range(3)]
        SKEW = SEQ * (2 * SEQ + 1)
        skewed = nc.dram_tensor("skewed_taps", [D, SKEW], F32, kind="Internal").ap()
        self.taps_out = skewed.rearrange("d (j m) -> d j m", j=SEQ)[:, :, 0:2 * SEQ]
        self.toeplitz = bass.AP(skewed.tensor, SEQ, [[2 * SEQ, SEQ], [SKEW, D], [1, SEQ]])
        self.u_t = nc.dram_tensor("u_t", [C + 1, TOK], F32, kind="Internal").ap()

    def xt(self, q, t):
        flat = self.x[:, :, :].rearrange("p t d -> p (t d)")
        return flat[:, bass.ds(q * QN + t * P, P)] if not isinstance(q, int) else flat[:, q * QN + t * P:q * QN + t * P + P]

    def xq(self, q):
        flat = self.x[:, :, :].rearrange("p t d -> p (t d)")
        return flat[:, bass.ds(q * QN, QN)] if not isinstance(q, int) else flat[:, q * QN:q * QN + QN]


FFN = [gate_max, gate, up, down]
ATTENTION1 = [attention1, filter_tokens, mix]


def program(nc, a, out, stages=None):
    with ExitStack() as stack:
        g = Resident(nc, stack)
        g.out = out

        def run(some):
            for stage in some:
                if stages is None or stage in stages:
                    stage(nc, a, g)
        with ExitStack() as ffn:
            g.f = Quantised(nc, ffn)
            with ExitStack() as tables:
                g.s4 = FilterTables(nc, tables, g.taps_sb)
                run([prepare, attention0])
            g.f.hold_act(nc, ffn)
            run(FFN)
        with ExitStack() as second:
            g.v = Mixer(nc, second)
            run(ATTENTION1 + [experts])
        if stages and mix not in stages and experts not in stages:
            dump(nc, a, g, out)


def dump(nc, a, g, out):
    with ExitStack() as stack:
        m = Memory(nc, stack, "dump")
        done = m.sem("done")
        block = stack.enter_context(nc.Block())

        @block.sync
        def _(sp):
            sp.dma_start(out.rearrange("b s d -> (b s) d").rearrange("(t p) d -> p t d", p=P), g.x[:, :, :]).then_inc(done, 16)
            sp.wait_ge(done, 16)


_NAMES = [
    "x", "ctx_768", "mask_BxS2_bk0", "mask_BxS_bf1", "mask_BxS2_bf1",
    "L0_xattn_W_q", "L0_xattn_W_k", "L0_xattn_W_v", "L0_xattn_W_o", "L0_xattn_b_o",
    "L0_ffn_w_gate", "L0_ffn_w_up", "L0_ffn_w_down",
    "L1_xattn_Wq", "L1_xattn_Wk", "L1_xattn_Wv", "L1_xattn_W_film_in", "L1_xattn_b_film_in",
    "L1_xattn_W_film_out", "L1_xattn_b_film_out", "L1_xattn_g_norm_in", "L1_xattn_b_norm_in",
    "L1_xattn_g_norm_out", "L1_xattn_b_norm_out", "L1_xattn_g_ffn", "L1_xattn_b_ffn",
    "L1_xattn_W1", "L1_xattn_b1", "L1_xattn_W2", "L1_xattn_b2", "L1_xattn_log_dt",
    "L1_xattn_A_re", "L1_xattn_A_im", "L1_xattn_C_re", "L1_xattn_C_im", "L1_xattn_D_skip",
    "L1_xattn_mod_gate", "L1_ffn_router_indices", "L1_ffn_routing_weights",
    "L1_ffn_gate_up_proj", "L1_ffn_gate_up_proj_bias", "L1_ffn_down_proj", "L1_ffn_down_proj_bias",
]


def kernel(**inputs):
    import concourse.bacc as bacc
    from concourse.bass_utils import run_bass_kernel_spmd

    nc = bacc.Bacc("TRN2", target_bir_lowering=False, num_devices=1)
    arrays, args = {}, {}
    for name in _NAMES:
        v = np.ascontiguousarray(inputs[name])
        if v.ndim == 0:
            v = v.reshape(1)
        arrays[f"in_{name}"] = v
        args[name] = nc.dram_tensor(f"in_{name}", v.shape, mybir.dt.from_np(v.dtype), kind="ExternalInput").ap()
    out = nc.dram_tensor("out", (BATCH, SEQ, D), F32, kind="ExternalOutput").ap()
    program(nc, args, out)
    return run_bass_kernel_spmd(nc, [arrays], core_ids=[0]).results[0]["out"]
```
